# Optimizing a Trainium2 kernel written in Bass

```python
import numpy as np
import jax
import jax.numpy as jnp

def _softmax(x, axis=-1):
    return jax.nn.softmax(x, axis=axis)

def _gelu(x):
    return jax.nn.gelu(x, approximate=True)

def _silu(x):
    return jax.nn.silu(x)

def _sigmoid(x):
    return jax.nn.sigmoid(x)

def _layernorm(x, axis=-1, eps=1e-05):
    m = jnp.mean(x, axis=axis, keepdims=True)
    v = jnp.var(x, axis=axis, keepdims=True)
    return (x - m) / jnp.sqrt(v + eps)

def _scatter_add(tgt, idx, src, axis=0):
    return tgt.at[idx].add(src)

def _segment_sum(src, seg, n):
    return jax.ops.segment_sum(src, seg, n)
kernel_name = 'mk_decoder_preln_d2_seqx_r8_6e50c3'

def setup_inputs(seed: int=0):
    np.random.seed(seed)
    _w = jnp.asarray

    def _rec_inputs():
        import jax
        import jax.numpy as jnp
        _rk = jax.random.key(seed)
        x = -0.000125 + 0.9999 * jax.random.normal(jax.random.fold_in(_rk, 1), (2, 256, 512), jnp.float32)
        _lenS = 256 - jax.random.randint(jax.random.fold_in(_rk, 7), (2,), 0, max(1, 256 // 4) + 1, jnp.int32)
        _lenS2 = 512 - jax.random.randint(jax.random.fold_in(_rk, 8), (2,), 0, max(1, 512 // 4) + 1, jnp.int32)
        _ctx_4096P = jax.random.normal(jax.random.fold_in(_rk, 11), (2, 16, 512), jnp.float32)
        _ctx_4096c = jax.random.dirichlet(jax.random.fold_in(_rk, 511), 0.3 * jnp.ones((16,), jnp.float32), (2, 512))
        _ctx_4096t = jnp.einsum('bsk,bkd->bsd', _ctx_4096c, _ctx_4096P)
        _ctx_4096t = _ctx_4096t * jax.lax.rsqrt(jnp.mean(jnp.square(_ctx_4096t)) + 1e-12) * 0.953939
        ctx_4096 = -5.72187e-05 + 0.999849 * (_ctx_4096t + 0.3 * jax.random.normal(jax.random.fold_in(_rk, 611), (2, 512, 512), jnp.float32))
        return (x, ctx_4096)
    x, ctx_4096 = _rec_inputs()

    def _L0_attn_setup():
        import jax, jax.numpy as jnp
        import numpy as np
        DIM = 512
        N_HEADS = 32
        HEAD_DIM = DIM // N_HEADS
        key = jax.random.key(seed)
        k0, k1, k2, k3, k4 = jax.random.split(key, 5)
        B, T = (2, 256)
        x = jax.random.normal(k0, (B, T, DIM), dtype=jnp.float32)
        s = 1.0 / np.sqrt(DIM)
        wq = jax.random.normal(k1, (DIM, DIM), dtype=jnp.float32) * s
        wk = jax.random.normal(k2, (DIM, HEAD_DIM), dtype=jnp.float32) * s
        wv = jax.random.normal(k3, (DIM, HEAD_DIM), dtype=jnp.float32) * s
        wo = jax.random.normal(k4, (DIM, DIM), dtype=jnp.float32) * s
        return {'x': x, 'wq': wq, 'wk': wk, 'wv': wv, 'wo': wo}
    _L0_attn_all = _L0_attn_setup()
    _L0_attn_in = {k: v for k, v in _L0_attn_all.items() if k in ('wq', 'wk', 'wv', 'wo')}
    del _L0_attn_all

    def _L0_xattn_setup():
        import jax, jax.numpy as jnp
        import numpy as np
        QMIN = 0.0
        QMAX = 255.0

        def fake_quant(x, scale, zp):
            s = scale.reshape(())
            z = zp.reshape(())
            q = jnp.clip(jnp.round(x / s + z), QMIN, QMAX)
            return (q - z) * s
        key = jax.random.key(seed)
        k1, k2 = jax.random.split(key)
        B, M, K, N = (4, 256, 512, 512)
        x1 = jax.random.normal(k1, (B, M, K), dtype=jnp.float32)
        x2 = jax.random.normal(k2, (B, K, N), dtype=jnp.float32)
        x1_scale = jnp.full((1,), 8.0 / 255.0, dtype=jnp.float32)
        x1_zp = jnp.full((1,), 128.0, dtype=jnp.float32)
        x2_scale = jnp.full((1,), 8.0 / 255.0, dtype=jnp.float32)
        x2_zp = jnp.full((1,), 128.0, dtype=jnp.float32)
        return {'x1': x1, 'x2': x2, 'x1_scale': x1_scale, 'x1_zp': x1_zp, 'x2_scale': x2_scale, 'x2_zp': x2_zp}
    _L0_xattn_all = _L0_xattn_setup()
    _L0_xattn_in = {k: v for k, v in _L0_xattn_all.items() if k in ('x1_scale', 'x1_zp', 'x2_scale', 'x2_zp')}
    del _L0_xattn_all

    def _L0_ffn_setup():
        import jax, jax.numpy as jnp
        import numpy as np
        R = 16
        NUM_EXPERTS = 8
        TOP_K = 2
        LORA_ALPHA = 32
        SCALING = LORA_ALPHA / R
        key = jax.random.key(seed)
        ks = jax.random.split(key, 6)
        d_in, d_out = (512, 512)
        x = jax.random.normal(ks[0], (4, 256, d_in), dtype=jnp.float32)
        W_base = jax.random.normal(ks[1], (d_out, d_in), dtype=jnp.float32) * 0.02
        b_base = jax.random.normal(ks[2], (d_out,), dtype=jnp.float32) * 0.02
        W_router = jax.random.normal(ks[3], (NUM_EXPERTS, d_in), dtype=jnp.float32) * 0.01
        A = jax.random.normal(ks[4], (NUM_EXPERTS, R, d_in), dtype=jnp.float32) * 0.02
        B = jax.random.normal(ks[5], (NUM_EXPERTS, d_out, R), dtype=jnp.float32) * 0.02
        return {'x': x, 'W_base': W_base, 'b_base': b_base, 'W_router': W_router, 'A': A, 'B': B}
    _L0_ffn_all = _L0_ffn_setup()
    _L0_ffn_in = {k: v for k, v in _L0_ffn_all.items() if k in ('W_base', 'b_base', 'W_router', 'A', 'B')}
    del _L0_ffn_all

    def _L1_attn_setup():
        import jax, jax.numpy as jnp
        import numpy as np
        HIDDEN = 512
        NUM_HEADS = 32
        HEAD_DIM = HIDDEN // NUM_HEADS

        def _fp8_roundtrip(x):
            return x.astype(jnp.float8_e4m3fn).astype(jnp.float32)
        key = jax.random.key(seed)
        ks = jax.random.split(key, 10)
        B, S = (2, 512)
        hidden_states = jax.random.normal(ks[0], (B, S, HIDDEN), dtype=jnp.float32)
        scale = 0.02

        def lin(kw, kb):
            w = jax.random.normal(kw, (HIDDEN, HIDDEN), dtype=jnp.float32) * scale
            b = jax.random.normal(kb, (HIDDEN,), dtype=jnp.float32) * scale
            return (w, b)
        wq, bq = lin(ks[1], ks[2])
        wk, bk = lin(ks[3], ks[4])
        wv, bv = lin(ks[5], ks[6])
        wl, bl = lin(ks[7], ks[8])
        wq, bq = (_fp8_roundtrip(wq), _fp8_roundtrip(bq))
        wk, bk = (_fp8_roundtrip(wk), _fp8_roundtrip(bk))
        wv, bv = (_fp8_roundtrip(wv), _fp8_roundtrip(bv))
        return {'hidden_states': hidden_states, 'wq': wq, 'bq': bq, 'wk': wk, 'bk': bk, 'wv': wv, 'bv': bv, 'wl': wl, 'bl': bl}
    _L1_attn_all = _L1_attn_setup()
    _L1_attn_in = {k: v for k, v in _L1_attn_all.items() if k in ('wq', 'bq', 'wk', 'bk', 'wv', 'bv', 'wl', 'bl')}
    del _L1_attn_all

    def _L1_xattn_setup():
        import jax, jax.numpy as jnp
        import numpy as np
        B, Q, D = (8, 64, 512)
        CTX = 512
        H, KV, HD = (16, 4, 96)
        G = H // KV
        key = jax.random.key(seed)
        ks = jax.random.split(key, 6)
        s = 0.02
        return {'latents': jax.random.normal(ks[0], (B, Q, D), jnp.float32), 'context': jax.random.normal(ks[1], (B, CTX, D), jnp.float32), 'Wq': jax.random.normal(ks[2], (H * HD, D), jnp.float32) * s, 'Wk': jax.random.normal(ks[3], (KV * HD, D), jnp.float32) * s, 'Wv': jax.random.normal(ks[4], (KV * HD, D), jnp.float32) * s, 'Wo': jax.random.normal(ks[5], (D, H * HD), jnp.float32) * s}
    _L1_xattn_all = _L1_xattn_setup()
    _L1_xattn_in = {k: v for k, v in _L1_xattn_all.items() if k in ('Wq', 'Wk', 'Wv', 'Wo')}
    del _L1_xattn_all

    def _L1_ffn_setup():
        import jax, jax.numpy as jnp
        import numpy as np
        import math
        B, S, IN, OUT = (4, 256, 512, 512)
        E, R, K = (8, 64, 128)
        SCALE = 64.0 / 64.0
        MULTIPLIER = 1.0
        key = jax.random.key(seed)
        ks = jax.random.split(key, 6)
        return {'x': jax.random.normal(ks[0], (B, S, IN), jnp.float32), 'W_org': jax.random.normal(ks[1], (OUT, IN), jnp.float32) * 0.02, 'lora_down': jax.random.normal(ks[2], (E, IN, R), jnp.float32) * 0.02, 'lora_up': jax.random.normal(ks[3], (E, R, OUT), jnp.float32) * 0.02, 'lora_keys': jax.random.normal(ks[4], (E, K), jnp.float32), 'Wq': jax.random.normal(ks[5], (K, IN), jnp.float32) * 0.02}
    _L1_ffn_all = _L1_ffn_setup()
    _L1_ffn_in = {k: v for k, v in _L1_ffn_all.items() if k in ('W_org', 'lora_down', 'lora_up', 'lora_keys', 'Wq')}
    del _L1_ffn_all
    return {'x': x, 'ctx_4096': ctx_4096, 'L0_attn_wq': _L0_attn_in['wq'], 'L0_attn_wk': _L0_attn_in['wk'], 'L0_attn_wv': _L0_attn_in['wv'], 'L0_attn_wo': _L0_attn_in['wo'], 'L0_xattn_x1_scale': _L0_xattn_in['x1_scale'], 'L0_xattn_x1_zp': _L0_xattn_in['x1_zp'], 'L0_xattn_x2_scale': _L0_xattn_in['x2_scale'], 'L0_xattn_x2_zp': _L0_xattn_in['x2_zp'], 'L0_ffn_W_base': _L0_ffn_in['W_base'], 'L0_ffn_b_base': _L0_ffn_in['b_base'], 'L0_ffn_W_router': _L0_ffn_in['W_router'], 'L0_ffn_A': _L0_ffn_in['A'], 'L0_ffn_B': _L0_ffn_in['B'], 'L1_attn_wq': _L1_attn_in['wq'], 'L1_attn_bq': _L1_attn_in['bq'], 'L1_attn_wk': _L1_attn_in['wk'], 'L1_attn_bk': _L1_attn_in['bk'], 'L1_attn_wv': _L1_attn_in['wv'], 'L1_attn_bv': _L1_attn_in['bv'], 'L1_attn_wl': _L1_attn_in['wl'], 'L1_attn_bl': _L1_attn_in['bl'], 'L1_xattn_Wq': _L1_xattn_in['Wq'], 'L1_xattn_Wk': _L1_xattn_in['Wk'], 'L1_xattn_Wv': _L1_xattn_in['Wv'], 'L1_xattn_Wo': _L1_xattn_in['Wo'], 'L1_ffn_W_org': _L1_ffn_in['W_org'], 'L1_ffn_lora_down': _L1_ffn_in['lora_down'], 'L1_ffn_lora_up': _L1_ffn_in['lora_up'], 'L1_ffn_lora_keys': _L1_ffn_in['lora_keys'], 'L1_ffn_Wq': _L1_ffn_in['Wq']}

def reference(x, ctx_4096, L0_attn_wq, L0_attn_wk, L0_attn_wv, L0_attn_wo, L0_xattn_x1_scale, L0_xattn_x1_zp, L0_xattn_x2_scale, L0_xattn_x2_zp, L0_ffn_W_base, L0_ffn_b_base, L0_ffn_W_router, L0_ffn_A, L0_ffn_B, L1_attn_wq, L1_attn_bq, L1_attn_wk, L1_attn_bk, L1_attn_wv, L1_attn_bv, L1_attn_wl, L1_attn_bl, L1_xattn_Wq, L1_xattn_Wk, L1_xattn_Wv, L1_xattn_Wo, L1_ffn_W_org, L1_ffn_lora_down, L1_ffn_lora_up, L1_ffn_lora_keys, L1_ffn_Wq):
    import jax
    import jax.numpy as jnp

    def _L0_attn_ref(x, wq, wk, wv, wo):
        import jax, jax.numpy as jnp
        import numpy as np
        DIM = 512
        N_HEADS = 32
        HEAD_DIM = DIM // N_HEADS
        B, T, C = x.shape
        q = (x @ wq).reshape(B, T, N_HEADS, HEAD_DIM)
        k = x @ wk
        v = x @ wv
        scale = 1.0 / jnp.sqrt(jnp.asarray(HEAD_DIM, dtype=x.dtype))
        scores = jnp.einsum('bqhd,bkd->bhqk', q, k) * scale
        causal = jnp.tril(jnp.ones((T, T), dtype=bool))
        scores = jnp.where(causal[None, None], scores, -jnp.inf)
        probs = jax.nn.softmax(scores.astype(jnp.float32), axis=-1).astype(x.dtype)
        out = jnp.einsum('bhqk,bkd->bqhd', probs, v).reshape(B, T, C)
        return out @ wo

    def _L0_xattn_ref(x1, x2, x1_scale, x1_zp, x2_scale, x2_zp):
        import jax, jax.numpy as jnp
        import numpy as np
        QMIN = 0.0
        QMAX = 255.0

        def fake_quant(x, scale, zp):
            s = scale.reshape(())
            z = zp.reshape(())
            q = jnp.clip(jnp.round(x / s + z), QMIN, QMAX)
            return (q - z) * s
        q1 = fake_quant(x1, x1_scale, x1_zp)
        q2 = fake_quant(x2, x2_scale, x2_zp)
        return jnp.matmul(q1, q2)

    def _L0_ffn_ref(x, W_base, b_base, W_router, A, B):
        import jax, jax.numpy as jnp
        import numpy as np
        R = 16
        NUM_EXPERTS = 8
        TOP_K = 2
        LORA_ALPHA = 32
        SCALING = LORA_ALPHA / R
        orig_shape = x.shape
        d_in = x.shape[-1]
        x_flat = x.reshape(-1, d_in)
        logits = x_flat @ W_router.T
        probs = jax.nn.softmax(logits, axis=-1)
        topk_probs, topk_idx = jax.lax.top_k(probs, TOP_K)
        topk_probs = topk_probs / jnp.sum(topk_probs, axis=-1, keepdims=True)
        onehot = jax.nn.one_hot(topk_idx, NUM_EXPERTS, dtype=x.dtype)
        combine = jnp.einsum('nk,nke->ne', topk_probs, onehot)
        h = jnp.einsum('nd,erd->ner', x_flat, A)
        hw = h * combine[:, :, None]
        expert_out = jnp.einsum('ner,eor->no', hw, B) * SCALING
        base_out = x_flat @ W_base.T + b_base
        out = base_out + expert_out
        return out.reshape(*orig_shape[:-1], W_base.shape[0])

    def _L1_attn_ref(hidden_states, wq, bq, wk, bk, wv, bv, wl, bl):
        import jax, jax.numpy as jnp
        import numpy as np
        HIDDEN = 512
        NUM_HEADS = 32
        HEAD_DIM = HIDDEN // NUM_HEADS

        def _fp8_roundtrip(x):
            return x.astype(jnp.float8_e4m3fn).astype(jnp.float32)
        B, S, E = hidden_states.shape
        H, D = (NUM_HEADS, HEAD_DIM)
        q = (hidden_states @ wq.T + bq).reshape(B, S, H, D)
        k = (hidden_states @ wk.T + bk).reshape(B, S, H, D)
        v = (hidden_states @ wv.T + bv).reshape(B, S, H, D)
        latent = hidden_states @ wl.T + bl
        scores = jnp.einsum('bshd,bstd->bsht', q, k) / np.sqrt(D).astype(np.float32)
        probs = jax.nn.softmax(scores, axis=-1)
        context = jnp.einsum('bsht,bstd->bshd', probs, v).reshape(B, S, E)
        return context

    def _L1_xattn_ref(latents, context, Wq, Wk, Wv, Wo):
        import jax, jax.numpy as jnp
        import numpy as np
        B, Q, D = (8, 64, 512)
        CTX = 512
        H, KV, HD = (16, 4, 96)
        G = H // KV
        b, q_len, _ = latents.shape
        hidden = jnp.concatenate([context, latents], axis=1)
        s_len = hidden.shape[1]
        q = (latents @ Wq.T).reshape(b, q_len, H, HD)
        k = (hidden @ Wk.T).reshape(b, s_len, KV, HD)
        v = (hidden @ Wv.T).reshape(b, s_len, KV, HD)
        q = q.transpose(0, 2, 1, 3).reshape(b, KV, G, q_len, HD)
        k = k.transpose(0, 2, 1, 3)
        v = v.transpose(0, 2, 1, 3)
        scale = 1.0 / jnp.sqrt(jnp.asarray(HD, q.dtype))
        scores = jnp.einsum('bkgqd,bksd->bkgqs', q, k) * scale
        attn = jax.nn.softmax(scores.astype(jnp.float32), axis=-1).astype(q.dtype)
        out = jnp.einsum('bkgqs,bksd->bkgqd', attn, v)
        out = out.reshape(b, H, q_len, HD).transpose(0, 2, 1, 3).reshape(b, q_len, H * HD)
        return out @ Wo.T

    def _L1_ffn_ref(x, W_org, lora_down, lora_up, lora_keys, Wq):
        import jax, jax.numpy as jnp
        import numpy as np
        import math
        B, S, IN, OUT = (4, 256, 512, 512)
        E, R, K = (8, 64, 128)
        SCALE = 64.0 / 64.0
        MULTIPLIER = 1.0
        base = jnp.einsum('bsi,oi->bso', x, W_org)
        q = jnp.einsum('bi,ki->bk', x.mean(axis=1), Wq)
        scores = jnp.einsum('bk,ek->be', q, lora_keys) / math.sqrt(K)
        coeffs = jax.nn.softmax(scores, axis=-1)
        h = jnp.einsum('bsi,eir->bser', x, lora_down)
        delta = jnp.einsum('be,bser,ero->bso', coeffs, h, lora_up)
        return base + delta * (SCALE * MULTIPLIER)
    x = x + _L0_attn_ref(_layernorm(x, axis=-1), L0_attn_wq, L0_attn_wk, L0_attn_wv, L0_attn_wo)
    x = x + _L0_xattn_ref(_layernorm(x, axis=-1), ctx_4096, L0_xattn_x1_scale, L0_xattn_x1_zp, L0_xattn_x2_scale, L0_xattn_x2_zp)
    x = x + _L0_ffn_ref(_layernorm(x, axis=-1), L0_ffn_W_base, L0_ffn_b_base, L0_ffn_W_router, L0_ffn_A, L0_ffn_B)
    x = x + _L1_attn_ref(_layernorm(x, axis=-1), L1_attn_wq, L1_attn_bq, L1_attn_wk, L1_attn_bk, L1_attn_wv, L1_attn_bv, L1_attn_wl, L1_attn_bl)
    x = x + _L1_xattn_ref(_layernorm(x, axis=-1), ctx_4096, L1_xattn_Wq, L1_xattn_Wk, L1_xattn_Wv, L1_xattn_Wo)
    x = x + _L1_ffn_ref(_layernorm(x, axis=-1), L1_ffn_W_org, L1_ffn_lora_down, L1_ffn_lora_up, L1_ffn_lora_keys, L1_ffn_Wq)
    return x

_drawn_inputs = setup_inputs


def setup_inputs(seed=0):
    import zlib

    import numpy as np

    out = dict(_drawn_inputs(seed))
    spreads = {}
    factors = {'L0_ffn_b_base': 8.0,
     'L0_ffn_W_router': 8.0,
     'L0_ffn_A': 8.0,
     'L0_ffn_B': 8.0,
     'L1_attn_wq': 8.0,
     'L1_attn_bq': 8.0,
     'L1_attn_wk': 8.0,
     'L1_attn_bk': 8.0,
     'L1_attn_wv': 8.0,
     'L1_attn_bv': 8.0,
     'L1_xattn_Wq': 8.0,
     'L1_xattn_Wk': 8.0,
     'L1_xattn_Wv': 8.0,
     'L1_xattn_Wo': 8.0,
     'L1_ffn_lora_down': 8.0,
     'L1_ffn_lora_up': 8.0,
     'L1_ffn_lora_keys': 8.0,
     'L1_ffn_Wq': 8.0,
     'L1_ffn_W_org': 3.914}
    for name, (base, spread) in spreads.items():
        noise = np.random.default_rng([zlib.crc32(name.encode()), seed]).standard_normal(out[name].shape)
        drawn = base * np.exp(spread * noise) if base else spread * noise
        out[name] = jnp.asarray(drawn.astype(out[name].dtype))
    for name, factor in factors.items():
        out[name] = (out[name] * factor).astype(out[name].dtype)
    return out
```

```python
from contextlib import ExitStack
import math

import concourse.bass as bass
from concourse import mybir

F32 = mybir.dt.float32
F32R = mybir.dt.float32r
BF16 = mybir.dt.bfloat16
ALU = mybir.AluOpType
ACT = mybir.ActivationFunctionType
AX = mybir.AxisListType.X

D = 512
B = 2
T = 256
P = 128
NI = T // P
C = D // P
NH, HD = 32, 16
NG = P // 4
KV, GQ, XD = 4, 4, 96
CTX = 512
SX = CTX + T
E0, R0 = 8, 16
E1, R1 = 8, 64
EPS = 1e-5
BIG = 2.0 ** 100
ROUND = 12582912.0
SX_SCALE = 1.0 / math.sqrt(XD)

ITEMS = [("wq0", 4, 512, 0), ("wkv0", 4, 32, 1), ("ctxn0", 4, 512, None), ("ctxn1", 4, 512, None), ("wo0", 4, 512, 2),
         ("wbase", 4, 512, 0), ("wexp", 4, E0 * R0 + E0, 1), ("wexpb", 1, 512, 2),
         ("wq1", 4, 512, 0), ("wk1", 4, 512, 1), ("wv1", 4, 512, 2),
         ("wxk", 4, 384, 0), ("wxv", 4, 384, 1), ("ctxt0", 4, 512, 2), ("ctxt1", 4, 512, 2)]
ITEMS += [(f"{n}{kv}", r, c, (2 + 2 * kv + j) % 3) for kv in range(KV) for j, (n, r, c) in enumerate([("wxq", 4, 384), ("wxo", 3, 512)])]
ITEMS += [("wdown", 4, 512, 1), ("worg", 4, 512, 2), ("wup", 4, 512, 0)]
ITEM = {name: k for k, (name, _, _, _) in enumerate(ITEMS)}

SCHEDULE = [("w", "wq0"), ("w", "wkv0"), ("ln", 0, 0), ("qkv0", 0), ("ln", 0, 1), ("ctxq", 0), ("ctxq", 1),
            ("w", "wo0"), ("smax0", 0), ("qkv0", 1), ("w", "wbase"), ("w", "wexp"),
            ("mrow0", 0), ("smax0", 1), ("att0", 0), ("mrow0", 1), ("out0", 0), ("ln", 1, 0), ("att0", 1), ("quant", 0), ("out0", 1),
            ("w", "wexpb"), ("ln", 1, 1), ("ln", 2, 0), ("quant", 1), ("ffn0", 0), ("ln", 2, 1), ("ln", 3, 0), ("ffn0", 1), ("ln", 3, 1),
            ("w", "wq1"), ("w", "wk1"), ("w", "wv1"),
            ("qkv1", 0), ("qkv1", 1), ("smax1", 0), ("att1", 0), ("smax1", 1), ("qkv1", 2), ("att1", 1), ("out1", 0),
            ("smax1", 2), ("qkv1", 3), ("w", "wxk"), ("w", "wxv"), ("w", "ctxt0"), ("out1", 1), ("ln", 4, 0), ("att1", 2), ("smax1", 3), ("att1", 3), ("out1", 2), ("out1", 3),
            ("kvctx", 0), ("w", "ctxt1"), ("kvlat", 0), ("ln", 4, 1), ("kvctx", 1), ("kvlat", 1)]
UNITS4 = [(kv, b) for kv in range(KV) for b in range(B)]
for n, u in enumerate(UNITS4):
    kv, b = u
    if b == 0:
        SCHEDULE += [("w", f"wxq{kv}"), ("w", f"wxo{kv}")] if kv == 0 else []
    SCHEDULE += [("q4", *u), ("smax4", *u)]
    if n >= 1:
        SCHEDULE += [("att4", *UNITS4[n - 1])]
    if n >= 2:
        SCHEDULE += [("out4", *UNITS4[n - 2])]
    if b == 1 and kv + 1 < KV:
        SCHEDULE += [("w", f"wxq{kv + 1}")]
    if b == 1 and kv + 1 < KV:
        SCHEDULE += [("w", f"wxo{kv + 1}")]
SCHEDULE += [("w", "wdown"), ("att4", *UNITS4[-1]), ("out4", *UNITS4[-2]), ("ln", 5, 0), ("out4", *UNITS4[-1]), ("w", "worg"), ("w", "wup"),
             ("ffn1a", 0), ("ln", 5, 1), ("ffn1b", 0), ("ffn1a", 1), ("ffn1b", 1)]


def program(nc, dram, out, counts, schedule):
    found, total, sems = {}, {}, {}
    ctx = ExitStack()

    def semaphore(kind):
        if kind not in sems:
            sems[kind] = ctx.enter_context(nc.semaphore(kind))
        return sems[kind]

    def ev(kind, *key, by=1):
        total[kind] = total.get(kind, 0) + by
        found[(kind, *key)] = total[kind]
        return semaphore(kind), by

    def on(kind, *key):
        return semaphore(kind), counts.get((kind, *key), 1)

    def so_far(kind):
        return semaphore(kind), total[kind]

    place, banks_of = {}, {}

    def bank(pe, ring, key, *drains):
        n = banks_of.get(id(ring), 0)
        banks_of[id(ring)] = n + 1
        tile, readers = ring[n % len(ring)]
        for reader in readers:
            pe.wait_ge(*on(*reader))
        readers[:] = drains
        place[key] = tile
        return tile

    with ctx:
        def sb(name, shape, dt=F32):
            return ctx.enter_context(nc.sbuf_tensor(name, shape, dt))

        X = sb("X", [P, B * NI, D])
        H = sb("H", [P, NI, D])
        HH = sb("HH", [P, B, C, T], F32R)
        HL = sb("HL", [P, B, C, T], F32R)
        STK = sb("STK", [P, 16384], F32R)
        STAGE = [sb(f"stage{n}", [P, 2048]) for n in range(2)]
        WH = [sb(f"WH{n}", [P, 2048], F32R) for n in range(3)]
        WL = [sb(f"WL{n}", [P, 2048], F32R) for n in range(3)]
        PT = [sb(f"PT{n}", [P, 1536]) for n in range(2)]
        VX = sb("VX", [P, 5184])
        SG = sb("SG", [P, 2048], F32R)
        ON = sb("ON", [P, 1024])
        KS0 = sb("KS0", [P, B, T], F32R)
        KL0 = sb("KL0", [HD, B, T], F32R)
        V0 = sb("V0", [P, B, NI, HD + 1])
        MT = sb("MT", [NH, T], F32R)
        MX = sb("MX", [P, B, NI, NH])
        DIAG = sb("DIAG", [P, 2, 512], BF16)
        ident = sb("ident", [P, P])
        negid = sb("negid", [P, P])
        identb = sb("identb", [P, P], BF16)
        onesb = sb("onesb", [P, P], BF16)
        mask_s = sb("mask_s", [P, P], BF16)
        mask_t = sb("mask_t", [P, P], BF16)
        rows_a = sb("rows_a", [4, P])
        rows_b = sb("rows_b", [4, P])
        tri = sb("tri", [P, E0, E0])
        stats = sb("stats", [P, NI, 6])
        mv = sb("mv", [P, NI, 2])
        var = sb("var", [P, NI])
        rstd = sb("rstd", [P, NI])
        minushalf = sb("minushalf", [P, NI])
        sc = sb("sc", [P, 16])
        biases = sb("biases", [P, 3, C])
        rden = sb("rden", [P, NH])
        rt = sb("rt", [P, NI, 4, E0])
        rc = sb("rc", [P, NI, 2, E0 * E0])
        small = sb("small", [P, 64])
        keys_t = sb("keys_t", [P, E1])
        wqx = sb("wqx", [P, C, P])

        ringA = [(ctx.enter_context(nc.psum_tensor(f"psA{n}", [P, 512], F32)), []) for n in range(5)]
        ringB = [(ctx.enter_context(nc.psum_tensor(f"psB{n}", [P, 512], F32)), []) for n in range(3)]

        def q2n(b):
            return VX[:, b * 1024:(b + 1) * 1024].bitcast(BF16).rearrange("p (c n) -> p c n", c=C)

        def corr(b):
            return VX[:, 2048 + b * 512:2560 + b * 512]

        bias0 = VX[:, 3072:3584]
        def q1t(b):
            return VX[:, 3584 + b * 512:4096 + b * 512].bitcast(BF16).rearrange("p (c t) -> p c t", c=C)

        q1n = VX[:, 4608:5120].bitcast(BF16).rearrange("p (i n) -> p i n", i=NI)
        VP = VX[:, 0:NG * 17].rearrange("p (g d) -> p g d", d=17)
        OTS = VX[:, 1088:1088 + 4096].rearrange("p (h t) -> p h t", t=P)
        def vx(b):
            return VX[:, b * 2328:(b + 1) * 2328].rearrange("p (s k d) -> p s k d", s=6, k=KV)

        def qs0(b):
            return STK[:, b * 8192:(b + 1) * 8192].rearrange("p (h t) -> p h t", h=NH)

        def st1(u, what):
            o = (u % 2) * 8192 + what * 4096
            return STK[:, o:o + 4096].rearrange("p (h t) -> p h t", h=NH)

        def group(u, what, rows, g):
            o = (u % 2) * 8192 + what * 4096 + g
            return STK[rows, o:o + 32 * 127 + 1:32]

        def kx(b, half):
            o = b * 6144 + half * 3072
            return STK[:, o:o + 3072].rearrange("p (k s) -> p k s", k=KV)

        def qx(n, half):
            o = 12288 + (n % 2) * 2048 + half * 1024
            return STK[:, o:o + 1024].rearrange("p (h t) -> p h t", h=GQ)

        sg4 = SG[:, :].rearrange("p (s m t) -> p s m t", s=2, m=C)
        sg1 = SG[:, :].rearrange("p (s m t) -> p s m t", s=4, m=C)
        sg3 = SG[:, 0:1536].rearrange("p (s c t) -> p s c t", s=2, c=3)
        sgh = SG[:, 0:512].rearrange("p (s t) -> p s t", s=2)

        expand = ON[0:1, 0:D]

        def item(name):
            _, r, c, slot = ITEMS[ITEM[name]]
            return tuple(w[slot][:, 0:r * c].rearrange("p (r c) -> p r c", r=r) for w in (WH, WL))

        def plain(ap):
            return ap.bitcast(F32)

        last_use = {"wq0": ("p_v0", 1), "wkv0": ("p_v0", 1), "wo0": ("p_y", "out0", 1, 1), "wbase": ("p_y", "ffn0", 1, 1),
                    "wexp": ("p_y", "ffn0", 1, 1), "wexpb": ("p_y", "ffn0", 1, 1), "wq1": ("p_q1", 3, 0), "wk1": ("p_q1", 3, 1),
                    "wv1": ("p_q1", 3, 2), "wxk": ("p_kx", "kvlat", 1, 3), "wxv": ("p_vx", "kvlat", 1, 1),
                    "ctxt0": ("p_vx", "kvctx", 0, 3), "ctxt1": ("p_vx", "kvctx", 1, 3)}
        for kv in range(KV):
            last_use[f"wxq{kv}"] = ("p_q4", kv, 1, 1)
            last_use[f"wxo{kv}"] = ("p_y", "out4", kv, 1, 1)
        block = ctx.enter_context(nc.Block())

        @block.tensor
        def _(pe):
            def split_mm(o, sh, sl, mh, ml, first, last):
                pe.matmul(o, sh, mh, start=first, stop=False)
                pe.matmul(o, sh, ml, start=False, stop=False)
                return pe.matmul(o, sl, mh, start=False, stop=last)

            def values0(pe, b, g):
                pt = PT[g % 2]
                pe.wait_ge(*on("e0", b, g, 2))
                if g % 2 == 0:
                    t = bank(pe, ringB, ("o0", b, g // 2), ("on0", b, g // 2))
                else:
                    t = place[("o0", b, g // 2)]
                tv = t[:, 0:272].rearrange("p (i h d) -> p i h d", i=NI, h=8)
                for j in range(4):
                    hh = (g % 2) * 4 + j
                    early = pt[:, 0:1024].rearrange("p (h q) -> p h q", h=4)
                    late = pt[:, 1024:1536].rearrange("p (h q) -> p h q", h=4)
                    pe.matmul(tv[:, 0, hh, :], early[:, j, 0:P], V0[:, b, 0, :], start=True, stop=True)
                    pe.matmul(tv[:, 1, hh, :], early[:, j, P:T], V0[:, b, 0, :], start=True, stop=False)
                    last = pe.matmul(tv[:, 1, hh, :], late[:, j, :], V0[:, b, 1, :], start=False, stop=True)
                last.then_inc(*ev("p_o0", b, g))

            pe.wait_ge(*on("consts"))
            for step in schedule:
                what, *k = step
                if what == "ln":
                    s, b = k
                    for i in range(NI):
                        pe.wait_ge(*on("h", s, b, i))
                        if s == 1:
                            t = bank(pe, ringA, ("hT", s, b, i), ("q1T", b, i))
                            tv = t[:, 0:256].bitcast(BF16)
                            for c in range(C):
                                last = pe.transpose(tv[:, c * P:(c + 1) * P], q1n[:, i, c * P:(c + 1) * P], identb[:, :])
                        else:
                            t = bank(pe, ringA, ("hT", s, b, i), ("h_low", s, b, i))
                            for c in range(C):
                                last = pe.transpose(t[:, c * P:(c + 1) * P], H[:, i, c * P:(c + 1) * P], ident[:, :])
                        last.then_inc(*ev("p_hT", s, b, i))
                elif what == "qkv0":
                    b, = k
                    pe.wait_ge(*on("h_low", 0, b, NI - 1))
                    wh, wl = (pe.wait_ge(*on("split", "wq0")), item("wq0"))[1]
                    for mp in range(2):
                        t = bank(pe, ringA, ("q0", b, mp), ("q0_low", b, mp))
                        for j in range(2):
                            m = 2 * mp + j
                            for c in range(C):
                                last = split_mm(t[:, j * T:(j + 1) * T], wh[:, c, m * P:(m + 1) * P], wl[:, c, m * P:(m + 1) * P],
                                                HH[:, b, c, :], HL[:, b, c, :], c == 0, c == C - 1)
                        last.then_inc(*ev("p_q0", b, mp))
                    pe.wait_ge(*on("split", "wkv0"))
                    wh, wl = item("wkv0")
                    t = bank(pe, ringA, ("k0", b), ("k0_low", b))
                    for c in range(C):
                        last = split_mm(t[0:HD, 0:T], wh[:, c, 0:HD], wl[:, c, 0:HD], HH[:, b, c, :], HL[:, b, c, :], c == 0, c == C - 1)
                    last.then_inc(*ev("p_k0", b))
                    t = bank(pe, ringA, ("v0", b), ("v0_out", b))
                    for i in range(NI):
                        for c in range(C):
                            last = split_mm(t[:, i * HD:(i + 1) * HD], HH[:, b, c, i * P:(i + 1) * P], HL[:, b, c, i * P:(i + 1) * P],
                                            wh[:, c, HD:2 * HD], wl[:, c, HD:2 * HD], c == 0, c == C - 1)
                    last.then_inc(*ev("p_v0", b))
                elif what == "smax0":
                    b, = k
                    pe.wait_ge(*on(f"d_q0_{b}"))
                    pe.wait_ge(*on(f"d_k0_{b}"))
                    n = 0
                    for i in range(NI):
                        per = 4 // (i + 1)
                        for g in range(NH // per):
                            t = bank(pe, ringA, ("s0", b, n), ("m0", b, n))
                            tv = t[:, :].rearrange("p (h k) -> p h k", h=per)
                            pe.matmul(tv[:, :, i * P:(i + 1) * P], identb[:, :], mask_s[:, :].unsqueeze(1).broadcast_to([P, per, P]),
                                      start=True, stop=False, skip_group_check=True)
                            for j in range(per):
                                last = pe.matmul(tv[:, j, :], qs0(b)[0:48, g * per + j, i * P:(i + 1) * P], KS0[0:48, b, 0:(i + 1) * P],
                                                 start=False, stop=True, skip_group_check=True)
                            last.then_inc(*ev("p_s0", b, n))
                            n += 1
                elif what == "mrow0":
                    b, = k
                    pe.wait_ge(*on("m0", b, 23))
                    t = bank(pe, ringA, ("mr0", b), ("mrow0", b))
                    for i in range(NI):
                        last = pe.transpose(t[0:NH, i * P:(i + 1) * P], MX[:, b, i, :], ident[:, :])
                    last.then_inc(*ev("p_mr0", b))
                elif what == "att0":
                    b, = k
                    pe.wait_ge(*on(f"d_m0_{b}"))
                    pe.wait_ge(*on("v0_out", b))
                    for g in range(NH // 4):
                        for j in range(2):
                            t = bank(pe, ringA, ("t0", b, g, j), ("e0", b, g, j))
                            tv = t[:, :].rearrange("p (h q) -> p h q", h=2)
                            pe.matmul(tv[:, :, 0:P], identb[:, :], mask_t[:, :].unsqueeze(1).broadcast_to([P, 2, P]),
                                      start=True, stop=False, skip_group_check=True)
                            pe.matmul(tv, KS0[0:49, b, 0:P], qs0(b)[0:49, g * 4 + j * 2:g * 4 + j * 2 + 2, :],
                                      start=False, stop=True, skip_group_check=True).then_inc(*ev("p_t0", b, g, j))
                        t = bank(pe, ringA, ("t0", b, g, 2), ("e0", b, g, 2))
                        tv = t[:, :].rearrange("p (h q) -> p h q", h=4)
                        pe.matmul(tv, identb[:, :], mask_t[:, :].unsqueeze(1).broadcast_to([P, 4, P]),
                                  start=True, stop=False, skip_group_check=True)
                        pe.matmul(tv, KS0[0:49, b, P:T], qs0(b)[0:49, g * 4:g * 4 + 4, P:T],
                                  start=False, stop=True, skip_group_check=True).then_inc(*ev("p_t0", b, g, 2))
                        if g >= 1:
                            values0(pe, b, g - 1)
                    values0(pe, b, NH // 4 - 1)
                elif what == "out0":
                    b, = k
                    for i in range(NI):
                        pe.wait_ge(*on("on0", b, NH // 8 - 1))
                        t = bank(pe, ringA, ("ot0", b, i), ("ot0_low", b, i))
                        for c in range(C):
                            last = pe.transpose(t[:, c * P:(c + 1) * P], ON[:, i * D + c * P:i * D + (c + 1) * P], ident[:, :])
                        last.then_inc(*ev("p_ot0", b, i))
                    pe.wait_ge(*on("split", "wo0"))
                    wh, wl = item("wo0")
                    for i in range(NI):
                        pe.wait_ge(*on("ot0_low", b, i))
                        t = bank(pe, ringA, ("y", "out0", b, i), ("x", "out0", b, i))
                        for c in range(C):
                            last = split_mm(t[:, :], HH[:, b, c, i * P:(i + 1) * P], HL[:, b, c, i * P:(i + 1) * P],
                                            wh[:, c, :], wl[:, c, :], c == 0, c == C - 1)
                        last.then_inc(*ev("p_y", "out0", b, i))
                elif what == "ctxq":
                    b, = k
                    pe.wait_ge(*on("q2", b))
                    t = bank(pe, ringA, ("cs", b), ("corr", b))
                    for c in range(C):
                        last = pe.matmul(t[:, :], onesb[:, :], q2n(b)[:, c, :], start=c == 0, stop=c == C - 1)
                    last.then_inc(*ev("p_cs", b))
                elif what == "quant":
                    b, = k
                    for i in range(NI):
                        pe.wait_ge(*on("q1T", b, i))
                        t = bank(pe, ringA, ("y", "quant", b, i), ("x1t", b, i))
                        for c in range(C):
                            last = pe.matmul(t[:, :], q1t(b)[:, c, i * P:(i + 1) * P], q2n(b)[:, c, :], start=c == 0, stop=c == C - 1)
                        last.then_inc(*ev("p_y", "quant", b, i))
                elif what == "ffn0":
                    b, = k
                    pe.wait_ge(*on("h_low", 2, b, NI - 1))
                    pe.wait_ge(*on("split", "wexp"))
                    wh, wl = item("wexp")
                    t = bank(pe, ringA, ("g0", b), ("hw", b, NI - 1))
                    n = E0 * R0 + E0
                    for i in range(NI):
                        for c in range(C):
                            last = split_mm(t[:, i * n:(i + 1) * n], HH[:, b, c, i * P:(i + 1) * P], HL[:, b, c, i * P:(i + 1) * P],
                                            wh[:, c, :], wl[:, c, :], c == 0, c == C - 1)
                    last.then_inc(*ev("p_g0", b))
                    pe.wait_ge(*on("split", "wbase"))
                    wh, wl = item("wbase")
                    outs = []
                    for i in range(NI):
                        t = bank(pe, ringB, ("y", "ffn0", b, i), ("x", "ffn0", b, i))
                        outs.append(t)
                        for c in range(C):
                            split_mm(t[:, :], HH[:, b, c, i * P:(i + 1) * P], HL[:, b, c, i * P:(i + 1) * P],
                                     wh[:, c, :], wl[:, c, :], c == 0, False)
                    pe.wait_ge(*on("hw", b, NI - 1))
                    t = bank(pe, ringA, ("hwt", b), ("hwt_low", b))
                    for i in range(NI):
                        last = pe.transpose(t[:, i * P:(i + 1) * P], ON[:, i * D:i * D + P], ident[:, :])
                    last.then_inc(*ev("p_hwt", b))
                    pe.wait_ge(*on("hwt_low", b))
                    pe.wait_ge(*on("split", "wexpb"))
                    wh, wl = item("wexpb")
                    for i in range(NI):
                        split_mm(outs[i][:, :], sgh[:, 0, i * P:(i + 1) * P], sgh[:, 1, i * P:(i + 1) * P], wh[:, 0, :], wl[:, 0, :],
                                 False, True).then_inc(*ev("p_y", "ffn0", b, i))
                elif what == "qkv1":
                    u, = k
                    b, i = divmod(u, NI)
                    pe.wait_ge(*on("h_low", 3, b, i))
                    for n, name in enumerate(("wq1", "wk1", "wv1")):
                        pe.wait_ge(*on("split", name))
                        wh, wl = item(name)
                        t = bank(pe, ringA, ("q1", u, n), ("qkv1", u, n))
                        for m in range(C):
                            for c in range(C):
                                last = split_mm(t[:, m * P:(m + 1) * P], wh[:, c, m * P:(m + 1) * P], wl[:, c, m * P:(m + 1) * P],
                                                HH[:, b, c, i * P:(i + 1) * P], HL[:, b, c, i * P:(i + 1) * P], c == 0, c == C - 1)
                        last.then_inc(*ev("p_q1", u, n))
                elif what == "smax1":
                    u, = k
                    pe.wait_ge(*on(f"d_q1_{u % 2}", u))
                    for g4 in range(NG // 4):
                        t = bank(pe, ringA, ("s1", u, g4), ("m1", u, g4))
                        for j in range(4):
                            g = 4 * g4 + j
                            last = pe.matmul(t[:, j * P:(j + 1) * P], group(u, 0, slice(0, 52), g), group(u, 1, slice(0, 52), g),
                                             start=True, stop=True)
                        last.then_inc(*ev("p_s1", u, g4))
                    t = bank(pe, ringA, ("v1", u), ("vp", u))
                    for g in range(NG):
                        last = pe.transpose(t[:, g * HD:(g + 1) * HD], plain(group(u, 0, slice(64, 80), g)), ident[64:80, 64:80])
                    last.then_inc(*ev("p_v1", u))
                elif what == "att1":
                    u, = k
                    pe.wait_ge(*on("vp", u))
                    for g4 in range(NG // 4 + 1):
                        if g4 < NG // 4:
                            pe.wait_ge(*on("diag", u, g4))
                            t = bank(pe, ringA, ("t1", u, g4), ("e1", u, g4))
                            pe.matmul(t[:, :], onesb[:, :], DIAG[:, g4 % 2, :], start=True, stop=False, skip_group_check=True)
                            for j in range(4):
                                g = 4 * g4 + j
                                last = pe.matmul(t[:, j * P:(j + 1) * P], group(u, 1, slice(0, 52), g),
                                                 group(u, 0, slice(0, 52), g), start=False, stop=True, skip_group_check=True)
                            last.then_inc(*ev("p_t1", u, g4))
                        if g4 >= 1:
                            n = g4 - 1
                            pe.wait_ge(*on("e1", u, n))
                            t = bank(pe, ringB, ("o1", u, n), ("ots", u, n))
                            pt = PT[n // 3 % 2][:, n % 3 * 512:(n % 3 + 1) * 512]
                            for j in range(4):
                                last = pe.matmul(t[0:17, j * P:(j + 1) * P], VP[:, 4 * n + j, :], pt[:, j * P:(j + 1) * P],
                                                 start=True, stop=True)
                            last.then_inc(*ev("p_o1", u, n))
                elif what == "out1":
                    u, = k
                    pe.wait_ge(*on("d_o1", u))
                    t = bank(pe, ringB, ("den1", u), ("rden1", u))
                    pe.transpose(t[:, 0:NH], ON[0:NH, 512:512 + P], ident[0:NH, 0:NH]).then_inc(*ev("p_den1", u))
                    t = bank(pe, ringB, ("y", "out1", u), ("x1o", u))
                    for m in range(C):
                        last = pe.transpose(t[:, m * P:(m + 1) * P], ON[:, m * P:(m + 1) * P], ident[:, :])
                    last.then_inc(*ev("p_y", "out1", u))
                elif what in ("kvctx", "kvlat"):
                    b, = k
                    if what == "kvctx":
                        pe.wait_ge(*on("split", f"ctxt{b}"))
                        xh, xl = item(f"ctxt{b}")
                        n, tiles = CTX, 4
                    else:
                        pe.wait_ge(*on("h_low", 4, b, NI - 1))
                        xh, xl = HH[:, b, :, :], HL[:, b, :, :]
                        n, tiles = T, 2
                    pe.wait_ge(*on("split", "wxk"))
                    wh, wl = item("wxk")
                    for kv in range(KV):
                        t = bank(pe, ringA, (what, b, kv), ("kx_low", what, b, kv))
                        for c in range(C):
                            last = split_mm(t[0:XD, 0:n], wh[:, c, kv * XD:(kv + 1) * XD], wl[:, c, kv * XD:(kv + 1) * XD],
                                            xh[:, c, :], xl[:, c, :], c == 0, c == C - 1)
                        last.then_inc(*ev("p_kx", what, b, kv))
                    pe.wait_ge(*on("split", "wxv"))
                    wh, wl = item("wxv")
                    for st in range(tiles):
                        t = bank(pe, ringA, (what, "v", b, st), ("vx", what, b, st))
                        for c in range(C):
                            last = split_mm(t[:, 0:KV * XD], xh[:, c, st * P:(st + 1) * P], xl[:, c, st * P:(st + 1) * P],
                                            wh[:, c, :], wl[:, c, :], c == 0, c == C - 1)
                        last.then_inc(*ev("p_vx", what, b, st))
                elif what == "q4":
                    kv, b = k
                    pe.wait_ge(*on("split", f"wxq{kv}"))
                    pe.wait_ge(*on("h_low", 4, b, NI - 1))
                    wh, wl = item(f"wxq{kv}")
                    for j in range(2):
                        t = bank(pe, ringA, ("q4", kv, b, j), ("q4_low", kv, b, j))
                        for h in range(2):
                            f = (2 * j + h) * XD
                            for c in range(C):
                                last = split_mm(t[0:XD, h * T:(h + 1) * T], wh[:, c, f:f + XD], wl[:, c, f:f + XD],
                                                HH[:, b, c, :], HL[:, b, c, :], c == 0, c == C - 1)
                        last.then_inc(*ev("p_q4", kv, b, j))
                elif what == "smax4":
                    kv, b = k
                    n = 2 * kv + b
                    pe.wait_ge(*on("q4_low", kv, b, 1))
                    pe.wait_ge(*on("kx_low", "kvlat", b, KV - 1))
                    for i in range(NI):
                        for h in range(GQ):
                            for j in range(2):
                                t = bank(pe, ringA, ("s4", kv, b, i, h, j), ("m4", kv, b, i, h, j))
                                pe.matmul(t[:, 0:384], qx(n, 0)[0:XD, h, i * P:(i + 1) * P], kx(b, 0)[0:XD, kv, j * 384:(j + 1) * 384],
                                          start=True, stop=True).then_inc(*ev("p_s4", kv, b, i, h, j))
                    pe.wait_ge(*on("m4s", kv, b))
                    t = bank(pe, ringA, ("mr4", kv, b), ("mrow4", kv, b))
                    pe.transpose(t[0:8, 0:P], small[:, 16:24], ident[:, :]).then_inc(*ev("p_mr4", kv, b))
                elif what == "att4":
                    kv, b = k
                    n = 2 * kv + b
                    pe.wait_ge(*on("d_m4", kv, b))
                    pe.wait_ge(*on("vx", "kvlat", b, 1))
                    os = [bank(pe, ringB, ("o4", kv, b, i), ("on4", kv, b, i)) for i in range(NI)]

                    def values4(h):
                        pt = PT[h % 2][:, :].rearrange("p (s q) -> p s q", q=T)
                        pe.wait_ge(*on("e4", kv, b, h, 2))
                        for i in range(NI):
                            for st in range(6):
                                last = pe.matmul(os[i][:, h * (XD + 1):(h + 1) * (XD + 1)], pt[:, st, i * P:(i + 1) * P], vx(b)[:, st, kv, :],
                                                 start=st == 0, stop=st == 5)
                        last.then_inc(*ev("p_o4", kv, b, h))
                    for h in range(GQ):
                        for s2 in range(3):
                            t = bank(pe, ringA, ("t4", kv, b, h, s2), ("e4", kv, b, h, s2))
                            for j in range(2):
                                o = t[:, j * T:(j + 1) * T]
                                ks = slice((2 * s2 + j) * P, (2 * s2 + j + 1) * P)
                                pe.matmul(o, kx(b, 0)[0:XD + 1, kv, ks], qx(n, 0)[0:XD + 1, h, :], start=True, stop=False)
                                pe.matmul(o, kx(b, 0)[0:XD, kv, ks], qx(n, 1)[0:XD, h, :], start=False, stop=False)
                                last = pe.matmul(o, kx(b, 1)[0:XD, kv, ks], qx(n, 0)[0:XD, h, :], start=False, stop=True)
                            last.then_inc(*ev("p_t4", kv, b, h, s2))
                        if h >= 1:
                            values4(h - 1)
                    values4(GQ - 1)
                elif what == "out4":
                    kv, b = k
                    for i in range(NI):
                        pe.wait_ge(*on("on4", kv, b, i))
                        t = bank(pe, ringA, ("ot4", kv, b, i), ("ot4_low", kv, b, i))
                        for c in range(3):
                            last = pe.transpose(t[:, c * P:(c + 1) * P], ON[:, i * 384 + c * P:i * 384 + (c + 1) * P], ident[:, :])
                        last.then_inc(*ev("p_ot4", kv, b, i))
                    pe.wait_ge(*on("split", f"wxo{kv}"))
                    wh, wl = item(f"wxo{kv}")
                    for i in range(NI):
                        pe.wait_ge(*on("ot4_low", kv, b, i))
                        t = bank(pe, ringA, ("y", "out4", kv, b, i), ("x", "out4", kv, b, i))
                        for c in range(3):
                            last = split_mm(t[:, :], sg3[:, 0, c, i * P:(i + 1) * P], sg3[:, 1, c, i * P:(i + 1) * P],
                                            wh[:, c, :], wl[:, c, :], c == 0, c == 2)
                        last.then_inc(*ev("p_y", "out4", kv, b, i))
                elif what == "ffn1a":
                    b, = k
                    pe.wait_ge(*on("mean", b))
                    t = bank(pe, ringA, ("cq", b), ("cq", b))
                    for c in range(C):
                        last = pe.matmul(t[:, 0:1], wqx[:, c, :], small[:, 32 + c:33 + c], start=c == 0, stop=c == C - 1)
                    last.then_inc(*ev("p_cq", b))
                    pe.wait_ge(*on("cq", b))
                    t = bank(pe, ringA, ("cs1", b), ("cexp", b))
                    pe.matmul(t[0:1, 0:E1], small[:, 36:37], keys_t[:, :], start=True, stop=True).then_inc(*ev("p_cs1", b))
                    pe.wait_ge(*on("split", "wdown"))
                    wh, wl = item("wdown")
                    pe.wait_ge(*on("h_low", 5, b, NI - 1))
                    for mp in range(2):
                        t = bank(pe, ringB, ("dn", b, mp), ("dn_low", b, mp))
                        for j in range(2):
                            m = 2 * mp + j
                            for c in range(C):
                                last = split_mm(t[:, j * T:(j + 1) * T], wh[:, c, m * P:(m + 1) * P], wl[:, c, m * P:(m + 1) * P],
                                                HH[:, b, c, :], HL[:, b, c, :], c == 0, c == C - 1)
                        last.then_inc(*ev("p_dn", b, mp))
                    pe.wait_ge(*on("coef", b))
                    t = bank(pe, ringA, ("cc", b), ("cc", b))
                    for m in range(C):
                        last = pe.matmul(t[:, m:m + 1], expand[0:1, m * P:(m + 1) * P], ident[0:1, 0:1], start=True, stop=True)
                    last.then_inc(*ev("p_cc", b))
                elif what == "ffn1b":
                    b, = k
                    pe.wait_ge(*on("split", "worg"))
                    oh, ol = item("worg")
                    pe.wait_ge(*on("split", "wup"))
                    uh, ul = item("wup")
                    for i in range(NI):
                        t = bank(pe, ringA, ("y", "ffn1", b, i), ("x", "ffn1", b, i))
                        for c in range(C):
                            split_mm(t[:, :], HH[:, b, c, i * P:(i + 1) * P], HL[:, b, c, i * P:(i + 1) * P],
                                     oh[:, c, :], ol[:, c, :], c == 0, False)
                        pe.wait_ge(*on("dn_low", b, 1))
                        for c in range(C):
                            last = split_mm(t[:, :], sg4[:, 0, c, i * P:(i + 1) * P], sg4[:, 1, c, i * P:(i + 1) * P],
                                            uh[:, c, :], ul[:, c, :], False, c == C - 1)
                        last.then_inc(*ev("p_y", "ffn1", b, i))

        @block.scalar
        def _(act):
            for step in schedule:
                what, *k = step
                if what == "ln":
                    s, b = k
                    for i in range(NI):
                        act.wait_ge(*on("p_hT", s, b, i))
                        t = place[("hT", s, b, i)]
                        if s == 1:
                            act.activation(q1t(b)[:, :, i * P:(i + 1) * P], t[:, 0:256].bitcast(BF16).rearrange("p (c t) -> p c t", c=C),
                                           ACT.Copy).then_inc(*ev("q1T", b, i))
                        else:
                            act.activation(HH[:, b, :, i * P:(i + 1) * P], t[:, :].rearrange("p (c t) -> p c t", c=C),
                                           ACT.Copy).then_inc(*ev("h_high", s, b, i))
                elif what == "qkv0":
                    b, = k
                    if b:
                        act.wait_ge(*on("d_q0_0"))
                    for mp in range(2):
                        act.wait_ge(*on("p_q0", b, mp))
                        act.activation(sg4[:, 0, 2 * mp:2 * mp + 2, :], place[("q0", b, mp)][:, :].rearrange("p (m t) -> p m t", m=2),
                                       ACT.Copy).then_inc(*ev("q0_high", b, mp))
                    act.wait_ge(*on("p_k0", b))
                    act.wait_ge(*on("consts_v"))
                    act.activation(KS0[0:HD, b, :], place[("k0", b)][0:HD, 0:T], ACT.Copy).then_inc(*ev("k0_high", b))
                elif what == "mrow0":
                    b, = k
                    act.wait_ge(*on("p_mr0", b))
                    if b:
                        act.wait_ge(*on("d_m0_0"))
                    act.activation(MT[:, :], place[("mr0", b)][0:NH, 0:T], ACT.Copy, scale=-1.0).then_inc(*ev("mrow0", b))
                elif what == "att0":
                    b, = k
                    for g in range(NH // 4):
                        if g >= 2:
                            act.wait_ge(*on("p_o0", b, g - 2))
                        elif b:
                            act.wait_ge(*on("p_o0", b - 1, 6 + g))
                        for j in range(3):
                            act.wait_ge(*on("p_t0", b, g, j))
                            act.activation(PT[g % 2][:, j * 512:(j + 1) * 512], place[("t0", b, g, j)][:, :], ACT.Exp,
                                           scale=0.25).then_inc(*ev("e0", b, g, j))
                elif what == "out0":
                    b, = k
                    for i in range(NI):
                        act.wait_ge(*on("p_ot0", b, i))
                        act.activation(HH[:, b, :, i * P:(i + 1) * P], place[("ot0", b, i)][:, :].rearrange("p (c t) -> p c t", c=C),
                                       ACT.Copy).then_inc(*ev("ot0_high", b, i))
                elif what == "ffn0":
                    b, = k
                    act.wait_ge(*on("lmm", b))
                    act.activation(rt[:, :, 1, :], rt[:, :, 0, :], ACT.Exp).then_inc(*ev("lexp", b))
                    act.wait_ge(*on("p_hwt", b))
                    act.activation(sgh[:, 0, :], place[("hwt", b)][:, 0:T], ACT.Copy).then_inc(*ev("hwt_high", b))
                elif what == "qkv1":
                    u, = k
                    for n in range(2):
                        act.wait_ge(*on("qkv1", u, n))
                        if u and n == 0:
                            act.wait_ge(*on(f"d_q1_{(u - 1) % 2}", u - 1))
                        act.activation(sg1[:, 2 * n, :, :], PT[n][:, 0:512].rearrange("p (m t) -> p m t", m=C), ACT.Copy).then_inc(*ev("qk1_high", u, n))
                elif what == "smax1":
                    u, = k
                    act.wait_ge(*on("p_v1", u))
                    if u:
                        act.wait_ge(*on("p_o1", u - 1, 7))
                    act.wait_ge(*on("vp_ones"))
                    act.activation(VP[:, :, 0:HD], place[("v1", u)][:, :].rearrange("p (g d) -> p g d", d=HD), ACT.Copy).then_inc(*ev("vp", u))
                elif what == "att1":
                    u, = k
                    act.wait_ge(*on("qk1_low", min(u + 1, 3), 1))
                    for g4 in range(NG // 4):
                        act.wait_ge(*on("p_t1", u, g4))
                        if g4 >= 6:
                            act.wait_ge(*on("p_o1", u, g4 - 6))
                        act.activation(PT[g4 // 3 % 2][:, g4 % 3 * 512:(g4 % 3 + 1) * 512], place[("t1", u, g4)][:, :], ACT.Exp,
                                       scale=0.25).then_inc(*ev("e1", u, g4))
                elif what in ("kvctx", "kvlat"):
                    b, = k
                    s0, n = (0, CTX) if what == "kvctx" else (CTX, T)
                    for kv in range(KV):
                        act.wait_ge(*on("p_kx", what, b, kv))
                        act.activation(kx(b, 0)[0:XD, kv, s0:s0 + n], place[(what, b, kv)][0:XD, 0:n], ACT.Copy).then_inc(*ev("kx_high", what, b, kv))
                    for st in range(n // P):
                        act.wait_ge(*on("p_vx", what, b, st))
                        act.wait_ge(*on("vx_ones"))
                        act.activation(vx(b)[:, s0 // P + st, :, 0:XD], place[(what, "v", b, st)][:, 0:KV * XD].rearrange("p (k d) -> p k d", k=KV),
                                       ACT.Copy).then_inc(*ev("vx", what, b, st))
                elif what == "q4":
                    kv, b = k
                    n = 2 * kv + b
                    for j in range(2):
                        act.wait_ge(*on("p_q4", kv, b, j))
                        if n >= 2:
                            act.wait_ge(*on("p_t4", (n - 2) // 2, n % 2, GQ - 1, 2))
                        act.activation(qx(n, 0)[0:XD, 2 * j:2 * j + 2, :], place[("q4", kv, b, j)][0:XD, :].rearrange("p (h t) -> p h t", h=2),
                                       ACT.Copy).then_inc(*ev("q4_high", kv, b, j))
                elif what == "smax4":
                    kv, b = k
                    act.wait_ge(*on("p_mr4", kv, b))
                    if kv or b:
                        act.wait_ge(*on("d_m4", *UNITS4[2 * kv + b - 1]))
                    act.activation(MT[0:8, 0:P], place[("mr4", kv, b)][0:8, 0:P], ACT.Copy, scale=-1.0).then_inc(*ev("mrow4", kv, b))
                elif what == "att4":
                    kv, b = k
                    for h in range(GQ):
                        if h >= 2:
                            act.wait_ge(*on("p_o4", kv, b, h - 2))
                        elif kv or b:
                            act.wait_ge(*on("p_o4", *UNITS4[2 * kv + b - 1], h + 2))
                        for s2 in range(3):
                            act.wait_ge(*on("p_t4", kv, b, h, s2))
                            act.activation(PT[h % 2][:, s2 * 512:(s2 + 1) * 512], place[("t4", kv, b, h, s2)][:, :], ACT.Exp,
                                           scale=SX_SCALE).then_inc(*ev("e4", kv, b, h, s2))
                elif what == "out4":
                    kv, b = k
                    for i in range(NI):
                        act.wait_ge(*on("p_ot4", kv, b, i))
                        if kv or b:
                            act.wait_ge(*on("p_y", "out4", *UNITS4[2 * kv + b - 1], i))
                        act.activation(sg3[:, 0, :, i * P:(i + 1) * P], place[("ot4", kv, b, i)][:, 0:384].rearrange("p (c t) -> p c t", c=3),
                                       ACT.Copy).then_inc(*ev("ot4_high", kv, b, i))
                elif what == "ffn1a":
                    b, = k
                    act.wait_ge(*on("cmax", b))
                    act.activation(small[0:1, 48:56], place[("cs1", b)][0:1, 0:E1], ACT.Exp, scale=1.0 / math.sqrt(128.0),
                                   bias=small[0:1, 41:42]).then_inc(*ev("cexp", b))
                    if b:
                        act.wait_ge(*on("p_y", "ffn1", 0, NI - 1))
                    for mp in range(2):
                        act.wait_ge(*on("p_dn", b, mp))
                        act.wait_ge(*on("cc", b))
                        for j in range(2):
                            m = 2 * mp + j
                            act.activation(sg4[:, 0, m, :], place[("dn", b, mp)][:, j * T:(j + 1) * T], ACT.Copy,
                                           scale=small[:, 44 + m:45 + m]).then_inc(*ev("dn_high", b, m))

        @block.vector
        def _(dve):
            def link(ins):
                ins.then_inc(*ev("v_step"))
                dve.wait_ge(semaphore("v_step"), total["v_step"])

            def low(o, t, high, key):
                dve.tensor_tensor(out=o, in0=t, in1=plain(high), op=ALU.subtract).then_inc(*ev(*key))

            dve.memset(V0[:, :, :, HD:HD + 1], 1.0)
            dve.memset(onesb[:, :], 1.0)
            dve.memset(plain(STK[96:97, 0:12288]), 1.0)
            dve.memset(plain(KS0[:, :, :]), 1.0).then_inc(*ev("consts_v"))
            dve.wait_ge(*on("d_small", "sc"))
            link(dve.reciprocal(sc[:, 4:5], sc[:, 0:1]))
            link(dve.reciprocal(sc[:, 5:6], sc[:, 2:3]))
            link(dve.tensor_scalar(sc[:, 6:7], sc[:, 1:2], -128.0, None, ALU.add))
            link(dve.tensor_scalar(sc[:, 7:8], sc[:, 3:4], -128.0, None, ALU.add))
            link(dve.tensor_tensor(out=sc[:, 8:9], in0=sc[:, 0:1], in1=sc[:, 2:3], op=ALU.mult))
            link(dve.tensor_scalar(sc[:, 9:10], sc[:, 6:7], sc[:, 8:9], -1.0, ALU.mult, ALU.mult))
            link(dve.tensor_scalar(sc[:, 10:11], sc[:, 9:10], sc[:, 7:8], -float(CTX), ALU.mult, ALU.mult))
            link(dve.tensor_scalar(sc[:, 11:12], sc[:, 7:8], -1.0, None, ALU.mult))
            for step in schedule:
                what, *k = step
                if what == "ln":
                    s, b = k
                    if s == 0:
                        dve.wait_ge(*on("d_small", f"x{b}"))
                    for i in range(NI):
                        last = dve.bn_stats(stats[:, i, :], X[:, 2 * b + i, :])
                    link(last)
                    if s or b:
                        dve.wait_ge(*so_far("h"))
                    if s == 4 and b == 0:
                        dve.wait_ge(*on("d_q1_1", 3))
                    for i in range(NI):
                        last = dve.bn_aggr(mv[:, i, :], stats[:, i, :])
                    link(last)
                    dve.tensor_scalar(var[:, :], mv[:, :, 1], EPS, None, ALU.add).then_inc(*ev("var", s, b))
                    dve.wait_ge(*on("rstd", s, b))
                    for i in range(NI):
                        ins = dve.tensor_scalar(H[:, i, :], X[:, 2 * b + i, :], mv[:, i, 0:1], rstd[:, i:i + 1], ALU.subtract, ALU.mult)
                        if s == 1:
                            link(ins)
                            link(dve.tensor_scalar(H[:, i, :], H[:, i, :], sc[:, 4:5], sc[:, 1:2], ALU.mult, ALU.add))
                            link(dve.tensor_scalar(H[:, i, :], H[:, i, :], 0.0, 255.0, ALU.max, ALU.min))
                            if b:
                                dve.wait_ge(*on("p_hT", 1, 0, i))
                            dve.tensor_scalar(q1n[:, i, :], H[:, i, :], ROUND, ROUND + 128.0, ALU.add, ALU.subtract).then_inc(*ev("h", s, b, i))
                        else:
                            ins.then_inc(*ev("h", s, b, i))
                    if s == 1:
                        for i in range(NI):
                            dve.wait_ge(*on("h", s, b, i))
                            link(dve.tensor_reduce(small[:, 2 * b + i:2 * b + i + 1], q1n[:, i, :], AX, ALU.add))
                            link(dve.tensor_scalar(small[:, 2 * b + i:2 * b + i + 1], small[:, 2 * b + i:2 * b + i + 1], sc[:, 11:12], None, ALU.mult))
                    else:
                        for i in range(NI):
                            dve.wait_ge(*on("p_hT", s, b, i))
                            t = place[("hT", s, b, i)]
                            if s == 5:
                                dve.wait_ge(*on("h_high", s, b, i))
                                link(dve.tensor_reduce(small[:, 24 + 4 * i:28 + 4 * i], t[:, :].rearrange("p (c t) -> p c t", c=C), AX, ALU.add))
                            dve.wait_ge(*on("h_high", s, b, i))
                            low(HL[:, b, :, i * P:(i + 1) * P], t[:, :].rearrange("p (c t) -> p c t", c=C), HH[:, b, :, i * P:(i + 1) * P], ("h_low", s, b, i))
                        if s == 5:
                            link(dve.tensor_tensor(out=small[:, 32:36], in0=small[:, 24:28], in1=small[:, 28:32], op=ALU.add))
                            dve.tensor_scalar(small[:, 32:36], small[:, 32:36], 1.0 / T, None, ALU.mult).then_inc(*ev("mean", b))
                elif what == "qkv0":
                    b, = k
                    for mp in range(2):
                        dve.wait_ge(*on("p_q0", b, mp))
                        dve.wait_ge(*on("q0_high", b, mp))
                        low(sg4[:, 1, 2 * mp:2 * mp + 2, :], place[("q0", b, mp)][:, :].rearrange("p (m t) -> p m t", m=2),
                            sg4[:, 0, 2 * mp:2 * mp + 2, :], ("q0_low", b, mp))
                    dve.wait_ge(*on("k0_high", b))
                    low(KL0[:, b, :], place[("k0", b)][0:HD, 0:T], KS0[0:HD, b, :], ("k0_low", b))
                    dve.wait_ge(*on("p_v0", b))
                    dve.tensor_copy(V0[:, b, :, 0:HD], place[("v0", b)][:, 0:2 * HD].rearrange("p (i d) -> p i d", i=NI)).then_inc(*ev("v0_out", b))
                elif what == "smax0":
                    b, = k
                    n = 0
                    for i in range(NI):
                        per = 4 // (i + 1)
                        for g in range(NH // per):
                            dve.wait_ge(*on("p_s0", b, n))
                            dve.tensor_reduce(MX[:, b, i, g * per:(g + 1) * per], place[("s0", b, n)][:, :].rearrange("p (h k) -> p h k", h=per),
                                              AX, ALU.max).then_inc(*ev("m0", b, n))
                            n += 1
                elif what == "att0":
                    b, = k
                    for g in range(NH // 8):
                        dve.wait_ge(*on("p_o0", b, 2 * g + 1))
                        tv = place[("o0", b, g)][:, 0:272].rearrange("p (i h d) -> p i h d", i=NI, h=8)
                        if b or g:
                            dve.wait_ge(*so_far("on0"))
                        link(dve.reciprocal(rden[:, 0:16].rearrange("p (i h) -> p i h", i=NI), tv[:, :, :, HD]))
                        if b and g == 0:
                            dve.wait_ge(*on("p_ot0", 0, NI - 1))
                        for i in range(NI):
                            ins = dve.tensor_tensor(out=ON[:, i * D + g * P:i * D + (g + 1) * P].rearrange("p (h d) -> p h d", d=HD), in0=tv[:, i, :, 0:HD],
                                                    in1=rden[:, i * 8:(i + 1) * 8].unsqueeze(2).broadcast_to([P, 8, HD]), op=ALU.mult)
                        ins.then_inc(*ev("on0", b, g))
                elif what == "out0":
                    b, = k
                    for i in range(NI):
                        dve.wait_ge(*on("ot0_high", b, i))
                        low(HL[:, b, :, i * P:(i + 1) * P], place[("ot0", b, i)][:, :].rearrange("p (c t) -> p c t", c=C),
                            HH[:, b, :, i * P:(i + 1) * P], ("ot0_low", b, i))
                    for i in range(NI):
                        dve.wait_ge(*on("p_y", "out0", b, i))
                        x = X[:, 2 * b + i, :]
                        dve.tensor_tensor(out=x, in0=place[("y", "out0", b, i)][:, :], in1=x, op=ALU.add).then_inc(*ev("x", "out0", b, i))
                    dve.wait_ge(*on("x", "out0", b, NI - 1))
                elif what == "ctxq":
                    b, = k
                    name = f"ctxn{b}"
                    n = ITEM[name]
                    st = STAGE[n % 2]
                    dve.wait_ge(*on(f"d_stage{n % 2}", name))
                    link(dve.tensor_scalar(st[:, :], st[:, :], sc[:, 5:6], sc[:, 3:4], ALU.mult, ALU.add))
                    link(dve.tensor_scalar(st[:, :], st[:, :], 0.0, 255.0, ALU.max, ALU.min))
                    dve.tensor_scalar(q2n(b).rearrange("p c n -> p (c n)"), st[:, :], ROUND, ROUND + 128.0, ALU.add, ALU.subtract).then_inc(*ev("q2", b))
                    dve.wait_ge(*on("p_cs", b))
                    dve.tensor_scalar(corr(b), place[("cs", b)][:, :], sc[:, 9:10], sc[:, 10:11], ALU.mult, ALU.add).then_inc(*ev("corr", b))
                elif what == "quant":
                    b, = k
                    for i in range(NI):
                        dve.wait_ge(*on("p_y", "quant", b, i))
                        x = X[:, 2 * b + i, :]
                        dve.tensor_scalar(H[:, i, :], place[("y", "quant", b, i)][:, :], small[:, 2 * b + i:2 * b + i + 1], sc[:, 8:9],
                                          ALU.add, ALU.mult).then_inc(*ev("x1t", b, i))
                        dve.wait_ge(*on("x1t", b, i))
                        link(dve.tensor_tensor(out=H[:, i, :], in0=H[:, i, :], in1=corr(b), op=ALU.add))
                        dve.tensor_tensor(out=x, in0=H[:, i, :], in1=x, op=ALU.add).then_inc(*ev("x", "quant", b, i))
                    dve.wait_ge(*on("x", "quant", b, NI - 1))
                elif what == "ffn0":
                    b, = k
                    n = E0 * R0 + E0
                    dve.wait_ge(*on("p_g0", b))
                    tv = place[("g0", b)][:, 0:2 * n].rearrange("p (i n) -> p i n", i=NI)
                    logits = tv[:, :, E0 * R0:n]
                    link(dve.tensor_reduce(small[:, 8:10], logits, AX, ALU.max))
                    dve.tensor_tensor(out=rt[:, :, 0, :], in0=logits, in1=small[:, 8:10].unsqueeze(2).broadcast_to([P, NI, E0]),
                                      op=ALU.subtract).then_inc(*ev("lmm", b))
                    dve.wait_ge(*on("lexp", b))
                    for i in range(NI):
                        ex = rt[:, i, 1, :]
                        other = ex.unsqueeze(1).broadcast_to([P, E0, E0])
                        own = ex.unsqueeze(2).broadcast_to([P, E0, E0])
                        gt = rc[:, i, 0, :].rearrange("p (e j) -> p e j", e=E0)
                        eq = rc[:, i, 1, :].rearrange("p (e j) -> p e j", e=E0)
                        dve.tensor_tensor(out=gt, in0=other, in1=own, op=ALU.is_gt)
                        link(dve.tensor_tensor(out=eq, in0=other, in1=own, op=ALU.is_equal))
                        dve.wait_ge(*on("consts"))
                        link(dve.tensor_tensor(out=eq, in0=eq, in1=tri[:, :, :], op=ALU.mult))
                        link(dve.tensor_tensor(out=gt, in0=gt, in1=eq, op=ALU.add))
                        link(dve.tensor_reduce(rt[:, i, 2, :], gt, AX, ALU.add))
                        link(dve.tensor_scalar(rt[:, i, 2, :], rt[:, i, 2, :], 2.0, None, ALU.is_lt))
                        link(dve.tensor_tensor(out=rt[:, i, 3, :], in0=rt[:, i, 2, :], in1=ex, op=ALU.mult))
                        link(dve.tensor_reduce(small[:, 10 + i:11 + i], rt[:, i, 3, :], AX, ALU.add))
                        link(dve.reciprocal(small[:, 12 + i:13 + i], small[:, 10 + i:11 + i]))
                        link(dve.tensor_scalar(rt[:, i, 3, :], rt[:, i, 3, :], small[:, 12 + i:13 + i], 2.0, ALU.mult, ALU.mult))
                        dve.tensor_tensor(out=ON[:, i * D:i * D + P].rearrange("p (e r) -> p e r", e=E0),
                                          in0=tv[:, i, 0:E0 * R0].rearrange("p (e r) -> p e r", e=E0),
                                          in1=rt[:, i, 3, :].unsqueeze(2).broadcast_to([P, E0, R0]), op=ALU.mult).then_inc(*ev("hw", b, i))
                    dve.wait_ge(*on("hwt_high", b))
                    low(sgh[:, 1, :], place[("hwt", b)][:, 0:T], sgh[:, 0, :], ("hwt_low", b))
                    for i in range(NI):
                        x = X[:, 2 * b + i, :]
                        dve.wait_ge(*on("p_y", "ffn0", b, i))
                        dve.tensor_tensor(out=x, in0=place[("y", "ffn0", b, i)][:, :], in1=x, op=ALU.add).then_inc(*ev("x", "ffn0", b, i))
                        dve.wait_ge(*on("x", "ffn0", b, i))
                        if b == 0 and i == 0:
                            dve.wait_ge(*on("d_small", "bias0"))
                        link(dve.tensor_tensor(out=x, in0=x, in1=bias0, op=ALU.add))
                elif what == "qkv1":
                    u, = k
                    if u == 0:
                        dve.wait_ge(*on("x", "ffn0", 1, 1))
                        dve.memset(VP[:, :, HD:HD + 1], 1.0).then_inc(*ev("vp_ones"))
                        dve.wait_ge(*on("d_small", "biases"))
                    dst = [PT[0][:, 0:512], PT[1][:, 0:512], H[:, 1, :]]
                    for n in range(3):
                        dve.wait_ge(*on("p_q1", u, n))
                        if u == 0 and n == 0:
                            dve.wait_ge(*on("p_o0", 1, 7))
                        if u and n == 0:
                            dve.wait_ge(*on(f"d_q1_{(u - 1) % 2}", u - 1))
                        if u >= 2 and n == 0:
                            dve.wait_ge(*on("p_o1", u - 2, 7))
                        dve.tensor_tensor(out=dst[n].rearrange("p (m t) -> p m t", m=C), in0=place[("q1", u, n)][:, :].rearrange("p (m t) -> p m t", m=C),
                                          in1=biases[:, n, :].unsqueeze(2).broadcast_to([P, C, P]), op=ALU.add).then_inc(*ev("qkv1", u, n))
                        if n < 2:
                            dve.wait_ge(*on("qk1_high", u, n))
                            low(sg1[:, 2 * n + 1, :, :], dst[n].rearrange("p (m t) -> p m t", m=C), sg1[:, 2 * n, :, :], ("qk1_low", u, n))
                elif what == "smax1":
                    u, = k
                    mx = MX[:, :, :, :].rearrange("p b i h -> p (b i h)")
                    for g4 in range(NG // 4):
                        dve.wait_ge(*on("p_s1", u, g4))
                        o = mx[:, (u % 2) * 32 + 4 * g4:(u % 2) * 32 + 4 * g4 + 4]
                        dve.tensor_reduce(o, place[("s1", u, g4)][:, :].rearrange("p (g k) -> p g k", g=4), AX, ALU.max).then_inc(*ev("m1", u, g4))
                elif what == "att1":
                    u, = k
                    mx = MX[:, :, :, :].rearrange("p b i h -> p (b i h)")
                    dve.wait_ge(*on("m1", u, 7))

                    def diag(g4):
                        if g4 >= 2:
                            dve.wait_ge(*on("p_t1", u, g4 - 2))
                        elif u:
                            dve.wait_ge(*on("p_t1", u - 1, 6 + g4))
                        m = mx[:, (u % 2) * 32 + 4 * g4:(u % 2) * 32 + 4 * g4 + 4]
                        dve.tensor_tensor(out=DIAG[:, g4 % 2, :].rearrange("p (g k) -> p g k", g=4), in0=negid[:, :].unsqueeze(1).broadcast_to([P, 4, P]),
                                          in1=m.unsqueeze(2).broadcast_to([P, 4, P]), op=ALU.mult).then_inc(*ev("diag", u, g4))
                    diag(0)
                    diag(1)
                    for g4 in range(NG // 4):
                        if g4 + 2 < NG // 4:
                            diag(g4 + 2)
                        dve.wait_ge(*on("p_o1", u, g4))
                        if g4 == 0 and u:
                            dve.wait_ge(*on("d_o1", u - 1))
                        dve.tensor_copy(OTS[0:17, :, :].rearrange("p h (j g) -> p g h j", j=4)[:, 4 * g4:4 * g4 + 4, :, :],
                                        place[("o1", u, g4)][0:17, :].rearrange("p (g h j) -> p g h j", g=4, h=NH)).then_inc(*ev("ots", u, g4))
                elif what == "out1":
                    u, = k
                    x = X[:, u, :]
                    dve.wait_ge(*on("p_den1", u))
                    dve.reciprocal(rden[:, :], place[("den1", u)][:, 0:NH]).then_inc(*ev("rden1", u))
                    dve.wait_ge(*on("rden1", u))
                    dve.wait_ge(*on("p_y", "out1", u))
                    t = H[:, 0, :]
                    dve.tensor_tensor(out=t.rearrange("p (h d) -> p h d", h=NH), in0=place[("y", "out1", u)][:, :].rearrange("p (h d) -> p h d", h=NH),
                                      in1=rden[:, :].unsqueeze(2).broadcast_to([P, NH, HD]), op=ALU.mult).then_inc(*ev("x1o", u))
                    dve.wait_ge(*on("x1o", u))
                    link(dve.tensor_tensor(out=x, in0=t, in1=x, op=ALU.add))
                    if u == 3:
                        dve.memset(vx(0)[:, :, :, XD:XD + 1], 1.0)
                        dve.memset(vx(1)[:, :, :, XD:XD + 1], 1.0).then_inc(*ev("vx_ones"))
                elif what in ("kvctx", "kvlat"):
                    b, = k
                    s0, n = (0, CTX) if what == "kvctx" else (CTX, T)
                    for kv in range(KV):
                        dve.wait_ge(*on("kx_high", what, b, kv))
                        low(kx(b, 1)[0:XD, kv, s0:s0 + n], place[(what, b, kv)][0:XD, 0:n], kx(b, 0)[0:XD, kv, s0:s0 + n], ("kx_low", what, b, kv))
                elif what == "q4":
                    kv, b = k
                    n = 2 * kv + b
                    for j in range(2):
                        dve.wait_ge(*on("q4_high", kv, b, j))
                        low(qx(n, 1)[0:XD, 2 * j:2 * j + 2, :], place[("q4", kv, b, j)][0:XD, :].rearrange("p (h t) -> p h t", h=2),
                            qx(n, 0)[0:XD, 2 * j:2 * j + 2, :], ("q4_low", kv, b, j))
                elif what == "smax4":
                    kv, b = k
                    if kv or b:
                        dve.wait_ge(*on("p_mr4", *UNITS4[2 * kv + b - 1]))
                    for i in range(NI):
                        for h in range(GQ):
                            for j in range(2):
                                dve.wait_ge(*on("p_s4", kv, b, i, h, j))
                                o = small[:, i * 8 + h * 2 + j:i * 8 + h * 2 + j + 1]
                                ins = dve.tensor_reduce(o, place[("s4", kv, b, i, h, j)][:, 0:384], AX, ALU.max)
                                ins.then_inc(*ev("m4", kv, b, i, h, j))
                    dve.wait_ge(*on("m4", kv, b, NI - 1, GQ - 1, 1))
                    dve.tensor_reduce(small[:, 16:24], small[:, 0:16].rearrange("p (g j) -> p g j", j=2), AX, ALU.max).then_inc(*ev("m4s", kv, b))
                elif what == "att4":
                    kv, b = k
                    for i in range(NI):
                        dve.wait_ge(*on("p_o4", kv, b, GQ - 1))
                        tv = place[("o4", kv, b, i)][:, 0:GQ * (XD + 1)].rearrange("p (h d) -> p h d", h=GQ)
                        if kv or b or i:
                            dve.wait_ge(*so_far("on4"))
                        link(dve.reciprocal(rden[:, 4 * i:4 * i + 4], tv[:, :, XD]))
                        if kv or b:
                            dve.wait_ge(*on("p_ot4", *UNITS4[2 * kv + b - 1], i))
                        dve.tensor_tensor(out=ON[:, i * 384:(i + 1) * 384].rearrange("p (h d) -> p h d", h=GQ), in0=tv[:, :, 0:XD],
                                          in1=rden[:, 4 * i:4 * i + 4].unsqueeze(2).broadcast_to([P, GQ, XD]), op=ALU.mult).then_inc(*ev("on4", kv, b, i))
                elif what == "out4":
                    kv, b = k
                    for i in range(NI):
                        dve.wait_ge(*on("ot4_high", kv, b, i))
                        low(sg3[:, 1, :, i * P:(i + 1) * P], place[("ot4", kv, b, i)][:, 0:384].rearrange("p (c t) -> p c t", c=3),
                            sg3[:, 0, :, i * P:(i + 1) * P], ("ot4_low", kv, b, i))
                    for i in range(NI):
                        dve.wait_ge(*on("p_y", "out4", kv, b, i))
                        x = X[:, 2 * b + i, :]
                        dve.tensor_tensor(out=x, in0=place[("y", "out4", kv, b, i)][:, :], in1=x, op=ALU.add).then_inc(*ev("x", "out4", kv, b, i))
                    dve.wait_ge(*on("x", "out4", kv, b, NI - 1))
                elif what == "ffn1a":
                    b, = k
                    dve.wait_ge(*on("p_cq", b))
                    dve.tensor_copy(small[:, 36:37], place[("cq", b)][:, 0:1]).then_inc(*ev("cq", b))
                    dve.wait_ge(*on("p_cs1", b))
                    link(dve.tensor_reduce(small[0:1, 40:41], place[("cs1", b)][0:1, 0:E1], AX, ALU.max))
                    dve.tensor_scalar(small[0:1, 41:42], small[0:1, 40:41], -1.0 / math.sqrt(128.0), None, ALU.mult).then_inc(*ev("cmax", b))
                    dve.wait_ge(*on("cexp", b))
                    link(dve.tensor_reduce(small[0:1, 42:43], small[0:1, 48:56], AX, ALU.add))
                    link(dve.reciprocal(small[0:1, 43:44], small[0:1, 42:43]))
                    link(dve.tensor_scalar(small[0:1, 56:64], small[0:1, 48:56], small[0:1, 43:44], None, ALU.mult))
                    dve.tensor_copy(expand[0:1, :].rearrange("p (e r) -> p e r", e=E1), small[0:1, 56:64].unsqueeze(2).broadcast_to([1, E1, R1])).then_inc(*ev("coef", b))
                    dve.wait_ge(*on("p_cc", b))
                    dve.tensor_copy(small[:, 44:48], place[("cc", b)][:, 0:4]).then_inc(*ev("cc", b))
                    dve.wait_ge(*on("cc", b))
                    for m in range(C):
                        dve.wait_ge(*on("dn_high", b, m | 1))
                        ins = dve.scalar_tensor_tensor(out=sg4[:, 1, m, :], in0=place[("dn", b, m // 2)][:, m % 2 * T:(m % 2 + 1) * T],
                                                       scalar=small[:, 44 + m:45 + m], in1=plain(sg4[:, 0, m, :]), op0=ALU.mult, op1=ALU.subtract)
                        if m % 2:
                            ins.then_inc(*ev("dn_low", b, m // 2))
                elif what == "ffn1b":
                    b, = k
                    for i in range(NI):
                        dve.wait_ge(*on("p_y", "ffn1", b, i))
                        x = X[:, 2 * b + i, :]
                        dve.tensor_tensor(out=x, in0=place[("y", "ffn1", b, i)][:, :], in1=x, op=ALU.add).then_inc(*ev("x", "ffn1", b, i))
            dve.nop().then_inc(*ev("finished"))

        @block.gpsimd
        def _(pool):
            def load(n):
                if n >= len(ITEMS):
                    return
                name, r, c, _ = ITEMS[n]
                if n >= 2:
                    before, _, _, slot = ITEMS[n - 2]
                    pool.wait_ge(*(on("q2", int(before[-1])) if slot is None else on("split", before)))
                pool.dma_start(STAGE[n % 2][:, 0:r * c].rearrange("p (r c) -> p r c", r=r),
                               dram[name].rearrange("(r p) c -> p r c", p=P)).then_inc(*ev(f"d_stage{n % 2}", name, by=16))

            load(0)
            load(1)
            pool.memset(ident[:, :], 0.0)
            pool.memset(negid[:, :], 0.0)
            pool.memset(identb[:, :], 0.0)
            pool.memset(mask_s[:, :], 0.0)
            pool.memset(mask_t[:, :], 0.0)
            pool.memset(rows_a[:, :], 0.0)
            pool.memset(rows_b[:, :], -BIG)
            pool.memset(tri[:, :, :], 1.0)
            pool.memset(minushalf[:, :], -0.5).then_inc(*ev("zeros"))
            pool.wait_ge(*on("zeros"))
            for m, fill in ((ident, 1.0), (negid, -1.0), (identb, 1.0)):
                pool.affine_select(out=m[:, :], in_=m[:, :], compare_op=ALU.not_equal, fill=fill, base=0, pattern=[[-1, P]], channel_multiplier=1)
            pool.affine_select(out=mask_s[:, :], in_=mask_s[:, :], compare_op=ALU.is_ge, fill=-BIG, base=0, pattern=[[-1, P]], channel_multiplier=1)
            pool.affine_select(out=mask_t[:, :], in_=mask_t[:, :], compare_op=ALU.is_ge, fill=-BIG, base=0, pattern=[[1, P]], channel_multiplier=-1)
            for m, fill in ((rows_a, 1.0), (rows_b, 0.0)):
                v = m[:, :].rearrange("p (j g) -> p j g", j=4)
                pool.affine_select(out=v, in_=v, compare_op=ALU.not_equal, fill=fill, base=0, pattern=[[1, 4], [0, 32]], channel_multiplier=-1)
            pool.affine_select(out=tri[:, :, :], in_=tri[:, :, :], compare_op=ALU.is_gt, fill=0.0, base=0,
                               pattern=[[1, E0], [-1, E0]], channel_multiplier=0).then_inc(*ev("consts"))
            loaded = 2
            for step in schedule:
                what, *k = step
                if what == "w":
                    name, = k
                    n = ITEM[name]
                    _, r, c, slot = ITEMS[n]
                    while loaded <= n:
                        load(loaded)
                        loaded += 1
                    before = [m for m in range(n) if ITEMS[m][3] == slot]
                    if before:
                        pool.wait_ge(*on(*last_use[ITEMS[before[-1]][0]]))
                    pool.wait_ge(*on(f"d_stage{n % 2}", name))
                    st = STAGE[n % 2][:, 0:r * c]
                    pool.tensor_copy(WH[slot][:, 0:r * c], st).then_inc(*ev("split_high", name))
                    pool.wait_ge(*on("split_high", name))
                    pool.tensor_tensor(out=WL[slot][:, 0:r * c], in0=st, in1=plain(WH[slot][:, 0:r * c]), op=ALU.subtract).then_inc(*ev("split", name))
                    while loaded <= min(n + 2, len(ITEMS) - 1):
                        load(loaded)
                        loaded += 1
                elif what == "ln":
                    s, b = k
                    pool.wait_ge(*on("var", s, b))
                    pool.tensor_tensor(out=rstd[:, :], in0=var[:, :], in1=minushalf[:, :], op=ALU.pow).then_inc(*ev("rstd", s, b))

        @block.sync
        def _(sp):
            for n, (name, dst) in enumerate((("sc", sc[:, 0:4]), ("x0", X[:, 0:2, :]), ("x1", X[:, 2:4, :]), ("biases", biases[:, :, :]),
                                             ("bias0", bias0), ("keys", keys_t[:, :]), ("wqx", wqx[:, :, :]))):
                src = {"sc": lambda: dram["scales"].partition_broadcast(P), "x0": lambda: dram["x"][0:256, :].rearrange("(i p) d -> p i d", p=P),
                       "x1": lambda: dram["x"][256:512, :].rearrange("(i p) d -> p i d", p=P), "biases": lambda: dram["biases1"],
                       "bias0": lambda: dram["bias0"].partition_broadcast(P), "keys": lambda: dram["keys"],
                       "wqx": lambda: dram["wqx"].rearrange("(c p) k -> p c k", p=P)}[name]()
                sp.dma_start(dst, src).then_inc(*ev("d_small", name, by=16))
                sp.wait_ge(*on("d_small", name))
            sp.wait_ge(*on("consts"))
            for step in schedule:
                what, *k = step
                if what == "qkv0":
                    b, = k
                    sp.wait_ge(*on("q0_high", b, 1))
                    sp.wait_ge(*on("q0_low", b, 1))
                    qv = qs0(b).rearrange("p (m h) t -> p m h t", h=8)
                    for row, half in enumerate((0, 1, 0)):
                        for h in range(8):
                            sp.dma_start(plain(qv[row * HD:(row + 1) * HD, :, h, :]), plain(sg4[h * HD:(h + 1) * HD, half, :, :])
                                         ).then_inc(*ev(f"d_q0_{b}", by=16))
                    sp.wait_ge(*on("k0_low", b))
                    sp.dma_start(plain(KS0[HD:2 * HD, b, :]), plain(KS0[0:HD, b, :])).then_inc(*ev(f"d_k0_{b}", by=16))
                    sp.dma_start(plain(KS0[2 * HD:3 * HD, b, :]), plain(KL0[:, b, :])).then_inc(*ev(f"d_k0_{b}", by=16))
                elif what == "mrow0":
                    b, = k
                    sp.wait_ge(*on("mrow0", b))
                    sp.dma_start(plain(qs0(b)[48:49, :, :]), plain(MT[:, :])).then_inc(*ev(f"d_m0_{b}", by=16))
                elif what == "qkv1":
                    u, = k
                    name = f"d_q1_{u % 2}"
                    sp.wait_ge(*on("qk1_low", u, 1))
                    sp.wait_ge(*on("qkv1", u, 2))
                    if u == 0:
                        sp.wait_ge(*on("p_t0", 1, 7, 2))
                    if u < 2:
                        sp.dma_start(plain(st1(u, 0)[48:52, :, :]), rows_b[:, :].unsqueeze(1).broadcast_to([4, NH, P])).then_inc(*ev(name, u, by=16))
                        sp.dma_start(plain(st1(u, 1)[48:52, :, :]), rows_a[:, :].unsqueeze(1).broadcast_to([4, NH, P])).then_inc(*ev(name, u, by=16))
                    else:
                        sp.wait_ge(*on("p_t1", u - 2, 7))
                    for side, halves in ((0, (0, 1, 0)), (1, (2, 2, 3))):
                        v = st1(u, side).rearrange("p (m h) t -> p m h t", h=8)
                        for row, half in enumerate(halves):
                            for h in range(8):
                                sp.dma_start(plain(v[row * HD:(row + 1) * HD, :, h, :]), plain(sg1[h * HD:(h + 1) * HD, half, :, :])
                                             ).then_inc(*ev(name, u, by=16))
                    v = st1(u, 0).rearrange("p (m h) t -> p m h t", h=8)
                    vs = H[:, 1, :].rearrange("p (m t) -> p m t", m=C)
                    for h in range(8):
                        sp.dma_start(plain(v[64:64 + HD, :, h, :]), vs[h * HD:(h + 1) * HD, :, :]).then_inc(*ev(name, u, by=16))
                elif what == "att1":
                    u, = k
                    sp.wait_ge(*on("ots", u, 7))
                    if u:
                        sp.wait_ge(*on("p_y", "out1", u - 1))
                    ov = OTS[0:HD, :, :].rearrange("p (m h) t -> p m h t", h=8)
                    for h in range(8):
                        sp.dma_start(ON[h * HD:(h + 1) * HD, 0:512].rearrange("p (m t) -> p m t", m=C), ov[:, :, h, :]).then_inc(*ev("d_o1", u, by=16))
                    sp.dma_start(ON[0:NH, 512:512 + P], OTS[HD:HD + 1, :, :]).then_inc(*ev("d_o1", u, by=16))
                    sp.wait_ge(*on("d_o1", u))
                elif what == "smax4":
                    kv, b = k
                    sp.wait_ge(*on("mrow4", kv, b))
                    for i in range(NI):
                        sp.dma_start(plain(qx(2 * kv + b, 0)[XD:XD + 1, :, i * P:(i + 1) * P]), plain(MT[i * 4:(i + 1) * 4, 0:P])
                                     ).then_inc(*ev("d_m4", kv, b, by=16))
                    sp.wait_ge(*on("d_m4", kv, b))
                elif what == "ffn1b":
                    b, = k
                    for i in range(NI):
                        sp.wait_ge(*on("x", "ffn1", b, i))
                        sp.dma_start(out[b * T + i * P:b * T + (i + 1) * P, :], X[:, 2 * b + i, :]).then_inc(*ev("d_out", by=16))
            if schedule[-1][0] != "ffn1b":
                sp.wait_ge(*on("finished"))
                sp.dma_start(out.rearrange("(i p) d -> p i d", p=P), X[:, :, :]).then_inc(*ev("d_out", by=16))
            sp.wait_ge(*on("d_out"))
    return found


def kernel(**inputs):
    import numpy as np
    import concourse.bacc as bacc
    from concourse.bass_utils import run_bass_kernel_spmd as run

    a = {k: np.asarray(v) for k, v in inputs.items()}
    t = {
        "x": a["x"].reshape(B * T, D), "wq0": a["L0_attn_wq"], "wo0": a["L0_attn_wo"],
        "wkv0": np.concatenate([a["L0_attn_wk"], a["L0_attn_wv"]], axis=1),
        "ctxn0": a["ctx_4096"][0], "ctxn1": a["ctx_4096"][1], "ctxt0": a["ctx_4096"][0].T, "ctxt1": a["ctx_4096"][1].T,
        "scales": np.concatenate([a[f"L0_xattn_{n}"] for n in ("x1_scale", "x1_zp", "x2_scale", "x2_zp")]),
        "wbase": a["L0_ffn_W_base"].T, "bias0": a["L0_ffn_b_base"],
        "wexp": np.concatenate([a["L0_ffn_A"].reshape(E0 * R0, D).T, a["L0_ffn_W_router"].T], axis=1),
        "wexpb": a["L0_ffn_B"].transpose(0, 2, 1).reshape(E0 * R0, D),
        "wq1": a["L1_attn_wq"].T, "wk1": a["L1_attn_wk"].T, "wv1": a["L1_attn_wv"].T,
        "biases1": np.stack([a[f"L1_attn_b{n}"].reshape(C, P).T for n in "qkv"], axis=1),
        "wxk": a["L1_xattn_Wk"].T, "wxv": a["L1_xattn_Wv"].T,
        "worg": a["L1_ffn_W_org"].T, "wdown": a["L1_ffn_lora_down"].transpose(1, 0, 2).reshape(D, E1 * R1),
        "wup": a["L1_ffn_lora_up"].reshape(E1 * R1, D), "keys": a["L1_ffn_lora_keys"].T, "wqx": a["L1_ffn_Wq"].T,
    }
    for kv in range(KV):
        t[f"wxq{kv}"] = a["L1_xattn_Wq"].T[:, kv * GQ * XD:(kv + 1) * GQ * XD]
        t[f"wxo{kv}"] = a["L1_xattn_Wo"].T[kv * GQ * XD:(kv + 1) * GQ * XD, :]
    arrays = {f"in_{k}": np.ascontiguousarray(v) for k, v in t.items()}

    def build(counts):
        nc = bacc.Bacc("TRN2", target_bir_lowering=False, num_devices=1, dynamic_dma_scratch_size=8192)
        dram = {k: nc.dram_tensor(f"in_{k}", arrays[f"in_{k}"].shape, mybir.dt.from_np(arrays[f"in_{k}"].dtype), kind="ExternalInput").ap() for k in t}
        out = nc.dram_tensor("out_0", (B * T, D), F32, kind="ExternalOutput").ap()
        return nc, program(nc, dram, out, counts, SCHEDULE)

    _, counts = build({})
    nc, _ = build(counts)
    got = run(nc, [arrays], core_ids=[0]).results[0]["out_0"]
    return got.reshape(B, T, D)
```

```python
from contextlib import ExitStack
import math

import concourse.bass as bass
from concourse import mybir

F32 = mybir.dt.float32
F32R = mybir.dt.float32r
BF16 = mybir.dt.bfloat16
ALU = mybir.AluOpType
ACT = mybir.ActivationFunctionType
AX = mybir.AxisListType.X

D = 512
B = 2
T = 256
P = 128
NI = T // P
C = D // P
NH, HD = 32, 16
NG = P // 4
KV, GQ, XD = 4, 4, 96
CTX = 512
SX = CTX + T
E0, R0 = 8, 16
E1, R1 = 8, 64
EPS = 1e-5
BIG = 2.0 ** 100
ROUND = 12582912.0
SX_SCALE = 1.0 / math.sqrt(XD)

ITEMS = [("wq0", 4, 512, 0), ("wkv0", 4, 32, 1), ("ctxn0", 4, 512, None), ("ctxn1", 4, 512, None), ("wo0", 4, 512, 2),
         ("wbase", 4, 512, 0), ("wexp", 4, E0 * R0 + E0, 1), ("wexpb", 1, 512, 2),
         ("wq1", 4, 512, 0), ("wk1", 4, 512, 1), ("wv1", 4, 512, 2),
         ("wxk", 4, 384, 0), ("wxv", 4, 384, 1), ("ctxt0", 4, 512, 2), ("ctxt1", 4, 512, 2)]
ITEMS += [(f"{n}{kv}", r, c, (2 + 2 * kv + j) % 3) for kv in range(KV) for j, (n, r, c) in enumerate([("wxq", 4, 384), ("wxo", 3, 512)])]
ITEMS += [("wdown", 4, 512, 1), ("worg", 4, 512, 2), ("wup", 4, 512, 0)]
ITEM = {name: k for k, (name, _, _, _) in enumerate(ITEMS)}

SCHEDULE = [("ln", 0, 0), ("ln", 0, 1), ("w", "wq0"), ("w", "wkv0"), ("consts",), ("qkv0", 0), ("qkv0", 1), ("ctxq", 0), ("ctxq", 1),
            ("w", "wo0"), ("smax0", 0), ("mrow0", 0), ("w", "wbase"), ("w", "wexp"),
            ("att0", 0, 1, 0, 8), ("mrow0", 1), ("att0", 1, None, 0, 3), ("out0", 0), ("att0", 1, None, 3, 6), ("ln", 1, 0),
            ("att0", 1, None, 6, 8), ("quant", 0), ("out0", 1),
            ("w", "wexpb"), ("ln", 1, 1), ("ln", 2, 0), ("quant", 1), ("ffn0", 0), ("ln", 2, 1), ("ln", 3, 0), ("ffn0", 1),
            ("w", "wq1"), ("w", "wk1"), ("w", "wv1"), ("qkv1", 0), ("ln", 3, 1), ("qkv1", 1), ("load1", 0), ("load1", 1),
            ("w", "wxk"), ("w", "wxv"), ("w", "ctxt0"),
            ("smax1", 0), ("att1", 0, 1), ("load1", 2), ("att1", 1, 2), ("out1", 0), ("load1", 3), ("att1", 2, 3), ("out1", 1), ("ln", 4, 0),
            ("att1", 3, None), ("out1", 2), ("kvctx", 0), ("w", "ctxt1"), ("out1", 3), ("kvlat", 0), ("ln", 4, 1), ("kvctx", 1), ("kvlat", 1)]
UNITS4 = [(kv, b) for kv in range(KV) for b in range(B)]
SCHEDULE += [("w", "wxq0"), ("w", "wxo0")]
for n in range(len(UNITS4) + 2):
    u = [UNITS4[m] if 0 <= m < len(UNITS4) else (None, None) for m in (n, n - 1, n - 2)]
    if n >= 2:
        SCHEDULE += [("turn4", *u[2])]
    if n < len(UNITS4):
        SCHEDULE += [("q4", *u[0])]
        if u[0][1] == 1 and u[0][0] + 1 < KV:
            SCHEDULE += [("w", f"wxq{u[0][0] + 1}")]
        if n == 7:
            SCHEDULE += [("w", "wdown")]
    if n >= 2:
        SCHEDULE += [("out4", *u[2])]
        if u[2][1] == 1 and u[2][0] + 1 < KV:
            SCHEDULE += [("w", f"wxo{u[2][0] + 2}")] if u[2][0] + 2 < KV else []
    if n == 1:
        SCHEDULE += [("w", "wxo1")]
    if n == 0:
        SCHEDULE += [("smax4", *u[0])]
    if 1 <= n <= len(UNITS4):
        SCHEDULE += [("att4", *u[1], *u[0])]
    if n < len(UNITS4):
        SCHEDULE += [("mrow4", *u[0])]
    if n == len(UNITS4):
        SCHEDULE += [("ln", 5, 0)]
SCHEDULE += [("w", "worg"), ("w", "wup"), ("ffn1a", 0), ("ln", 5, 1), ("ffn1b", 0), ("ffn1a", 1), ("ffn1b", 1)]


def program(nc, dram, out, counts, schedule):
    found, total, sems = {}, {}, {}
    ctx = ExitStack()

    def semaphore(kind):
        if kind not in sems:
            sems[kind] = ctx.enter_context(nc.semaphore(kind))
        return sems[kind]

    def ev(kind, *key, by=1):
        total[kind] = total.get(kind, 0) + by
        found[(kind, *key)] = total[kind]
        return semaphore(kind), by

    def on(kind, *key):
        return semaphore(kind), counts.get((kind, *key), 1)

    def so_far(kind):
        return semaphore(kind), total[kind]

    place, banks_of = {}, {}

    def bank(pe, ring, key, *drains):
        n = banks_of.get(id(ring), 0)
        banks_of[id(ring)] = n + 1
        tile, readers = ring[n % len(ring)]
        for reader in readers:
            pe.wait_ge(*on(*reader))
        readers[:] = drains
        place[key] = tile
        return tile

    with ctx:
        def sb(name, shape, dt=F32):
            return ctx.enter_context(nc.sbuf_tensor(name, shape, dt))

        X = sb("X", [P, B * NI, D])
        H = sb("H", [P, NI, D])
        HH = sb("HH", [P, B, C, T], F32R)
        HL = sb("HL", [P, B, C, T], F32R)
        STK = sb("STK", [P, 16384], F32R)
        STAGE = [sb(f"stage{n}", [P, 2048]) for n in range(2)]
        WH = [sb(f"WH{n}", [P, 2048], F32R) for n in range(3)]
        WL = [sb(f"WL{n}", [P, 2048], F32R) for n in range(3)]
        PT = [sb(f"PT{n}", [P, 1536]) for n in range(2)]
        VX = sb("VX", [P, 5184])
        SG = sb("SG", [P, 2048], F32R)
        ON = sb("ON", [P, 1024])
        KS0 = sb("KS0", [P, B, T], F32R)
        KL0 = sb("KL0", [HD, B, T], F32R)
        V0 = sb("V0", [P, B, NI, 2 * HD])
        MT = sb("MT", [NH, T], F32R)
        MX = sb("MX", [P, B, NI, NH])
        DIAG = sb("DIAG", [P, 2, 512], BF16)
        ident = sb("ident", [P, P])
        negid = sb("negid", [P, P])
        identb = sb("identb", [P, P], BF16)
        onesb = sb("onesb", [P, P], BF16)
        mask_s = sb("mask_s", [P, P], BF16)
        mask_t = sb("mask_t", [P, P], BF16)
        rows_a = sb("rows_a", [4, P])
        rows_b = sb("rows_b", [4, P])
        tri = sb("tri", [P, E0, E0])
        stats = sb("stats", [P, NI, 6])
        mv = sb("mv", [P, NI, 2])
        var = sb("var", [P, NI])
        rstd = sb("rstd", [P, NI])
        minushalf = sb("minushalf", [P, NI])
        sc = sb("sc", [P, 16])
        biases = sb("biases", [P, 3, C])
        rden = sb("rden", [P, NH])
        rt = sb("rt", [P, NI, 4, E0])
        rc = sb("rc", [P, NI, 2, E0 * E0])
        small = sb("small", [P, 64])
        keys_t = sb("keys_t", [P, E1])
        wqx = sb("wqx", [P, C, P])

        ringA = [(ctx.enter_context(nc.psum_tensor(f"psA{n}", [P, 512], F32)), []) for n in range(5)]
        ringB = [(ctx.enter_context(nc.psum_tensor(f"psB{n}", [P, 512], F32)), []) for n in range(3)]

        def q2n(b):
            return VX[:, b * 1024:(b + 1) * 1024].bitcast(BF16).rearrange("p (c n) -> p c n", c=C)

        def corr(b):
            return VX[:, 2048 + b * 512:2560 + b * 512]

        bias0 = VX[:, 3072:3584]
        def q1t(b):
            return VX[:, 3584 + b * 512:4096 + b * 512].bitcast(BF16).rearrange("p (c t) -> p c t", c=C)

        q1n = VX[:, 4608:5120].bitcast(BF16).rearrange("p (i n) -> p i n", i=NI)
        VP = VX[:, 0:NG * 17].rearrange("p (g d) -> p g d", d=17)
        OTS = VX[:, 1088:1088 + 4096].rearrange("p (h t) -> p h t", t=P)
        def vx(b):
            return VX[:, b * 2328:(b + 1) * 2328].rearrange("p (s k d) -> p s k d", s=6, k=KV)

        def qs0(b):
            return STK[:, b * 8192:(b + 1) * 8192].rearrange("p (h t) -> p h t", h=NH)

        def st1(u, what):
            o = (u % 2) * 8192 + what * 4096
            return STK[:, o:o + 4096].rearrange("p (h t) -> p h t", h=NH)

        def group(u, what, rows, g):
            o = (u % 2) * 8192 + what * 4096 + g
            return STK[rows, o:o + 32 * 127 + 1:32].bitcast(F32)

        def kx(b, half):
            o = b * 6144 + half * 3072
            return STK[:, o:o + 3072].rearrange("p (k s) -> p k s", k=KV)

        def qx(n, half):
            o = 12288 + (n % 2) * 2048 + half * 1024
            return STK[:, o:o + 1024].rearrange("p (h t) -> p h t", h=GQ)

        sg4 = SG[:, :].rearrange("p (s m t) -> p s m t", s=2, m=C)
        sg1 = SG[:, :].rearrange("p (s m t) -> p s m t", s=4, m=C)
        sg3 = SG[:, 0:1536].rearrange("p (s c t) -> p s c t", s=2, c=3)
        sgh = SG[:, 0:512].rearrange("p (s t) -> p s t", s=2)

        expand = ON[0:1, 0:D]

        def sent0(g):
            return ON[g % 2 * 32:g % 2 * 32 + 2 * HD, :].rearrange("p (h t) -> p h t", h=4)

        def item(name):
            _, r, c, slot = ITEMS[ITEM[name]]
            return tuple(w[slot][:, 0:r * c].rearrange("p (r c) -> p r c", r=r) for w in (WH, WL))

        def plain(ap):
            return ap.bitcast(F32)

        last_use = {"wq0": ("p_v0", 1), "wkv0": ("p_v0", 1), "wo0": ("p_y", "out0", 1, 1), "wbase": ("p_y", "ffn0", 1, 1),
                    "wexp": ("p_y", "ffn0", 1, 1), "wexpb": ("p_y", "ffn0", 1, 1), "wq1": ("p_q1", 1, 0, 1), "wk1": ("p_q1", 1, 1, 1),
                    "wv1": ("p_q1", 1, 2, 1), "wxk": ("p_kx", "kvlat", 1, 3), "wxv": ("p_vx", "kvlat", 1, 1),
                    "ctxt0": ("p_vx", "kvctx", 0, 3), "ctxt1": ("p_vx", "kvctx", 1, 3)}
        for kv in range(KV):
            last_use[f"wxq{kv}"] = ("p_q4", kv, 1, 1)
            last_use[f"wxo{kv}"] = ("p_y", "out4", kv, 1, 1)
        scratch0 = nc.dram_tensor("scratch0", (B, 2, D, T), F32, kind="Internal").ap()
        scratch1 = nc.dram_tensor("scratch1", (B, 3, D, T), F32, kind="Internal").ap()
        scratch3 = nc.dram_tensor("scratch3", (B, 2, D, T), F32, kind="Internal").ap()
        scratch2 = nc.dram_tensor("scratch2", (B * NI, D, P), F32, kind="Internal").ap()
        proj1 = [v.rearrange("p (m t) -> p m t", m=C) for v in (H[:, :, :].rearrange("p i d -> p (i d)"), ON[:, :], PT[1][:, 0:1024])]
        rsum0 = VX[:, 4096:4096 + T]
        on0 = H[:, :, :].rearrange("p i d -> p (i d)").rearrange("p (c t) -> p c t", c=C)
        ot0 = plain(SG[:, 0:1024]).rearrange("p (c t) -> p c t", c=C)
        sum0 = plain(SG[:, 1024:2048]).rearrange("p (c t) -> p c t", c=C)
        block = ctx.enter_context(nc.Block())

        @block.tensor
        def _(pe):
            def split_mm(o, sh, sl, mh, ml, first, last):
                pe.matmul(o, sh, mh, start=first, stop=False)
                pe.matmul(o, sh, ml, start=False, stop=False)
                return pe.matmul(o, sl, mh, start=False, stop=last)

            def scores0(pe, b, n):
                if n == 0:
                    pe.wait_ge(*on("consts"))
                    pe.wait_ge(*on(f"d_q0_{b}"))
                    pe.wait_ge(*on(f"d_k0_{b}"))
                i, g = (0, n) if n < 8 else (1, n - 8)
                per = 4 // (i + 1)
                t = bank(pe, ringA, ("s0", b, n), ("m0", b, n))
                tv = t[:, :].rearrange("p (h k) -> p h k", h=per)
                pe.matmul(tv[:, :, i * P:(i + 1) * P], identb[:, :], mask_s[:, :].unsqueeze(1).broadcast_to([P, per, P]),
                          start=True, stop=False, skip_group_check=True)
                for j in range(per):
                    last = pe.matmul(tv[:, j, :], qs0(b)[0:48, g * per + j, i * P:(i + 1) * P], KS0[0:48, b, 0:(i + 1) * P],
                                     start=False, stop=True, skip_group_check=True)
                last.then_inc(*ev("p_s0", b, n))

            def scores1(pe, u, g4):
                if g4 == 0:
                    pe.wait_ge(*on(f"d_l1_{u % 2}", u))
                t = bank(pe, ringA, ("s1", u, g4), ("m1", u, g4))
                for j in range(4):
                    g = 4 * g4 + j
                    last = pe.matmul(t[:, j * P:(j + 1) * P], group(u, 0, slice(0, 20), g), group(u, 1, slice(0, 20), g), start=True, stop=True)
                last.then_inc(*ev("p_s1", u, g4))

            def turn1(pe, u):
                t = bank(pe, ringA, ("v1", u), ("vp", u))
                for g in range(NG):
                    last = pe.transpose(t[:, g * HD:(g + 1) * HD], group(u, 0, slice(64, 80), g), ident[64:80, 64:80])
                last.then_inc(*ev("p_v1", u))

            def scores4(pe, kv, b, n):
                i, h, j = n // 8, n // 2 % 4, n % 2
                if n == 0:
                    pe.wait_ge(*on("q4_low", kv, b, 1))
                    pe.wait_ge(*on("kx_low", "kvlat", b, KV - 1))
                t = bank(pe, ringA, ("s4", kv, b, n), ("m4", kv, b, n))
                pe.matmul(t[:, 0:384], qx(2 * kv + b, 0)[0:XD, h, i * P:(i + 1) * P], kx(b, 0)[0:XD, kv, j * 384:(j + 1) * 384],
                          start=True, stop=True).then_inc(*ev("p_s4", kv, b, n))

            def values0(pe, b, g):
                pt = PT[g % 2]
                pe.wait_ge(*on("e0", b, g, 2))
                for j in range(2):
                    t = bank(pe, ringB, ("o0", b, g, j), ("on0", b, g, j))
                    tv = t[0:2 * HD, :].rearrange("p (h q) -> p h q", h=2)
                    late = pt[:, 1024 + j * T:1024 + (j + 1) * T].rearrange("p (h q) -> p h q", h=2)
                    pe.matmul(t[0:2 * HD, :], V0[:, b, 0, :], pt[:, j * 512:(j + 1) * 512], start=True, stop=False, skip_group_check=True)
                    pe.matmul(tv[:, :, P:T], V0[:, b, 1, :], late, start=False, stop=True, skip_group_check=True).then_inc(*ev("p_o0", b, g, j))

            pe.wait_ge(*on("ident"))
            for step in schedule:
                what, *k = step
                if what == "ln":
                    s, b = k
                    for i in range(NI):
                        pe.wait_ge(*on("h", s, b, i))
                        if s == 1:
                            t = bank(pe, ringA, ("hT", s, b, i), ("q1T", b, i))
                            tv = t[:, 0:256].bitcast(BF16)
                            for c in range(C):
                                last = pe.transpose(tv[:, c * P:(c + 1) * P], q1n[:, i, c * P:(c + 1) * P], identb[:, :])
                        else:
                            t = bank(pe, ringA, ("hT", s, b, i), ("h_low", s, b, i))
                            for c in range(C):
                                last = pe.transpose(t[:, c * P:(c + 1) * P], H[:, i, c * P:(c + 1) * P], ident[:, :])
                        last.then_inc(*ev("p_hT", s, b, i))
                elif what == "qkv0":
                    b, = k
                    pe.wait_ge(*on("h_low", 0, b, NI - 1))
                    wh, wl = (pe.wait_ge(*on("split", "wq0")), item("wq0"))[1]
                    for mp in range(2):
                        t = bank(pe, ringA, ("q0", b, mp), ("q0_low", b, mp))
                        for j in range(2):
                            m = 2 * mp + j
                            for c in range(C):
                                last = split_mm(t[:, j * T:(j + 1) * T], wh[:, c, m * P:(m + 1) * P], wl[:, c, m * P:(m + 1) * P],
                                                HH[:, b, c, :], HL[:, b, c, :], c == 0, c == C - 1)
                        last.then_inc(*ev("p_q0", b, mp))
                    pe.wait_ge(*on("split", "wkv0"))
                    wh, wl = item("wkv0")
                    t = bank(pe, ringA, ("k0", b), ("k0_low", b))
                    for c in range(C):
                        last = split_mm(t[0:HD, 0:T], wh[:, c, 0:HD], wl[:, c, 0:HD], HH[:, b, c, :], HL[:, b, c, :], c == 0, c == C - 1)
                    last.then_inc(*ev("p_k0", b))
                    t = bank(pe, ringA, ("v0", b), ("v0_out", b))
                    for i in range(NI):
                        for c in range(C):
                            last = split_mm(t[:, i * HD:(i + 1) * HD], HH[:, b, c, i * P:(i + 1) * P], HL[:, b, c, i * P:(i + 1) * P],
                                            wh[:, c, HD:2 * HD], wl[:, c, HD:2 * HD], c == 0, c == C - 1)
                    last.then_inc(*ev("p_v0", b))
                elif what == "smax0":
                    b, = k
                    for n in range(24):
                        scores0(pe, b, n)
                elif what == "mrow0":
                    b, = k
                    pe.wait_ge(*on("m0", b, 23))
                    t = bank(pe, ringA, ("mr0", b), ("mrow0", b))
                    for i in range(NI):
                        last = pe.transpose(t[0:NH, i * P:(i + 1) * P], MX[:, b, i, :], ident[:, :])
                    last.then_inc(*ev("p_mr0", b))
                elif what == "att0":
                    b, other, g0, g1 = k
                    pe.wait_ge(*on(f"d_m0_{b}"))
                    pe.wait_ge(*on("v0_out", b))
                    for g in range(g0, g1):
                        if other is not None:
                            for n in range(3 * g, 3 * g + 3):
                                scores0(pe, other, n)
                        for j in range(2):
                            t = bank(pe, ringA, ("t0", b, g, j), ("e0", b, g, j))
                            tv = t[:, :].rearrange("p (h q) -> p h q", h=2)
                            pe.matmul(tv[:, :, 0:P], identb[:, :], mask_t[:, :].unsqueeze(1).broadcast_to([P, 2, P]),
                                      start=True, stop=False, skip_group_check=True)
                            pe.matmul(tv, KS0[0:49, b, 0:P], qs0(b)[0:49, g * 4 + j * 2:g * 4 + j * 2 + 2, :],
                                      start=False, stop=True, skip_group_check=True).then_inc(*ev("p_t0", b, g, j))
                        t = bank(pe, ringA, ("t0", b, g, 2), ("e0", b, g, 2))
                        tv = t[:, :].rearrange("p (h q) -> p h q", h=4)
                        pe.matmul(tv, identb[:, :], mask_t[:, :].unsqueeze(1).broadcast_to([P, 4, P]),
                                  start=True, stop=False, skip_group_check=True)
                        pe.matmul(tv, KS0[0:49, b, P:T], qs0(b)[0:49, g * 4:g * 4 + 4, P:T],
                                  start=False, stop=True, skip_group_check=True).then_inc(*ev("p_t0", b, g, 2))
                        if g >= 1:
                            values0(pe, b, g - 1)
                    if g1 == NH // 4:
                        values0(pe, b, g1 - 1)
                elif what == "out0":
                    b, = k
                    pe.wait_ge(*on("split", "wo0"))
                    wh, wl = item("wo0")
                    pe.wait_ge(*on("ot0_low", b, C - 1))
                    for i in range(NI):
                        t = bank(pe, ringA, ("y", "out0", b, i), ("x", "out0", b, i))
                        for c in range(C):
                            last = split_mm(t[:, :], HH[:, b, c, i * P:(i + 1) * P], HL[:, b, c, i * P:(i + 1) * P],
                                            wh[:, c, :], wl[:, c, :], c == 0, c == C - 1)
                        last.then_inc(*ev("p_y", "out0", b, i))
                elif what == "ctxq":
                    b, = k
                    pe.wait_ge(*on("q2", b))
                    t = bank(pe, ringA, ("cs", b), ("corr", b))
                    for c in range(C):
                        last = pe.matmul(t[:, :], onesb[:, :], q2n(b)[:, c, :], start=c == 0, stop=c == C - 1)
                    last.then_inc(*ev("p_cs", b))
                elif what == "quant":
                    b, = k
                    for i in range(NI):
                        pe.wait_ge(*on("q1T", b, i))
                        t = bank(pe, ringA, ("y", "quant", b, i), ("x1t", b, i))
                        for c in range(C):
                            last = pe.matmul(t[:, :], q1t(b)[:, c, i * P:(i + 1) * P], q2n(b)[:, c, :], start=c == 0, stop=c == C - 1)
                        last.then_inc(*ev("p_y", "quant", b, i))
                elif what == "ffn0":
                    b, = k
                    pe.wait_ge(*on("h_low", 2, b, NI - 1))
                    pe.wait_ge(*on("split", "wexp"))
                    wh, wl = item("wexp")
                    t = bank(pe, ringA, ("g0", b), ("hw", b, NI - 1))
                    n = E0 * R0 + E0
                    for i in range(NI):
                        for c in range(C):
                            last = split_mm(t[:, i * n:(i + 1) * n], HH[:, b, c, i * P:(i + 1) * P], HL[:, b, c, i * P:(i + 1) * P],
                                            wh[:, c, :], wl[:, c, :], c == 0, c == C - 1)
                    last.then_inc(*ev("p_g0", b))
                    pe.wait_ge(*on("split", "wbase"))
                    wh, wl = item("wbase")
                    outs = []
                    for i in range(NI):
                        t = bank(pe, ringB, ("y", "ffn0", b, i), ("x", "ffn0", b, i))
                        outs.append(t)
                        for c in range(C):
                            split_mm(t[:, :], HH[:, b, c, i * P:(i + 1) * P], HL[:, b, c, i * P:(i + 1) * P],
                                     wh[:, c, :], wl[:, c, :], c == 0, False)
                    pe.wait_ge(*on("hw", b, NI - 1))
                    t = bank(pe, ringA, ("hwt", b), ("hwt_low", b))
                    for i in range(NI):
                        last = pe.transpose(t[:, i * P:(i + 1) * P], ON[:, i * D:i * D + P], ident[:, :])
                    last.then_inc(*ev("p_hwt", b))
                    pe.wait_ge(*on("hwt_low", b))
                    pe.wait_ge(*on("split", "wexpb"))
                    wh, wl = item("wexpb")
                    for i in range(NI):
                        split_mm(outs[i][:, :], sgh[:, 0, i * P:(i + 1) * P], sgh[:, 1, i * P:(i + 1) * P], wh[:, 0, :], wl[:, 0, :],
                                 False, True).then_inc(*ev("p_y", "ffn0", b, i))
                elif what == "qkv1":
                    b, = k
                    pe.wait_ge(*on("h_low", 3, b, NI - 1))
                    for n, name in enumerate(("wq1", "wk1", "wv1")):
                        pe.wait_ge(*on("split", name))
                        wh, wl = item(name)
                        for mp in range(2):
                            t = bank(pe, ringA, ("q1", b, n, mp), ("qkv1", b, n, mp))
                            for j in range(2):
                                m = 2 * mp + j
                                for c in range(C):
                                    last = split_mm(t[:, j * T:(j + 1) * T], wh[:, c, m * P:(m + 1) * P], wl[:, c, m * P:(m + 1) * P],
                                                    HH[:, b, c, :], HL[:, b, c, :], c == 0, c == C - 1)
                            last.then_inc(*ev("p_q1", b, n, mp))
                elif what == "smax1":
                    u, = k
                    for g4 in range(NG // 4):
                        scores1(pe, u, g4)
                    turn1(pe, u)
                elif what == "att1":
                    u, other = k
                    pe.wait_ge(*on("vp", u))
                    for g4 in range(NG // 4 + 1):
                        if g4 < NG // 4:
                            pe.wait_ge(*on("diag", u, g4))
                            t = bank(pe, ringA, ("t1", u, g4), ("e1", u, g4))
                            pe.matmul(t[:, :], onesb[:, :], DIAG[:, g4 % 2, :], start=True, stop=False, skip_group_check=True)
                            for j in range(4):
                                g = 4 * g4 + j
                                last = pe.matmul(t[:, j * P:(j + 1) * P], group(u, 1, slice(0, 20), g),
                                                 group(u, 0, slice(0, 20), g), start=False, stop=True, skip_group_check=True)
                            last.then_inc(*ev("p_t1", u, g4))
                            if other is not None:
                                scores1(pe, other, g4)
                        if g4 >= 1:
                            n = g4 - 1
                            pe.wait_ge(*on("e1", u, n))
                            t = bank(pe, ringB, ("o1", u, n), ("ots", u, n))
                            pt = PT[n // 3 % 2][:, n % 3 * 512:(n % 3 + 1) * 512]
                            for j in range(4):
                                last = pe.matmul(t[0:17, j * P:(j + 1) * P], VP[:, 4 * n + j, :], pt[:, j * P:(j + 1) * P],
                                                 start=True, stop=True)
                            last.then_inc(*ev("p_o1", u, n))
                    if other is not None:
                        turn1(pe, other)
                elif what == "out1":
                    u, = k
                    pe.wait_ge(*on("d_o1", u))
                    t = bank(pe, ringB, ("den1", u), ("rden1", u))
                    pe.transpose(t[:, 0:NH], ON[0:NH, 512:512 + P], ident[0:NH, 0:NH]).then_inc(*ev("p_den1", u))
                    t = bank(pe, ringB, ("y", "out1", u), ("x1o", u))
                    for m in range(C):
                        last = pe.transpose(t[:, m * P:(m + 1) * P], ON[:, m * P:(m + 1) * P], ident[:, :])
                    last.then_inc(*ev("p_y", "out1", u))
                elif what in ("kvctx", "kvlat"):
                    b, = k
                    if what == "kvctx":
                        pe.wait_ge(*on("split", f"ctxt{b}"))
                        xh, xl = item(f"ctxt{b}")
                        n, tiles = CTX, 4
                    else:
                        pe.wait_ge(*on("h_low", 4, b, NI - 1))
                        xh, xl = HH[:, b, :, :], HL[:, b, :, :]
                        n, tiles = T, 2
                    pe.wait_ge(*on("split", "wxk"))
                    wh, wl = item("wxk")
                    for kv in range(KV):
                        t = bank(pe, ringA, (what, b, kv), ("kx_low", what, b, kv))
                        for c in range(C):
                            last = split_mm(t[0:XD, 0:n], wh[:, c, kv * XD:(kv + 1) * XD], wl[:, c, kv * XD:(kv + 1) * XD],
                                            xh[:, c, :], xl[:, c, :], c == 0, c == C - 1)
                        last.then_inc(*ev("p_kx", what, b, kv))
                    pe.wait_ge(*on("split", "wxv"))
                    wh, wl = item("wxv")
                    for st in range(tiles):
                        t = bank(pe, ringA, (what, "v", b, st), ("vx", what, b, st))
                        for c in range(C):
                            last = split_mm(t[:, 0:KV * XD], xh[:, c, st * P:(st + 1) * P], xl[:, c, st * P:(st + 1) * P],
                                            wh[:, c, :], wl[:, c, :], c == 0, c == C - 1)
                        last.then_inc(*ev("p_vx", what, b, st))
                elif what == "q4":
                    kv, b = k
                    pe.wait_ge(*on("split", f"wxq{kv}"))
                    pe.wait_ge(*on("h_low", 4, b, NI - 1))
                    wh, wl = item(f"wxq{kv}")
                    for j in range(2):
                        t = bank(pe, ringA, ("q4", kv, b, j), ("q4_low", kv, b, j))
                        for h in range(2):
                            f = (2 * j + h) * XD
                            for c in range(C):
                                last = split_mm(t[0:XD, h * T:(h + 1) * T], wh[:, c, f:f + XD], wl[:, c, f:f + XD],
                                                HH[:, b, c, :], HL[:, b, c, :], c == 0, c == C - 1)
                        last.then_inc(*ev("p_q4", kv, b, j))
                elif what == "smax4":
                    kv, b = k
                    for n in range(16):
                        scores4(pe, kv, b, n)
                elif what == "mrow4":
                    kv, b = k
                    pe.wait_ge(*on("m4s", kv, b))
                    t = bank(pe, ringA, ("mr4", kv, b), ("mrow4", kv, b))
                    pe.transpose(t[0:8, 0:P], small[:, 16:24], ident[:, :]).then_inc(*ev("p_mr4", kv, b))
                elif what == "att4":
                    kv, b, *other = k
                    n = 2 * kv + b
                    pe.wait_ge(*on("d_m4", kv, b))
                    pe.wait_ge(*on("vx", "kvlat", b, 1))
                    pe.wait_ge(*on("kx_ones"))
                    os = [bank(pe, ringB, ("o4", kv, b, i), ("on4", kv, b, i)) for i in range(NI)]

                    def values4(h):
                        pt = PT[h % 2][:, :].rearrange("p (s q) -> p s q", q=T)
                        pe.wait_ge(*on("e4", kv, b, h, 2))
                        for i in range(NI):
                            for st in range(6):
                                last = pe.matmul(os[i][:, h * (XD + 1):(h + 1) * (XD + 1)], pt[:, st, i * P:(i + 1) * P], vx(b)[:, st, kv, :],
                                                 start=st == 0, stop=st == 5)
                        last.then_inc(*ev("p_o4", kv, b, h))
                    for h in range(GQ):
                        for s2 in range(3):
                            t = bank(pe, ringA, ("t4", kv, b, h, s2), ("e4", kv, b, h, s2))
                            for j in range(2):
                                o = t[:, j * T:(j + 1) * T]
                                ks = slice((2 * s2 + j) * P, (2 * s2 + j + 1) * P)
                                pe.matmul(o, kx(b, 0)[0:XD + 1, kv, ks], qx(n, 0)[0:XD + 1, h, :], start=True, stop=False)
                                pe.matmul(o, kx(b, 0)[0:XD, kv, ks], qx(n, 1)[0:XD, h, :], start=False, stop=False)
                                last = pe.matmul(o, kx(b, 1)[0:XD, kv, ks], qx(n, 0)[0:XD, h, :], start=False, stop=True)
                            last.then_inc(*ev("p_t4", kv, b, h, s2))
                            if other[0] is not None:
                                scores4(pe, *other, 4 * h + s2)
                        if other[0] is not None:
                            scores4(pe, *other, 4 * h + 3)
                        if h >= 1:
                            values4(h - 1)
                    values4(GQ - 1)
                elif what == "turn4":
                    kv, b = k
                    for i in range(NI):
                        pe.wait_ge(*on("on4", kv, b, i))
                        t = bank(pe, ringA, ("ot4", kv, b, i), ("ot4_low", kv, b, i))
                        for c in range(3):
                            last = pe.transpose(t[:, c * P:(c + 1) * P], ON[:, i * 384 + c * P:i * 384 + (c + 1) * P], ident[:, :])
                        last.then_inc(*ev("p_ot4", kv, b, i))
                elif what == "out4":
                    kv, b = k
                    pe.wait_ge(*on("split", f"wxo{kv}"))
                    wh, wl = item(f"wxo{kv}")
                    for i in range(NI):
                        pe.wait_ge(*on("ot4_low", kv, b, i))
                        t = bank(pe, ringA, ("y", "out4", kv, b, i), ("x", "out4", kv, b, i))
                        for c in range(3):
                            last = split_mm(t[:, :], sg3[:, 0, c, i * P:(i + 1) * P], sg3[:, 1, c, i * P:(i + 1) * P],
                                            wh[:, c, :], wl[:, c, :], c == 0, c == 2)
                        last.then_inc(*ev("p_y", "out4", kv, b, i))
                elif what == "ffn1a":
                    b, = k
                    pe.wait_ge(*on("mean", b))
                    pe.wait_ge(*on("d_mix"))
                    t = bank(pe, ringA, ("cq", b), ("cq", b))
                    for c in range(C):
                        last = pe.matmul(t[:, 0:1], wqx[:, c, :], small[:, 32 + c:33 + c], start=c == 0, stop=c == C - 1)
                    last.then_inc(*ev("p_cq", b))
                    pe.wait_ge(*on("cq", b))
                    t = bank(pe, ringA, ("cs1", b), ("cexp", b))
                    pe.matmul(t[0:1, 0:E1], small[:, 36:37], keys_t[:, :], start=True, stop=True).then_inc(*ev("p_cs1", b))
                    pe.wait_ge(*on("split", "wdown"))
                    wh, wl = item("wdown")
                    pe.wait_ge(*on("h_low", 5, b, NI - 1))
                    for mp in range(2):
                        t = bank(pe, ringB, ("dn", b, mp), ("dn_low", b, mp))
                        for j in range(2):
                            m = 2 * mp + j
                            for c in range(C):
                                last = split_mm(t[:, j * T:(j + 1) * T], wh[:, c, m * P:(m + 1) * P], wl[:, c, m * P:(m + 1) * P],
                                                HH[:, b, c, :], HL[:, b, c, :], c == 0, c == C - 1)
                        last.then_inc(*ev("p_dn", b, mp))
                    pe.wait_ge(*on("coef", b))
                    t = bank(pe, ringA, ("cc", b), ("cc", b))
                    for m in range(C):
                        last = pe.matmul(t[:, m:m + 1], expand[0:1, m * P:(m + 1) * P], ident[0:1, 0:1], start=True, stop=True)
                    last.then_inc(*ev("p_cc", b))
                elif what == "ffn1b":
                    b, = k
                    pe.wait_ge(*on("split", "worg"))
                    oh, ol = item("worg")
                    pe.wait_ge(*on("split", "wup"))
                    uh, ul = item("wup")
                    for i in range(NI):
                        t = bank(pe, ringA, ("y", "ffn1", b, i), ("x", "ffn1", b, i))
                        for c in range(C):
                            split_mm(t[:, :], HH[:, b, c, i * P:(i + 1) * P], HL[:, b, c, i * P:(i + 1) * P],
                                     oh[:, c, :], ol[:, c, :], c == 0, False)
                        pe.wait_ge(*on("dn_low", b, 1))
                        for c in range(C):
                            last = split_mm(t[:, :], sg4[:, 0, c, i * P:(i + 1) * P], sg4[:, 1, c, i * P:(i + 1) * P],
                                            uh[:, c, :], ul[:, c, :], False, c == C - 1)
                        last.then_inc(*ev("p_y", "ffn1", b, i))

        @block.scalar
        def _(act):
            def turned1(act, u):
                act.wait_ge(*on("p_v1", u))
                if u:
                    act.wait_ge(*on("p_o1", u - 1, 7))
                act.wait_ge(*on("vp_ones"))
                act.activation(VP[:, :, 0:HD], place[("v1", u)][:, :].rearrange("p (g d) -> p g d", d=HD), ACT.Copy).then_inc(*ev("vp", u))

            def high0(act, b, c):
                act.wait_ge(*on("p_v0", b))
                act.wait_ge(*on("normed0", b, c))
                act.activation(HH[:, b, c, :], on0[:, c, :], ACT.Copy).then_inc(*ev("ot0_high", b, c))

            def outs1(act, u, g4):
                act.wait_ge(*on("p_o1", u, g4))
                if g4 == 0 and u:
                    act.wait_ge(*on("d_o1", u - 1))
                act.activation(OTS[0:17, :, :].rearrange("p h (j g) -> p g h j", j=4)[:, 4 * g4:4 * g4 + 4, :, :],
                               place[("o1", u, g4)][0:17, :].rearrange("p (g h j) -> p g h j", g=4, h=NH), ACT.Copy).then_inc(*ev("ots", u, g4))

            for step in schedule:
                what, *k = step
                if what == "w":
                    name, = k
                    n = ITEM[name]
                    _, r, c, slot = ITEMS[n]
                    before = [m for m in range(n) if ITEMS[m][3] == slot]
                    if before:
                        act.wait_ge(*on(*last_use[ITEMS[before[-1]][0]]))
                    act.wait_ge(*on(f"d_stage{n % 2}", name))
                    act.activation(WH[slot][:, 0:r * c], STAGE[n % 2][:, 0:r * c], ACT.Copy).then_inc(*ev("split_high", name))
                elif what == "ln":
                    s, b = k
                    for i in range(NI):
                        act.wait_ge(*on("p_hT", s, b, i))
                        t = place[("hT", s, b, i)]
                        if s == 1:
                            act.activation(q1t(b)[:, :, i * P:(i + 1) * P], t[:, 0:256].bitcast(BF16).rearrange("p (c t) -> p c t", c=C),
                                           ACT.Copy).then_inc(*ev("q1T", b, i))
                        else:
                            act.activation(HH[:, b, :, i * P:(i + 1) * P], t[:, :].rearrange("p (c t) -> p c t", c=C),
                                           ACT.Copy).then_inc(*ev("h_high", s, b, i))
                elif what == "qkv0":
                    b, = k
                    if b:
                        act.wait_ge(*on("d_w0_0"))
                    for mp in range(2):
                        act.wait_ge(*on("p_q0", b, mp))
                        act.activation(sg4[:, 0, 2 * mp:2 * mp + 2, :], place[("q0", b, mp)][:, :].rearrange("p (m t) -> p m t", m=2),
                                       ACT.Copy).then_inc(*ev("q0_high", b, mp))
                    act.wait_ge(*on("p_k0", b))
                    act.wait_ge(*on("consts_v"))
                    act.activation(KS0[0:HD, b, :], place[("k0", b)][0:HD, 0:T], ACT.Copy).then_inc(*ev("k0_high", b))
                elif what == "mrow0":
                    b, = k
                    act.wait_ge(*on("p_mr0", b))
                    if b:
                        act.wait_ge(*on("d_m0_0"))
                    act.activation(MT[:, :], place[("mr0", b)][0:NH, 0:T], ACT.Copy, scale=-1.0).then_inc(*ev("mrow0", b))
                elif what == "att0":
                    b, other, g0, g1 = k
                    for g in range(g0, g1):
                        if g >= 2:
                            act.wait_ge(*on("p_o0", b, g - 2, 1))
                        elif b:
                            act.wait_ge(*on("p_o0", b - 1, 6 + g, 1))
                        if g in (5, 7):
                            high0(act, b, (g - 5) // 2)
                        for j in range(3):
                            act.wait_ge(*on("p_t0", b, g, j))
                            act.activation(PT[g % 2][:, j * 512:(j + 1) * 512], place[("t0", b, g, j)][:, :], ACT.Exp,
                                           scale=0.25).then_inc(*ev("e0", b, g, j))
                    if g1 == NH // 4:
                        high0(act, b, 2)
                elif what == "out0":
                    b, = k
                    high0(act, b, C - 1)
                elif what == "ffn0":
                    b, = k
                    act.wait_ge(*on("lmm", b))
                    act.activation(rt[:, :, 1, :], rt[:, :, 0, :], ACT.Exp).then_inc(*ev("lexp", b))
                    act.wait_ge(*on("p_hwt", b))
                    act.activation(sgh[:, 0, :], place[("hwt", b)][:, 0:T], ACT.Copy).then_inc(*ev("hwt_high", b))
                elif what == "smax1":
                    turned1(act, k[0])
                elif what == "att1":
                    u, other = k
                    for g4 in range(NG // 4):
                        act.wait_ge(*on("p_t1", u, g4))
                        if g4 == 0 and u == 0:
                            act.wait_ge(*on("d_w1_1", 2))
                        if g4 >= 6:
                            act.wait_ge(*on("p_o1", u, g4 - 6))
                        act.activation(PT[g4 // 3 % 2][:, g4 % 3 * 512:(g4 % 3 + 1) * 512], place[("t1", u, g4)][:, :], ACT.Exp,
                                       scale=0.25).then_inc(*ev("e1", u, g4))
                        if g4 >= 2:
                            outs1(act, u, g4 - 2)
                    outs1(act, u, 6)
                    outs1(act, u, 7)
                    if other is not None:
                        turned1(act, other)
                elif what in ("kvctx", "kvlat"):
                    b, = k
                    s0, n = (0, CTX) if what == "kvctx" else (CTX, T)
                    for kv in range(KV):
                        act.wait_ge(*on("p_kx", what, b, kv))
                        act.activation(kx(b, 0)[0:XD, kv, s0:s0 + n], place[(what, b, kv)][0:XD, 0:n], ACT.Copy).then_inc(*ev("kx_high", what, b, kv))
                    for st in range(n // P):
                        act.wait_ge(*on("p_vx", what, b, st))
                        act.wait_ge(*on("vx_ones"))
                        act.activation(vx(b)[:, s0 // P + st, :, 0:XD], place[(what, "v", b, st)][:, 0:KV * XD].rearrange("p (k d) -> p k d", k=KV),
                                       ACT.Copy).then_inc(*ev("vx", what, b, st))
                elif what == "q4":
                    kv, b = k
                    n = 2 * kv + b
                    for j in range(2):
                        act.wait_ge(*on("p_q4", kv, b, j))
                        if n >= 2:
                            act.wait_ge(*on("p_t4", (n - 2) // 2, n % 2, GQ - 1, 2))
                        act.activation(qx(n, 0)[0:XD, 2 * j:2 * j + 2, :], place[("q4", kv, b, j)][0:XD, :].rearrange("p (h t) -> p h t", h=2),
                                       ACT.Copy).then_inc(*ev("q4_high", kv, b, j))
                elif what == "mrow4":
                    kv, b = k
                    act.wait_ge(*on("p_mr4", kv, b))
                    if kv or b:
                        act.wait_ge(*on("d_m4", *UNITS4[2 * kv + b - 1]))
                    act.activation(MT[0:8, 0:P], place[("mr4", kv, b)][0:8, 0:P], ACT.Copy, scale=-1.0).then_inc(*ev("mrow4", kv, b))
                elif what == "att4":
                    kv, b, *other = k
                    for h in range(GQ):
                        if h >= 2:
                            act.wait_ge(*on("p_o4", kv, b, h - 2))
                        elif kv or b:
                            act.wait_ge(*on("p_o4", *UNITS4[2 * kv + b - 1], h + 2))
                        for s2 in range(3):
                            act.wait_ge(*on("p_t4", kv, b, h, s2))
                            act.activation(PT[h % 2][:, s2 * 512:(s2 + 1) * 512], place[("t4", kv, b, h, s2)][:, :], ACT.Exp,
                                           scale=SX_SCALE).then_inc(*ev("e4", kv, b, h, s2))
                elif what == "turn4":
                    kv, b = k
                    for i in range(NI):
                        act.wait_ge(*on("p_ot4", kv, b, i))
                        if kv or b:
                            act.wait_ge(*on("p_y", "out4", *UNITS4[2 * kv + b - 1], i))
                        act.activation(sg3[:, 0, :, i * P:(i + 1) * P], place[("ot4", kv, b, i)][:, 0:384].rearrange("p (c t) -> p c t", c=3),
                                       ACT.Copy).then_inc(*ev("ot4_high", kv, b, i))
                elif what == "ffn1a":
                    b, = k
                    act.wait_ge(*on("cmax", b))
                    act.activation(small[0:1, 48:56], place[("cs1", b)][0:1, 0:E1], ACT.Exp, scale=1.0 / math.sqrt(128.0),
                                   bias=small[0:1, 41:42]).then_inc(*ev("cexp", b))
                    if b:
                        act.wait_ge(*on("p_y", "ffn1", 0, NI - 1))
                    for mp in range(2):
                        act.wait_ge(*on("p_dn", b, mp))
                        act.wait_ge(*on("cc", b))
                        for j in range(2):
                            m = 2 * mp + j
                            act.activation(sg4[:, 0, m, :], place[("dn", b, mp)][:, j * T:(j + 1) * T], ACT.Copy,
                                           scale=small[:, 44 + m:45 + m]).then_inc(*ev("dn_high", b, m))

        @block.vector
        def _(dve):
            def link(ins):
                ins.then_inc(*ev("v_step"))
                dve.wait_ge(semaphore("v_step"), total["v_step"])

            def maxima0(dve, b, n):
                i, g = (0, n) if n < 8 else (1, n - 8)
                per = 4 // (i + 1)
                dve.wait_ge(*on("p_s0", b, n))
                dve.tensor_reduce(MX[:, b, i, g * per:(g + 1) * per], place[("s0", b, n)][:, :].rearrange("p (h k) -> p h k", h=per),
                                  AX, ALU.max).then_inc(*ev("m0", b, n))

            def normed0(dve, b, c):
                dve.wait_ge(*on(f"d_ot0_{c}", b))
                if b or c:
                    dve.wait_ge(*so_far("normed0"))
                link(dve.reciprocal(rsum0, sum0[:, c, :]))
                dve.tensor_tensor(out=on0[:, c, :], in0=ot0[:, c, :], in1=rsum0, op=ALU.mult).then_inc(*ev("normed0", b, c))

            def low0(dve, b, c):
                dve.wait_ge(*on("ot0_high", b, c))
                low(HL[:, b, c, :], on0[:, c, :], HH[:, b, c, :], ("ot0_low", b, c))

            def maxima1(dve, u, g4):
                dve.wait_ge(*on("p_s1", u, g4))
                dve.tensor_reduce(mx1[:, (u % 2) * 32 + 4 * g4:(u % 2) * 32 + 4 * g4 + 4], place[("s1", u, g4)][:, :].rearrange("p (g k) -> p g k", g=4),
                                  AX, ALU.max).then_inc(*ev("m1", u, g4))

            def maxima4(dve, kv, b):
                if kv or b:
                    dve.wait_ge(*on("p_mr4", *UNITS4[2 * kv + b - 1]))
                for n in range(16):
                    dve.wait_ge(*on("p_s4", kv, b, n))
                    dve.tensor_reduce(small[:, n:n + 1], place[("s4", kv, b, n)][:, 0:384], AX, ALU.max).then_inc(*ev("m4", kv, b, n))
                dve.wait_ge(*on("m4", kv, b, 15))
                dve.tensor_reduce(small[:, 16:24], small[:, 0:16].rearrange("p (g j) -> p g j", j=2), AX, ALU.max).then_inc(*ev("m4s", kv, b))

            mx1 = MX[:, :, :, :].rearrange("p b i h -> p (b i h)")

            def low(o, t, high, key):
                dve.tensor_tensor(out=o, in0=t, in1=plain(high), op=ALU.subtract).then_inc(*ev(*key))

            dve.memset(V0[:, :, :, HD:2 * HD], 1.0)
            dve.memset(onesb[:, :], 1.0)
            dve.memset(plain(KS0[:, :, :]), 1.0).then_inc(*ev("consts_v"))
            dve.wait_ge(*on("d_sc"))
            link(dve.reciprocal(sc[:, 4:5], sc[:, 0:1]))
            link(dve.reciprocal(sc[:, 5:6], sc[:, 2:3]))
            link(dve.tensor_scalar(sc[:, 6:7], sc[:, 1:2], -128.0, None, ALU.add))
            link(dve.tensor_scalar(sc[:, 7:8], sc[:, 3:4], -128.0, None, ALU.add))
            link(dve.tensor_tensor(out=sc[:, 8:9], in0=sc[:, 0:1], in1=sc[:, 2:3], op=ALU.mult))
            link(dve.tensor_scalar(sc[:, 9:10], sc[:, 6:7], sc[:, 8:9], -1.0, ALU.mult, ALU.mult))
            link(dve.tensor_scalar(sc[:, 10:11], sc[:, 9:10], sc[:, 7:8], -float(CTX), ALU.mult, ALU.mult))
            link(dve.tensor_scalar(sc[:, 11:12], sc[:, 7:8], -1.0, None, ALU.mult))
            for step in schedule:
                what, *k = step
                if what == "ln":
                    s, b = k
                    if s == 0:
                        dve.wait_ge(*on(f"d_x{b}"))
                    for i in range(NI):
                        last = dve.bn_stats(stats[:, i, :], X[:, 2 * b + i, :])
                    link(last)
                    if s or b:
                        dve.wait_ge(*so_far("h"))
                    if s == 3 and b == 1:
                        dve.wait_ge(*on("d_w1_0", 2))
                    for i in range(NI):
                        last = dve.bn_aggr(mv[:, i, :], stats[:, i, :])
                    link(last)
                    dve.tensor_scalar(var[:, :], mv[:, :, 1], EPS, None, ALU.add).then_inc(*ev("var", s, b))
                    dve.wait_ge(*on("rstd", s, b))
                    for i in range(NI):
                        ins = dve.tensor_scalar(H[:, i, :], X[:, 2 * b + i, :], mv[:, i, 0:1], rstd[:, i:i + 1], ALU.subtract, ALU.mult)
                        if s == 1:
                            link(ins)
                            link(dve.tensor_scalar(H[:, i, :], H[:, i, :], sc[:, 4:5], sc[:, 1:2], ALU.mult, ALU.add))
                            link(dve.tensor_scalar(H[:, i, :], H[:, i, :], 0.0, 255.0, ALU.max, ALU.min))
                            if b:
                                dve.wait_ge(*on("p_hT", 1, 0, i))
                            dve.tensor_scalar(q1n[:, i, :], H[:, i, :], ROUND, ROUND + 128.0, ALU.add, ALU.subtract).then_inc(*ev("h", s, b, i))
                        else:
                            ins.then_inc(*ev("h", s, b, i))
                    if s == 1:
                        for i in range(NI):
                            dve.wait_ge(*on("h", s, b, i))
                            link(dve.tensor_reduce(small[:, 2 * b + i:2 * b + i + 1], q1n[:, i, :], AX, ALU.add))
                            link(dve.tensor_scalar(small[:, 2 * b + i:2 * b + i + 1], small[:, 2 * b + i:2 * b + i + 1], sc[:, 11:12], None, ALU.mult))
                    else:
                        for i in range(NI):
                            dve.wait_ge(*on("p_hT", s, b, i))
                            t = place[("hT", s, b, i)]
                            if s == 5:
                                dve.wait_ge(*on("h_high", s, b, i))
                                link(dve.tensor_reduce(small[:, 24 + 4 * i:28 + 4 * i], t[:, :].rearrange("p (c t) -> p c t", c=C), AX, ALU.add))
                            dve.wait_ge(*on("h_high", s, b, i))
                            low(HL[:, b, :, i * P:(i + 1) * P], t[:, :].rearrange("p (c t) -> p c t", c=C), HH[:, b, :, i * P:(i + 1) * P], ("h_low", s, b, i))
                        if s == 5:
                            link(dve.tensor_tensor(out=small[:, 32:36], in0=small[:, 24:28], in1=small[:, 28:32], op=ALU.add))
                            dve.tensor_scalar(small[:, 32:36], small[:, 32:36], 1.0 / T, None, ALU.mult).then_inc(*ev("mean", b))
                elif what == "qkv0":
                    b, = k
                    for mp in range(2):
                        dve.wait_ge(*on("p_q0", b, mp))
                        dve.wait_ge(*on("q0_high", b, mp))
                        low(sg4[:, 1, 2 * mp:2 * mp + 2, :], place[("q0", b, mp)][:, :].rearrange("p (m t) -> p m t", m=2),
                            sg4[:, 0, 2 * mp:2 * mp + 2, :], ("q0_low", b, mp))
                    dve.wait_ge(*on("k0_high", b))
                    low(KL0[:, b, :], place[("k0", b)][0:HD, 0:T], KS0[0:HD, b, :], ("k0_low", b))
                    dve.wait_ge(*on("p_v0", b))
                    dve.tensor_copy(V0[:, b, :, 0:HD], place[("v0", b)][:, 0:2 * HD].rearrange("p (i d) -> p i d", i=NI)).then_inc(*ev("v0_out", b))
                elif what == "smax0":
                    b, = k
                    for n in range(24):
                        maxima0(dve, b, n)
                elif what == "att0":
                    b, other, g0, g1 = k

                    def copied(g):
                        for j in range(2):
                            dve.wait_ge(*on("p_o0", b, g, j))
                            if b or g >= 2:
                                dve.wait_ge(*on(f"d_on{g % 2}", *((b, g - 2) if g >= 2 else (b - 1, NH // 4 - 2 + g))))
                            dve.tensor_copy(sent0(g)[:, 2 * j:2 * j + 2, :], place[("o0", b, g, j)][0:2 * HD, :].rearrange("p (h t) -> p h t", h=2)
                                            ).then_inc(*ev("on0", b, g, j))
                    for g in range(g0, g1):
                        if other is not None:
                            for n in range(3 * g, 3 * g + 3):
                                maxima0(dve, other, n)
                        if g in (5, 7):
                            low0(dve, b, (g - 5) // 2)
                        if g >= 1:
                            copied(g - 1)
                        if g in (4, 6):
                            normed0(dve, b, (g - 4) // 2)
                    if g1 == NH // 4:
                        copied(g1 - 1)
                        normed0(dve, b, 2)
                        low0(dve, b, 2)
                elif what == "out0":
                    b, = k
                    normed0(dve, b, C - 1)
                    low0(dve, b, C - 1)
                    for i in range(NI):
                        dve.wait_ge(*on("p_y", "out0", b, i))
                        x = X[:, 2 * b + i, :]
                        dve.tensor_tensor(out=x, in0=place[("y", "out0", b, i)][:, :], in1=x, op=ALU.add).then_inc(*ev("x", "out0", b, i))
                    dve.wait_ge(*on("x", "out0", b, NI - 1))
                elif what == "ctxq":
                    b, = k
                    name = f"ctxn{b}"
                    n = ITEM[name]
                    st = STAGE[n % 2]
                    dve.wait_ge(*on(f"d_stage{n % 2}", name))
                    link(dve.tensor_scalar(st[:, :], st[:, :], sc[:, 5:6], sc[:, 3:4], ALU.mult, ALU.add))
                    link(dve.tensor_scalar(st[:, :], st[:, :], 0.0, 255.0, ALU.max, ALU.min))
                    dve.tensor_scalar(q2n(b).rearrange("p c n -> p (c n)"), st[:, :], ROUND, ROUND + 128.0, ALU.add, ALU.subtract).then_inc(*ev("q2", b))
                    dve.wait_ge(*on("p_cs", b))
                    dve.tensor_scalar(corr(b), place[("cs", b)][:, :], sc[:, 9:10], sc[:, 10:11], ALU.mult, ALU.add).then_inc(*ev("corr", b))
                elif what == "quant":
                    b, = k
                    for i in range(NI):
                        dve.wait_ge(*on("p_y", "quant", b, i))
                        x = X[:, 2 * b + i, :]
                        dve.tensor_scalar(H[:, i, :], place[("y", "quant", b, i)][:, :], small[:, 2 * b + i:2 * b + i + 1], sc[:, 8:9],
                                          ALU.add, ALU.mult).then_inc(*ev("x1t", b, i))
                        dve.wait_ge(*on("x1t", b, i))
                        link(dve.tensor_tensor(out=H[:, i, :], in0=H[:, i, :], in1=corr(b), op=ALU.add))
                        dve.tensor_tensor(out=x, in0=H[:, i, :], in1=x, op=ALU.add).then_inc(*ev("x", "quant", b, i))
                    dve.wait_ge(*on("x", "quant", b, NI - 1))
                elif what == "ffn0":
                    b, = k
                    n = E0 * R0 + E0
                    dve.wait_ge(*on("p_g0", b))
                    tv = place[("g0", b)][:, 0:2 * n].rearrange("p (i n) -> p i n", i=NI)
                    logits = tv[:, :, E0 * R0:n]
                    link(dve.tensor_reduce(small[:, 8:10], logits, AX, ALU.max))
                    dve.tensor_tensor(out=rt[:, :, 0, :], in0=logits, in1=small[:, 8:10].unsqueeze(2).broadcast_to([P, NI, E0]),
                                      op=ALU.subtract).then_inc(*ev("lmm", b))
                    dve.wait_ge(*on("lexp", b))
                    for i in range(NI):
                        ex = rt[:, i, 1, :]
                        other = ex.unsqueeze(1).broadcast_to([P, E0, E0])
                        own = ex.unsqueeze(2).broadcast_to([P, E0, E0])
                        gt = rc[:, i, 0, :].rearrange("p (e j) -> p e j", e=E0)
                        eq = rc[:, i, 1, :].rearrange("p (e j) -> p e j", e=E0)
                        dve.tensor_tensor(out=gt, in0=other, in1=own, op=ALU.is_gt)
                        link(dve.tensor_tensor(out=eq, in0=other, in1=own, op=ALU.is_equal))
                        dve.wait_ge(*on("consts"))
                        link(dve.tensor_tensor(out=eq, in0=eq, in1=tri[:, :, :], op=ALU.mult))
                        link(dve.tensor_tensor(out=gt, in0=gt, in1=eq, op=ALU.add))
                        link(dve.tensor_reduce(rt[:, i, 2, :], gt, AX, ALU.add))
                        link(dve.tensor_scalar(rt[:, i, 2, :], rt[:, i, 2, :], 2.0, None, ALU.is_lt))
                        link(dve.tensor_tensor(out=rt[:, i, 3, :], in0=rt[:, i, 2, :], in1=ex, op=ALU.mult))
                        link(dve.tensor_reduce(small[:, 10 + i:11 + i], rt[:, i, 3, :], AX, ALU.add))
                        link(dve.reciprocal(small[:, 12 + i:13 + i], small[:, 10 + i:11 + i]))
                        link(dve.tensor_scalar(rt[:, i, 3, :], rt[:, i, 3, :], small[:, 12 + i:13 + i], 2.0, ALU.mult, ALU.mult))
                        dve.tensor_tensor(out=ON[:, i * D:i * D + P].rearrange("p (e r) -> p e r", e=E0),
                                          in0=tv[:, i, 0:E0 * R0].rearrange("p (e r) -> p e r", e=E0),
                                          in1=rt[:, i, 3, :].unsqueeze(2).broadcast_to([P, E0, R0]), op=ALU.mult).then_inc(*ev("hw", b, i))
                    dve.wait_ge(*on("hwt_high", b))
                    low(sgh[:, 1, :], place[("hwt", b)][:, 0:T], sgh[:, 0, :], ("hwt_low", b))
                    for i in range(NI):
                        x = X[:, 2 * b + i, :]
                        dve.wait_ge(*on("p_y", "ffn0", b, i))
                        dve.tensor_tensor(out=x, in0=place[("y", "ffn0", b, i)][:, :], in1=x, op=ALU.add).then_inc(*ev("x", "ffn0", b, i))
                        dve.wait_ge(*on("x", "ffn0", b, i))
                        if b == 0 and i == 0:
                            dve.wait_ge(*on("d_bias0"))
                        link(dve.tensor_tensor(out=x, in0=x, in1=bias0, op=ALU.add))
                elif what == "qkv1":
                    b, = k
                    if b == 0:
                        dve.wait_ge(*on("x", "ffn0", 1, 1))
                        dve.memset(VP[:, :, HD:HD + 1], 1.0).then_inc(*ev("vp_ones"))
                        dve.wait_ge(*on("d_biases"))
                        dve.wait_ge(*on("p_hT", 3, 0, 1))
                    else:
                        dve.wait_ge(*on("d_w1_0", 2))
                    for n in range(3):
                        for mp in range(2):
                            dve.wait_ge(*on("p_q1", b, n, mp))
                            dve.tensor_tensor(out=proj1[n][:, 2 * mp:2 * mp + 2, :], in0=place[("q1", b, n, mp)][:, :].rearrange("p (m t) -> p m t", m=2),
                                              in1=biases[:, n, 2 * mp:2 * mp + 2].unsqueeze(2).broadcast_to([P, 2, T]), op=ALU.add
                                              ).then_inc(*ev("qkv1", b, n, mp))
                elif what == "smax1":
                    for g4 in range(NG // 4):
                        maxima1(dve, k[0], g4)
                elif what == "att1":
                    u, other = k
                    dve.wait_ge(*on("m1", u, 7))

                    def diag(g4):
                        if g4 >= 2:
                            dve.wait_ge(*on("p_t1", u, g4 - 2))
                        elif u:
                            dve.wait_ge(*on("p_t1", u - 1, 6 + g4))
                        m = mx1[:, (u % 2) * 32 + 4 * g4:(u % 2) * 32 + 4 * g4 + 4]
                        dve.tensor_tensor(out=DIAG[:, g4 % 2, :].rearrange("p (g k) -> p g k", g=4), in0=negid[:, :].unsqueeze(1).broadcast_to([P, 4, P]),
                                          in1=m.unsqueeze(2).broadcast_to([P, 4, P]), op=ALU.mult).then_inc(*ev("diag", u, g4))
                    diag(0)
                    diag(1)
                    for g4 in range(NG // 4):
                        if g4 + 2 < NG // 4:
                            diag(g4 + 2)
                        if other is not None:
                            maxima1(dve, other, g4)
                elif what == "out1":
                    u, = k
                    x = X[:, u, :]
                    dve.wait_ge(*on("p_den1", u))
                    dve.reciprocal(rden[:, :], place[("den1", u)][:, 0:NH]).then_inc(*ev("rden1", u))
                    dve.wait_ge(*on("rden1", u))
                    dve.wait_ge(*on("p_y", "out1", u))
                    t = H[:, 0, :]
                    dve.tensor_tensor(out=t.rearrange("p (h d) -> p h d", h=NH), in0=place[("y", "out1", u)][:, :].rearrange("p (h d) -> p h d", h=NH),
                                      in1=rden[:, :].unsqueeze(2).broadcast_to([P, NH, HD]), op=ALU.mult).then_inc(*ev("x1o", u))
                    dve.wait_ge(*on("x1o", u))
                    link(dve.tensor_tensor(out=x, in0=t, in1=x, op=ALU.add))
                    if u == 3:
                        dve.memset(vx(0)[:, :, :, XD:XD + 1], 1.0)
                        dve.memset(vx(1)[:, :, :, XD:XD + 1], 1.0).then_inc(*ev("vx_ones"))
                elif what in ("kvctx", "kvlat"):
                    b, = k
                    s0, n = (0, CTX) if what == "kvctx" else (CTX, T)
                    for kv in range(KV):
                        dve.wait_ge(*on("kx_high", what, b, kv))
                        low(kx(b, 1)[0:XD, kv, s0:s0 + n], place[(what, b, kv)][0:XD, 0:n], kx(b, 0)[0:XD, kv, s0:s0 + n], ("kx_low", what, b, kv))
                elif what == "q4":
                    kv, b = k
                    n = 2 * kv + b
                    for j in range(2):
                        dve.wait_ge(*on("q4_high", kv, b, j))
                        low(qx(n, 1)[0:XD, 2 * j:2 * j + 2, :], place[("q4", kv, b, j)][0:XD, :].rearrange("p (h t) -> p h t", h=2),
                            qx(n, 0)[0:XD, 2 * j:2 * j + 2, :], ("q4_low", kv, b, j))
                elif what == "smax4":
                    maxima4(dve, *k)
                elif what == "att4":
                    kv, b, *other = k
                    if other[0] is not None:
                        maxima4(dve, *other)
                    for i in range(NI):
                        dve.wait_ge(*on("p_o4", kv, b, GQ - 1))
                        tv = place[("o4", kv, b, i)][:, 0:GQ * (XD + 1)].rearrange("p (h d) -> p h d", h=GQ)
                        if kv or b or i:
                            dve.wait_ge(*so_far("on4"))
                        link(dve.reciprocal(rden[:, 4 * i:4 * i + 4], tv[:, :, XD]))
                        if kv or b:
                            dve.wait_ge(*on("p_ot4", *UNITS4[2 * kv + b - 1], i))
                        dve.tensor_tensor(out=ON[:, i * 384:(i + 1) * 384].rearrange("p (h d) -> p h d", h=GQ), in0=tv[:, :, 0:XD],
                                          in1=rden[:, 4 * i:4 * i + 4].unsqueeze(2).broadcast_to([P, GQ, XD]), op=ALU.mult).then_inc(*ev("on4", kv, b, i))
                elif what == "turn4":
                    kv, b = k
                    for i in range(NI):
                        dve.wait_ge(*on("ot4_high", kv, b, i))
                        low(sg3[:, 1, :, i * P:(i + 1) * P], place[("ot4", kv, b, i)][:, 0:384].rearrange("p (c t) -> p c t", c=3),
                            sg3[:, 0, :, i * P:(i + 1) * P], ("ot4_low", kv, b, i))
                elif what == "out4":
                    kv, b = k
                    for i in range(NI):
                        dve.wait_ge(*on("p_y", "out4", kv, b, i))
                        x = X[:, 2 * b + i, :]
                        dve.tensor_tensor(out=x, in0=place[("y", "out4", kv, b, i)][:, :], in1=x, op=ALU.add).then_inc(*ev("x", "out4", kv, b, i))
                    dve.wait_ge(*on("x", "out4", kv, b, NI - 1))
                elif what == "ffn1a":
                    b, = k
                    dve.wait_ge(*on("p_cq", b))
                    dve.tensor_copy(small[:, 36:37], place[("cq", b)][:, 0:1]).then_inc(*ev("cq", b))
                    dve.wait_ge(*on("p_cs1", b))
                    link(dve.tensor_reduce(small[0:1, 40:41], place[("cs1", b)][0:1, 0:E1], AX, ALU.max))
                    dve.tensor_scalar(small[0:1, 41:42], small[0:1, 40:41], -1.0 / math.sqrt(128.0), None, ALU.mult).then_inc(*ev("cmax", b))
                    dve.wait_ge(*on("cexp", b))
                    link(dve.tensor_reduce(small[0:1, 42:43], small[0:1, 48:56], AX, ALU.add))
                    link(dve.reciprocal(small[0:1, 43:44], small[0:1, 42:43]))
                    link(dve.tensor_scalar(small[0:1, 56:64], small[0:1, 48:56], small[0:1, 43:44], None, ALU.mult))
                    dve.tensor_copy(expand[0:1, :].rearrange("p (e r) -> p e r", e=E1), small[0:1, 56:64].unsqueeze(2).broadcast_to([1, E1, R1])).then_inc(*ev("coef", b))
                    dve.wait_ge(*on("p_cc", b))
                    dve.tensor_copy(small[:, 44:48], place[("cc", b)][:, 0:4]).then_inc(*ev("cc", b))
                    dve.wait_ge(*on("cc", b))
                    for m in range(C):
                        dve.wait_ge(*on("dn_high", b, m | 1))
                        ins = dve.scalar_tensor_tensor(out=sg4[:, 1, m, :], in0=place[("dn", b, m // 2)][:, m % 2 * T:(m % 2 + 1) * T],
                                                       scalar=small[:, 44 + m:45 + m], in1=plain(sg4[:, 0, m, :]), op0=ALU.mult, op1=ALU.subtract)
                        if m % 2:
                            ins.then_inc(*ev("dn_low", b, m // 2))
                elif what == "ffn1b":
                    b, = k
                    for i in range(NI):
                        dve.wait_ge(*on("p_y", "ffn1", b, i))
                        x = X[:, 2 * b + i, :]
                        dve.tensor_tensor(out=x, in0=place[("y", "ffn1", b, i)][:, :], in1=x, op=ALU.add).then_inc(*ev("x", "ffn1", b, i))
            dve.nop().then_inc(*ev("finished"))

        @block.gpsimd
        def _(pool):
            def load(n):
                if n >= len(ITEMS):
                    return
                name, r, c, _ = ITEMS[n]
                if n >= 2:
                    before, _, _, slot = ITEMS[n - 2]
                    pool.wait_ge(*(on("q2", int(before[-1])) if slot is None else on("split", before)))
                pool.dma_start(STAGE[n % 2][:, 0:r * c].rearrange("p (r c) -> p r c", r=r),
                               dram[name].rearrange("(r p) c -> p r c", p=P)).then_inc(*ev(f"d_stage{n % 2}", name, by=16))

            load(0)
            load(1)
            pool.memset(ident[:, :], 0.0).then_inc(*ev("zeros"))
            pool.wait_ge(*on("zeros"))
            pool.affine_select(out=ident[:, :], in_=ident[:, :], compare_op=ALU.not_equal, fill=1.0, base=0, pattern=[[-1, P]],
                               channel_multiplier=1).then_inc(*ev("ident"))
            pool.memset(minushalf[:, :], -0.5).then_inc(*ev("minushalf"))
            pool.wait_ge(*on("minushalf"))
            loaded = 2
            for step in schedule:
                what, *k = step
                if what == "consts":
                    pool.memset(negid[:, :], 0.0)
                    pool.memset(identb[:, :], 0.0)
                    pool.memset(mask_s[:, :], 0.0)
                    pool.memset(mask_t[:, :], 0.0)
                    pool.memset(rows_a[:, :], 0.0)
                    pool.memset(rows_b[:, :], -BIG)
                    pool.memset(tri[:, :, :], 1.0).then_inc(*ev("flat"))
                    pool.wait_ge(*on("flat"))
                    for m, fill in ((negid, -1.0), (identb, 1.0)):
                        pool.affine_select(out=m[:, :], in_=m[:, :], compare_op=ALU.not_equal, fill=fill, base=0, pattern=[[-1, P]], channel_multiplier=1)
                    pool.affine_select(out=mask_s[:, :], in_=mask_s[:, :], compare_op=ALU.is_ge, fill=-BIG, base=0, pattern=[[-1, P]], channel_multiplier=1)
                    pool.affine_select(out=mask_t[:, :], in_=mask_t[:, :], compare_op=ALU.is_ge, fill=-BIG, base=0, pattern=[[1, P]], channel_multiplier=-1)
                    for m, fill in ((rows_a, 1.0), (rows_b, 0.0)):
                        v = m[:, :].rearrange("p (j g) -> p j g", j=4)
                        pool.affine_select(out=v, in_=v, compare_op=ALU.not_equal, fill=fill, base=0, pattern=[[1, 4], [0, 32]], channel_multiplier=-1)
                    pool.affine_select(out=tri[:, :, :], in_=tri[:, :, :], compare_op=ALU.is_gt, fill=0.0, base=0,
                                       pattern=[[1, E0], [-1, E0]], channel_multiplier=0).then_inc(*ev("consts"))
                elif what == "w":
                    name, = k
                    n = ITEM[name]
                    _, r, c, slot = ITEMS[n]
                    while loaded <= n:
                        load(loaded)
                        loaded += 1
                    before = [m for m in range(n) if ITEMS[m][3] == slot]
                    if before:
                        pool.wait_ge(*on(*last_use[ITEMS[before[-1]][0]]))
                    st = STAGE[n % 2][:, 0:r * c]
                    pool.wait_ge(*on("split_high", name))
                    pool.tensor_tensor(out=WL[slot][:, 0:r * c], in0=st, in1=plain(WH[slot][:, 0:r * c]), op=ALU.subtract).then_inc(*ev("split", name))
                    while loaded <= min(n + 2, len(ITEMS) - 1):
                        load(loaded)
                        loaded += 1
                elif what == "ctxq" and k[0] == 1:
                    pool.wait_ge(*so_far("rstd"))
                    pool.wait_ge(*on("consts"))
                    for b in range(B):
                        pool.memset(plain(kx(b, 0)[XD:XD + 1, :, :]), 1.0).then_inc(*ev("kx_ones"))
                        pool.wait_ge(*so_far("kx_ones"))
                elif what == "ln":
                    s, b = k
                    pool.wait_ge(*on("var", s, b))
                    pool.tensor_tensor(out=rstd[:, :], in0=var[:, :], in1=minushalf[:, :], op=ALU.pow).then_inc(*ev("rstd", s, b))

        @block.sync
        def _(sp):
            sp.dma_start(X[:, 0:2, :], dram["x"][0:T, :].rearrange("(i p) d -> p i d", p=P)).then_inc(*ev("d_x0", by=16))
            sp.dma_start(sc[:, 0:4], dram["scales"].partition_broadcast(P)).then_inc(*ev("d_sc", by=16))
            sp.dma_start(X[:, 2:4, :], dram["x"][T:2 * T, :].rearrange("(i p) d -> p i d", p=P)).then_inc(*ev("d_x1", by=16))
            sp.dma_start(biases[:, :, :], dram["biases1"]).then_inc(*ev("d_biases", by=16))
            sp.dma_start(bias0, dram["bias0"].partition_broadcast(P)).then_inc(*ev("d_bias0", by=16))
            sp.dma_start(keys_t[:, :], dram["keys"]).then_inc(*ev("d_mix", by=16))
            sp.dma_start(wqx[:, :, :], dram["wqx"].rearrange("(c p) k -> p c k", p=P)).then_inc(*ev("d_mix", by=16))
            for step in schedule:
                what, *k = step
                if what == "qkv0":
                    b, = k
                    sp.wait_ge(*on("q0_high", b, 1))
                    sp.wait_ge(*on("q0_low", b, 1))
                    sp.dma_start(scratch0[b].rearrange("s (m p) t -> p s m t", p=P), plain(SG[:, :]).rearrange("p (s m t) -> p s m t", s=2, m=C)
                                 ).then_inc(*ev(f"d_w0_{b}", by=16))
                    sp.wait_ge(*on("k0_low", b))
                    sp.dma_start(plain(KS0[HD:2 * HD, b, :]), plain(KS0[0:HD, b, :])).then_inc(*ev(f"d_k0_{b}", by=16))
                    sp.dma_start(plain(KS0[2 * HD:3 * HD, b, :]), plain(KL0[:, b, :])).then_inc(*ev(f"d_k0_{b}", by=16))
                    sp.wait_ge(*on(f"d_w0_{b}"))
                    for row, half in enumerate((0, 1, 0)):
                        sp.dma_start(plain(qs0(b)[row * HD:(row + 1) * HD, :, :]), scratch0[b, half].rearrange("(h d) t -> d h t", d=HD)
                                     ).then_inc(*ev(f"d_q0_{b}", by=16))
                elif what == "mrow0":
                    b, = k
                    sp.wait_ge(*on("mrow0", b))
                    sp.dma_start(plain(qs0(b)[48:49, :, :]), plain(MT[:, :])).then_inc(*ev(f"d_m0_{b}", by=16))
                elif what == "att0":
                    b, _, g0, g1 = k
                    for g in list(range(max(g0 - 1, 0), g1 - 1)) + [g1 - 1] * (g1 == NH // 4):
                        sp.wait_ge(*on("on0", b, g, 1))
                        for n in range(2):
                            sp.dma_start(scratch3[b, n, g * 4 * HD:(g + 1) * 4 * HD, :].rearrange("(h d) t -> d h t", d=HD),
                                         sent0(g)[n * HD:(n + 1) * HD, :, :]).then_inc(*ev(f"d_on{g % 2}", b, g, by=16))
                        if g % 2:
                            c = g // 2
                            sp.wait_ge(*on("d_on0", b, g - 1))
                            sp.wait_ge(*on("d_on1", b, g))
                            sp.wait_ge(*on("d_w0_1"))
                            if b:
                                sp.wait_ge(*on("ot0_low", 0, c))
                            sp.dma_start(plain(SG[:, :]).rearrange("p (n c t) -> p n c t", n=2, c=C)[:, :, c, :],
                                         scratch3[b, :, c * P:(c + 1) * P, :].rearrange("n p t -> p n t")).then_inc(*ev(f"d_ot0_{c}", b, by=16))
                elif what == "qkv1":
                    b, = k
                    for n in range(3):
                        sp.wait_ge(*on("qkv1", b, n, 1))
                        sp.dma_start(scratch1[b, n].rearrange("(m p) t -> p m t", p=P), proj1[n]).then_inc(*ev(f"d_w1_{b}", n, by=16))
                elif what == "load1":
                    u, = k
                    b, i = divmod(u, NI)
                    name = f"d_l1_{u % 2}"
                    sp.wait_ge(*on(f"d_w1_{b}", 2))
                    if u < 2:
                        sp.wait_ge(*on("p_t0", 1, 7, 2))
                        sp.wait_ge(*on("consts"))
                        sp.dma_start(plain(st1(u, 0)[HD:HD + 4, :, :]), rows_b[:, :].unsqueeze(1).broadcast_to([4, NH, P])).then_inc(*ev(name, u, by=16))
                        sp.dma_start(plain(st1(u, 1)[HD:HD + 4, :, :]), rows_a[:, :].unsqueeze(1).broadcast_to([4, NH, P])).then_inc(*ev(name, u, by=16))
                    else:
                        sp.wait_ge(*on("p_t1", u - 2, 7))
                    for n, to in enumerate((st1(u, 0)[0:HD], st1(u, 1)[0:HD], st1(u, 0)[64:64 + HD])):
                        sp.dma_start(plain(to), scratch1[b, n, :, i * P:(i + 1) * P].rearrange("(h d) t -> d h t", d=HD)).then_inc(*ev(name, u, by=16))
                elif what == "att1":
                    u, other = k
                    sp.wait_ge(*on("ots", u, 7))
                    if u == 0:
                        sp.wait_ge(*on("d_w1_1", 2))
                    else:
                        sp.wait_ge(*on("p_y", "out1", u - 1))
                    sp.dma_start(scratch2[u, 0:D, :].rearrange("(h d) t -> d h t", d=HD), OTS[0:HD, :, :]).then_inc(*ev("d_w2", u, by=16))
                    sp.dma_start(ON[0:NH, 512:512 + P], OTS[HD:HD + 1, :, :]).then_inc(*ev("d_o1", u, by=16))
                    sp.wait_ge(*on("d_w2", u))
                    sp.dma_start(ON[:, 0:512].rearrange("p (m t) -> p m t", m=C), scratch2[u, 0:D, :].rearrange("(m p) t -> p m t", p=P)
                                 ).then_inc(*ev("d_o1", u, by=16))
                    sp.wait_ge(*on("d_o1", u))
                elif what == "mrow4":
                    kv, b = k
                    sp.wait_ge(*on("mrow4", kv, b))
                    for i in range(NI):
                        sp.dma_start(plain(qx(2 * kv + b, 0)[XD:XD + 1, :, i * P:(i + 1) * P]), plain(MT[i * 4:(i + 1) * 4, 0:P])
                                     ).then_inc(*ev("d_m4", kv, b, by=16))
                    sp.wait_ge(*on("d_m4", kv, b))
                elif what == "ffn1b":
                    b, = k
                    for i in range(NI):
                        sp.wait_ge(*on("x", "ffn1", b, i))
                        sp.dma_start(out[b * T + i * P:b * T + (i + 1) * P, :], X[:, 2 * b + i, :]).then_inc(*ev("d_out", by=16))
            if schedule[-1][0] != "ffn1b":
                sp.wait_ge(*on("finished"))
                sp.dma_start(out.rearrange("(i p) d -> p i d", p=P), X[:, :, :]).then_inc(*ev("d_out", by=16))
            sp.wait_ge(*on("d_out"))
    return found


def kernel(**inputs):
    import numpy as np
    import concourse.bacc as bacc
    from concourse.bass_utils import run_bass_kernel_spmd as run

    a = {k: np.asarray(v) for k, v in inputs.items()}
    t = {
        "x": a["x"].reshape(B * T, D), "wq0": a["L0_attn_wq"], "wo0": a["L0_attn_wo"],
        "wkv0": np.concatenate([a["L0_attn_wk"], a["L0_attn_wv"]], axis=1),
        "ctxn0": a["ctx_4096"][0], "ctxn1": a["ctx_4096"][1], "ctxt0": a["ctx_4096"][0].T, "ctxt1": a["ctx_4096"][1].T,
        "scales": np.concatenate([a[f"L0_xattn_{n}"] for n in ("x1_scale", "x1_zp", "x2_scale", "x2_zp")]),
        "wbase": a["L0_ffn_W_base"].T, "bias0": a["L0_ffn_b_base"],
        "wexp": np.concatenate([a["L0_ffn_A"].reshape(E0 * R0, D).T, a["L0_ffn_W_router"].T], axis=1),
        "wexpb": a["L0_ffn_B"].transpose(0, 2, 1).reshape(E0 * R0, D),
        "wq1": a["L1_attn_wq"].T, "wk1": a["L1_attn_wk"].T, "wv1": a["L1_attn_wv"].T,
        "biases1": np.stack([a[f"L1_attn_b{n}"].reshape(C, P).T for n in "qkv"], axis=1),
        "wxk": a["L1_xattn_Wk"].T, "wxv": a["L1_xattn_Wv"].T,
        "worg": a["L1_ffn_W_org"].T, "wdown": a["L1_ffn_lora_down"].transpose(1, 0, 2).reshape(D, E1 * R1),
        "wup": a["L1_ffn_lora_up"].reshape(E1 * R1, D), "keys": a["L1_ffn_lora_keys"].T, "wqx": a["L1_ffn_Wq"].T,
    }
    for kv in range(KV):
        t[f"wxq{kv}"] = a["L1_xattn_Wq"].T[:, kv * GQ * XD:(kv + 1) * GQ * XD]
        t[f"wxo{kv}"] = a["L1_xattn_Wo"].T[kv * GQ * XD:(kv + 1) * GQ * XD, :]
    arrays = {f"in_{k}": np.ascontiguousarray(v) for k, v in t.items()}

    def build(counts):
        nc = bacc.Bacc("TRN2", target_bir_lowering=False, num_devices=1, dynamic_dma_scratch_size=8192)
        dram = {k: nc.dram_tensor(f"in_{k}", arrays[f"in_{k}"].shape, mybir.dt.from_np(arrays[f"in_{k}"].dtype), kind="ExternalInput").ap() for k in t}
        out = nc.dram_tensor("out_0", (B * T, D), F32, kind="ExternalOutput").ap()
        return nc, program(nc, dram, out, counts, SCHEDULE)

    _, counts = build({})
    nc, _ = build(counts)
    got = run(nc, [arrays], core_ids=[0]).results[0]["out_0"]
    return got.reshape(B, T, D)
```

```python
from contextlib import ExitStack
import math

import concourse.bass as bass
from concourse import mybir

F32 = mybir.dt.float32
F32R = mybir.dt.float32r
BF16 = mybir.dt.bfloat16
ALU = mybir.AluOpType
ACT = mybir.ActivationFunctionType
AX = mybir.AxisListType.X

D = 512
B = 2
T = 256
P = 128
NI = T // P
C = D // P
NH, HD = 32, 16
NG = P // 4
KV, GQ, XD = 4, 4, 96
CTX = 512
SX = CTX + T
E0, R0 = 8, 16
E1, R1 = 8, 64
EPS = 1e-5
BIG = 2.0 ** 100
ROUND = 12582912.0
PAIRS1 = [(0, 0), (0, 1), (0, 2), (1, 0), (1, 1), (2, 0)]
ROWS1 = 4 + 16 * len(PAIRS1)
SX_SCALE = 1.0 / math.sqrt(XD)

ITEMS = [("wq0", 4, 512, 0), ("wkv0", 4, 32, 1), ("ctxn0", 4, 512, None), ("ctxn1", 4, 512, None), ("wo0", 4, 512, 2),
         ("wbase", 4, 512, 0), ("wexp", 4, E0 * R0 + E0, 1), ("wexpb", 1, 512, 2),
         ("wq1", 4, 512, 1), ("wk1", 4, 512, 0), ("wv1", 4, 512, 2),
         ("wxk", 4, 384, 0), ("wxv", 4, 384, 1), ("ctxt0", 4, 512, 2), ("ctxt1", 4, 512, 2)]
ITEMS += [(f"{n}{kv}", r, c, (2 + 2 * kv + j) % 3) for kv in range(KV) for j, (n, r, c) in enumerate([("wxq", 4, 384), ("wxo", 3, 512)])]
ITEMS += [("wdown", 4, 512, 1), ("worg", 4, 512, 2), ("wup", 4, 512, 0)]
LOW_ON_VECTOR = ("wq0", "wk1")
ITEM = {name: k for k, (name, _, _, _) in enumerate(ITEMS)}

SCHEDULE = [("norm", 0, 0), ("turn", 0, 0), ("w", "wq0"), ("norm", 0, 1), ("w", "wkv0"), ("consts",), ("qkv0", 0), ("turn", 0, 1), ("qkv0", 1),
            ("ctxq", 0), ("w", "wo0"), ("smax0", 0), ("mrow0", 0),
            ("att0", 0, 1, 0, 8), ("mrow0", 1), ("att0", 0, 1, 8, 9), ("ctxq", 1), ("att0", 1, None, 0, 2), ("last0", 0), ("att0", 1, None, 2, 4), ("out0", 0), ("norm", 1, 0), ("att0", 1, None, 4, 5), ("turn", 1, 0),
            ("quant", 0), ("norm", 2, 0), ("att0", 1, None, 5, 7), ("turn", 2, 0), ("w", "wbase"), ("att0", 1, None, 7, 9),
            ("w", "wexp"), ("last0", 1), ("ffn0a", 0), ("out0", 1), ("w", "wexpb"), ("ffn0b", 0), ("norm", 1, 1), ("turn", 1, 1), ("quant", 1),
            ("norm", 2, 1), ("turn", 2, 1), ("norm", 3, 0), ("ffn0a", 1), ("w", "wq1"), ("turn", 3, 0), ("ffn0b", 1), ("norm", 3, 1),
            ("w", "wk1"), ("w", "wv1"), ("qkv1", 0), ("load1", 0), ("loadv", 0), ("load1", 1), ("turn", 3, 1), ("qkv1", 1),
            ("load1", 2), ("smax1", 0), ("loadv", 1), ("att1", 0, 1), ("w", "wxk"), ("load1", 3), ("loadv", 2),
            ("att1", 1, 2), ("w", "wxv"), ("loadv", 3), ("out1", 0), ("att1", 2, 3), ("w", "ctxt0"), ("out1", 1), ("att1", 3, None), ("out1", 2), ("norm", 4, 0),
            ("kvctx", 0), ("turn", 4, 0), ("out1", 3), ("w", "ctxt1"), ("norm", 4, 1), ("kvlat", 0), ("kvctx", 1), ("w", "wxq0"), ("turn", 4, 1), ("kvlat", 1)]
UNITS4 = [(kv, b) for kv in range(KV) for b in range(B)]
SCHEDULE += [("w", "wxo0")]
for n in range(len(UNITS4) + 2):
    new, now, old = [UNITS4[m] if 0 <= m < len(UNITS4) else None for m in (n, n - 1, n - 2)]
    if new:
        SCHEDULE += [("q4", *new, 0)]
    if old:
        SCHEDULE += [("turn4", *old)]
    if n == len(UNITS4) + 1:
        SCHEDULE += [("turn", 5, 0)]
    if new:
        SCHEDULE += [("q4", *new, 1)]
    if old:
        SCHEDULE += [("out4", *old)]
    if n == len(UNITS4):
        SCHEDULE += [("norm", 5, 0)]
    if n == 0:
        SCHEDULE += [("smax4", *new)]
    if now:
        SCHEDULE += [("att4", *now, new, 0, 2)]
        if n % 2:
            SCHEDULE += [("w", f"wxq{n // 2 + 1}"), ("w", f"wxo{n // 2 + 1}")] if n // 2 + 1 < KV else [("w", "wdown")]
        if n == len(UNITS4):
            SCHEDULE += [("w", "worg")]
        SCHEDULE += [("att4", *now, new, 2, 4)]
    if new:
        SCHEDULE += [("mrow4", *new)]
SCHEDULE += [("w", "wup"), ("ffn1a", 0), ("norm", 5, 1), ("ffn1b", 0), ("turn", 5, 1), ("ffn1a", 1), ("ffn1b", 1)]


def program(nc, dram, out, counts, schedule):
    found, total, sems = {}, {}, {}
    ctx = ExitStack()

    def semaphore(kind):
        if kind not in sems:
            sems[kind] = ctx.enter_context(nc.semaphore(kind))
        return sems[kind]

    def ev(kind, *key, by=1):
        total[kind] = total.get(kind, 0) + by
        found[(kind, *key)] = total[kind]
        return semaphore(kind), by

    def on(kind, *key):
        return semaphore(kind), counts.get((kind, *key), 1)

    def so_far(kind):
        return semaphore(kind), total[kind]

    place, banks_of = {}, {}

    def bank(pe, ring, key, *drains):
        n = banks_of.get(id(ring), 0)
        banks_of[id(ring)] = n + 1
        tile, readers = ring[n % len(ring)]
        for reader in readers:
            pe.wait_ge(*on(*reader))
        readers[:] = drains
        place[key] = tile
        return tile

    with ctx:
        def sb(name, shape, dt=F32):
            return ctx.enter_context(nc.sbuf_tensor(name, shape, dt))

        X = sb("X", [P, B * NI, D])
        H = sb("H", [P, NI, D])
        HH = sb("HH", [P, B, C, T], F32R)
        HL = sb("HL", [P, B, C, T], F32R)
        STK = sb("STK", [P, 16384], F32R)
        STAGE = [sb(f"stage{n}", [P, 2048]) for n in range(2)]
        WH = [sb(f"WH{n}", [P, 2048], F32R) for n in range(3)]
        WL = [sb(f"WL{n}", [P, 2048], F32R) for n in range(3)]
        PT = [sb(f"PT{n}", [P, 1536]) for n in range(2)]
        VX = sb("VX", [P, 5184])
        SG = sb("SG", [P, 2048], F32R)
        ON = sb("ON", [P, 1024])
        KS0 = sb("KS0", [P, B, T], F32R)
        KL0 = sb("KL0", [HD, B, T], F32R)
        V0 = sb("V0", [P, B, NI, 2 * HD])
        MT = sb("MT", [NH, T], F32R)
        MX = sb("MX", [P, B, NI, NH])
        DIAG = sb("DIAG", [P, 2, 512], BF16)
        ident = sb("ident", [P, P])
        negid = sb("negid", [P, P])
        identb = sb("identb", [P, P], BF16)
        onesb = sb("onesb", [P, P], BF16)
        mask_s = sb("mask_s", [P, P], BF16)
        mask_t = sb("mask_t", [P, P], BF16)
        rows_a = sb("rows_a", [4, P], BF16)
        rows_b = sb("rows_b", [4, P], BF16)
        tri = sb("tri", [P, E0, E0])
        stats = sb("stats", [P, NI, 6])
        mv = sb("mv", [P, NI, 2])
        var = sb("var", [P, NI])
        rstd = sb("rstd", [P, NI])
        minushalf = sb("minushalf", [P, NI])
        sc = sb("sc", [P, 16])
        biases = sb("biases", [P, 3, C])
        rden = sb("rden", [P, NH])
        rt = sb("rt", [P, NI, 4, E0])
        rc = sb("rc", [P, NI, 2, E0 * E0])
        small = sb("small", [P, 64])
        keys_t = sb("keys_t", [P, E1])
        wqx = sb("wqx", [P, C, P])

        ringA = [(ctx.enter_context(nc.psum_tensor(f"psA{n}", [P, 512], F32)), []) for n in range(5)]
        ringB = [(ctx.enter_context(nc.psum_tensor(f"psB{n}", [P, 512], F32)), []) for n in range(3)]

        def q2n(b):
            return VX[:, b * 1024:(b + 1) * 1024].bitcast(BF16).rearrange("p (c n) -> p c n", c=C)

        def corr(b):
            return VX[:, 2048 + b * 512:2560 + b * 512]

        bias0 = VX[:, 3072:3584]
        def q1t(b):
            return VX[:, 3584 + b * 512:4096 + b * 512].bitcast(BF16).rearrange("p (c t) -> p c t", c=C)

        q1n = VX[:, 4608:5120].bitcast(BF16).rearrange("p (i n) -> p i n", i=NI)
        VP = VX[:, 0:NG * 17].rearrange("p (g d) -> p g d", d=17)
        OTS = VX[:, 1088:1088 + 4096].rearrange("p (h t) -> p h t", t=P)
        def vx(b):
            return VX[:, b * 2328:(b + 1) * 2328].rearrange("p (s k d) -> p s k d", s=6, k=KV)

        def qs0(b):
            return STK[:, b * 8192:(b + 1) * 8192].rearrange("p (h t) -> p h t", h=NH)

        def st1(u, what):
            o = (u % 3) * 8192 + what * 4096
            return STK[:, :].bitcast(BF16)[:, o:o + 4096].rearrange("p (h t) -> p h t", h=NH)

        def group(u, what, rows, g):
            o = (u % 3) * 8192 + what * 4096 + g
            return STK[:, :].bitcast(BF16)[rows, o:o + 32 * 127 + 1:32]

        v1 = STK[0:HD, 12288:16384].bitcast(F32)

        def kx(b, half):
            o = b * 6144 + half * 3072
            return STK[:, o:o + 3072].rearrange("p (k s) -> p k s", k=KV)

        def qx(n, half):
            o = 12288 + (n % 2) * 2048 + half * 1024
            return STK[:, o:o + 1024].rearrange("p (h t) -> p h t", h=GQ)

        sg4 = SG[:, :].rearrange("p (s m t) -> p s m t", s=2, m=C)
        sg3 = SG[:, 0:1536].rearrange("p (s c t) -> p s c t", s=2, c=3)
        sgh = SG[:, 0:512].rearrange("p (s t) -> p s t", s=2)

        expand = ON[0:1, 0:D]

        def sent0(g):
            return ON[g % 2 * 32:g % 2 * 32 + 2 * HD, :].rearrange("p (h t) -> p h t", h=4)

        def item(name):
            _, r, c, slot = ITEMS[ITEM[name]]
            return tuple(w[slot][:, 0:r * c].rearrange("p (r c) -> p r c", r=r) for w in (WH, WL))

        def plain(ap):
            return ap.bitcast(F32)

        last_use = {"wq0": ("p_v0", 1), "wkv0": ("p_v0", 1), "wo0": ("p_y", "out0", 1, 1), "wbase": ("p_y", "ffn0", 1, 1),
                    "wexp": ("p_g0", 1), "wexpb": ("p_y", "ffn0", 1, 1), "wq1": ("p_q1", 1, 0, 1), "wk1": ("p_q1", 1, 1, 1),
                    "wv1": ("p_q1", 1, 2, 1), "wxk": ("p_kx", "kvlat", 1, 3), "wxv": ("p_vx", "kvlat", 1, 1),
                    "ctxt0": ("p_vx", "kvctx", 0, 3), "ctxt1": ("p_vx", "kvctx", 1, 3)}
        for kv in range(KV):
            last_use[f"wxq{kv}"] = ("p_q4", kv, 1, 1)
            last_use[f"wxo{kv}"] = ("p_y", "out4", kv, 1, 1)
        scratch0 = nc.dram_tensor("scratch0", (B, 2, D, T), F32, kind="Internal").ap()
        scratch1 = nc.dram_tensor("scratch1", (B, 2, 3, NI, HD, NH // C, C * P), BF16, kind="Internal").ap()
        scratch1v = nc.dram_tensor("scratch1v", (B, NI, HD, NH // C, C * P), F32, kind="Internal").ap()
        scratch3 = nc.dram_tensor("scratch3", (B, 2, D, T), F32, kind="Internal").ap()
        scratch2 = nc.dram_tensor("scratch2", (B * NI, D, P), F32, kind="Internal").ap()
        flat1 = [PT[0][:, 0:1024], ON[:, :], PT[1][:, 0:1024]]
        proj1 = [v.rearrange("p (i m t) -> p m i t", i=NI, m=C) for v in flat1]
        rsum0 = VX[:, 4096:4096 + T]
        on0 = VX[:, 4096 + T:4096 + 2 * T]
        ot0 = plain(SG[:, 0:1024]).rearrange("p (c t) -> p c t", c=C)
        sum0 = plain(SG[:, 1024:2048]).rearrange("p (c t) -> p c t", c=C)
        parts1 = VX[:, 1088:1088 + 3072].bitcast(BF16).rearrange("p (n s f) -> p n s f", n=2, s=3)
        block = ctx.enter_context(nc.Block())

        @block.tensor
        def _(pe):
            def split_mm(o, sh, sl, mh, ml, first, last):
                pe.matmul(o, sh, mh, start=first, stop=False)
                pe.matmul(o, sh, ml, start=False, stop=False)
                return pe.matmul(o, sl, mh, start=False, stop=last)

            def scores0(pe, b, n):
                if n == 0:
                    pe.wait_ge(*on("consts"))
                    pe.wait_ge(*on(f"d_q0_{b}"))
                    pe.wait_ge(*on(f"d_k0_{b}"))
                i, g = (0, n) if n < 8 else (1, n - 8)
                per = 4 // (i + 1)
                t = bank(pe, ringA, ("s0", b, n), ("m0", b, n))
                tv = t[:, :].rearrange("p (h k) -> p h k", h=per)
                pe.matmul(tv[:, :, i * P:(i + 1) * P], identb[:, :], mask_s[:, :].unsqueeze(1).broadcast_to([P, per, P]),
                          start=True, stop=False, skip_group_check=True)
                for j in range(per):
                    last = pe.matmul(tv[:, j, :], qs0(b)[0:48, g * per + j, i * P:(i + 1) * P], KS0[0:48, b, 0:(i + 1) * P],
                                     start=False, stop=True, skip_group_check=True)
                last.then_inc(*ev("p_s0", b, n))

            def scores1(pe, u, g4):
                if g4 == 0:
                    pe.wait_ge(*on(f"d_l1_{u % 3}", u))
                t = bank(pe, ringA, ("s1", u, g4), ("m1", u, g4))
                for j in range(4):
                    g = 4 * g4 + j
                    last = pe.matmul(t[:, j * P:(j + 1) * P], group(u, 0, slice(0, 4 + HD), g), group(u, 1, slice(0, 4 + HD), g), start=True, stop=True)
                last.then_inc(*ev("p_s1", u, g4))

            def turn1(pe, u):
                pe.wait_ge(*on("d_v1", u))
                t = bank(pe, ringA, ("v1", u), ("vp", u))
                for g in range(NG):
                    last = pe.transpose(t[:, g * HD:(g + 1) * HD], v1[:, g:g + 32 * 127 + 1:32], ident[0:HD, 0:HD])
                last.then_inc(*ev("p_v1", u))

            def scores4(pe, kv, b, n):
                i, h, j = n // 8, n // 2 % 4, n % 2
                if n == 0:
                    pe.wait_ge(*on("q4_low", kv, b, 1))
                    pe.wait_ge(*on("kx_low", "kvlat", b, KV - 1))
                t = bank(pe, ringA, ("s4", kv, b, n), ("m4", kv, b, n))
                pe.matmul(t[:, 0:384], qx(2 * kv + b, 0)[0:XD, h, i * P:(i + 1) * P], kx(b, 0)[0:XD, kv, j * 384:(j + 1) * 384],
                          start=True, stop=True).then_inc(*ev("p_s4", kv, b, n))

            def values0(pe, b, g):
                pt = PT[g % 2]
                pe.wait_ge(*on("e0", b, g, 2))
                for j in range(2):
                    t = bank(pe, ringB, ("o0", b, g, j), ("on0", b, g, j))
                    tv = t[0:2 * HD, :].rearrange("p (h q) -> p h q", h=2)
                    late = pt[:, 1024 + j * T:1024 + (j + 1) * T].rearrange("p (h q) -> p h q", h=2)
                    pe.matmul(t[0:2 * HD, :], V0[:, b, 0, :], pt[:, j * 512:(j + 1) * 512], start=True, stop=False, skip_group_check=True)
                    pe.matmul(tv[:, :, P:T], V0[:, b, 1, :], late, start=False, stop=True, skip_group_check=True).then_inc(*ev("p_o0", b, g, j))

            pe.wait_ge(*on("ident"))
            for step in schedule:
                what, *k = step
                if what == "turn":
                    s, b = k
                    for i in range(NI):
                        pe.wait_ge(*on("h", s, b, i))
                        if s == 1:
                            t = bank(pe, ringA, ("hT", s, b, i), ("q1T", b, i))
                            tv = t[:, 0:256].bitcast(BF16)
                            for c in range(C):
                                last = pe.transpose(tv[:, c * P:(c + 1) * P], q1n[:, i, c * P:(c + 1) * P], identb[:, :])
                        else:
                            t = bank(pe, ringA, ("hT", s, b, i), ("h_low", s, b, i))
                            for c in range(C):
                                last = pe.transpose(t[:, c * P:(c + 1) * P], H[:, i, c * P:(c + 1) * P], ident[:, :])
                        last.then_inc(*ev("p_hT", s, b, i))
                elif what == "qkv0":
                    b, = k
                    pe.wait_ge(*on("h_low", 0, b, NI - 1))
                    wh, wl = (pe.wait_ge(*on("split_v", "wq0")), item("wq0"))[1]
                    for mp in range(2):
                        t = bank(pe, ringA, ("q0", b, mp), ("q0_low", b, mp))
                        for j in range(2):
                            m = 2 * mp + j
                            for c in range(C):
                                last = split_mm(t[:, j * T:(j + 1) * T], wh[:, c, m * P:(m + 1) * P], wl[:, c, m * P:(m + 1) * P],
                                                HH[:, b, c, :], HL[:, b, c, :], c == 0, c == C - 1)
                        last.then_inc(*ev("p_q0", b, mp))
                    pe.wait_ge(*on("split", "wkv0"))
                    wh, wl = item("wkv0")
                    t = bank(pe, ringA, ("k0", b), ("k0_low", b))
                    for c in range(C):
                        last = split_mm(t[0:HD, 0:T], wh[:, c, 0:HD], wl[:, c, 0:HD], HH[:, b, c, :], HL[:, b, c, :], c == 0, c == C - 1)
                    last.then_inc(*ev("p_k0", b))
                    t = bank(pe, ringA, ("v0", b), ("v0_out", b))
                    for i in range(NI):
                        for c in range(C):
                            last = split_mm(t[:, i * HD:(i + 1) * HD], HH[:, b, c, i * P:(i + 1) * P], HL[:, b, c, i * P:(i + 1) * P],
                                            wh[:, c, HD:2 * HD], wl[:, c, HD:2 * HD], c == 0, c == C - 1)
                    last.then_inc(*ev("p_v0", b))
                elif what == "smax0":
                    b, = k
                    for n in range(24):
                        scores0(pe, b, n)
                elif what == "mrow0":
                    b, = k
                    pe.wait_ge(*on("m0", b, 23))
                    t = bank(pe, ringA, ("mr0", b), ("mrow0", b))
                    for i in range(NI):
                        last = pe.transpose(t[0:NH, i * P:(i + 1) * P], MX[:, b, i, :], ident[:, :])
                    last.then_inc(*ev("p_mr0", b))
                elif what == "att0":
                    b, other, g0, g1 = k
                    pe.wait_ge(*on(f"d_m0_{b}"))
                    pe.wait_ge(*on("v0_out", b))
                    for g in range(g0, g1):
                        if g < NH // 4:
                            if other is not None:
                                for n in range(3 * g, 3 * g + 3):
                                    scores0(pe, other, n)
                            for j in range(2):
                                t = bank(pe, ringA, ("t0", b, g, j), ("e0", b, g, j))
                                tv = t[:, :].rearrange("p (h q) -> p h q", h=2)
                                pe.matmul(tv[:, :, 0:P], identb[:, :], mask_t[:, :].unsqueeze(1).broadcast_to([P, 2, P]),
                                          start=True, stop=False, skip_group_check=True)
                                pe.matmul(tv, KS0[0:49, b, 0:P], qs0(b)[0:49, g * 4 + j * 2:g * 4 + j * 2 + 2, :],
                                          start=False, stop=True, skip_group_check=True).then_inc(*ev("p_t0", b, g, j))
                            t = bank(pe, ringA, ("t0", b, g, 2), ("e0", b, g, 2))
                            tv = t[:, :].rearrange("p (h q) -> p h q", h=4)
                            pe.matmul(tv, identb[:, :], mask_t[:, :].unsqueeze(1).broadcast_to([P, 4, P]),
                                      start=True, stop=False, skip_group_check=True)
                            pe.matmul(tv, KS0[0:49, b, P:T], qs0(b)[0:49, g * 4:g * 4 + 4, P:T],
                                      start=False, stop=True, skip_group_check=True).then_inc(*ev("p_t0", b, g, 2))
                        if g >= 1:
                            values0(pe, b, g - 1)
                elif what == "out0":
                    b, = k
                    pe.wait_ge(*on("split", "wo0"))
                    wh, wl = item("wo0")
                    pe.wait_ge(*on("ot0_low", b, C - 1))
                    for i in range(NI):
                        t = bank(pe, ringA, ("y", "out0", b, i), ("x", "out0", b, i))
                        for c in range(C):
                            last = split_mm(t[:, :], HH[:, b, c, i * P:(i + 1) * P], HL[:, b, c, i * P:(i + 1) * P],
                                            wh[:, c, :], wl[:, c, :], c == 0, c == C - 1)
                        last.then_inc(*ev("p_y", "out0", b, i))
                elif what == "quant":
                    b, = k
                    pe.wait_ge(*on("q2", b))
                    t = bank(pe, ringA, ("cs", b), ("corr", b))
                    for c in range(C):
                        last = pe.matmul(t[:, :], onesb[:, :], q2n(b)[:, c, :], start=c == 0, stop=c == C - 1)
                    last.then_inc(*ev("p_cs", b))
                    for i in range(NI):
                        pe.wait_ge(*on("q1T", b, i))
                        t = bank(pe, ringA, ("y", "quant", b, i), ("x1t", b, i))
                        for c in range(C):
                            last = pe.matmul(t[:, :], q1t(b)[:, c, i * P:(i + 1) * P], q2n(b)[:, c, :], start=c == 0, stop=c == C - 1)
                        last.then_inc(*ev("p_y", "quant", b, i))
                elif what == "ffn0a":
                    b, = k
                    pe.wait_ge(*on("h_low", 2, b, NI - 1))
                    pe.wait_ge(*on("split", "wexp"))
                    wh, wl = item("wexp")
                    t = bank(pe, ringA, ("g0", b), ("hw", b, NI - 1))
                    n = E0 * R0 + E0
                    for i in range(NI):
                        for c in range(C):
                            last = split_mm(t[:, i * n:(i + 1) * n], HH[:, b, c, i * P:(i + 1) * P], HL[:, b, c, i * P:(i + 1) * P],
                                            wh[:, c, :], wl[:, c, :], c == 0, c == C - 1)
                    last.then_inc(*ev("p_g0", b))
                    pe.wait_ge(*on("split", "wbase"))
                    wh, wl = item("wbase")
                    for i in range(NI):
                        t = bank(pe, ringB, ("y", "ffn0", b, i), ("x", "ffn0", b, i))
                        for c in range(C):
                            split_mm(t[:, :], HH[:, b, c, i * P:(i + 1) * P], HL[:, b, c, i * P:(i + 1) * P],
                                     wh[:, c, :], wl[:, c, :], c == 0, False)
                elif what == "ffn0b":
                    b, = k
                    pe.wait_ge(*on("hw", b, NI - 1))
                    t = bank(pe, ringA, ("hwt", b), ("hwt_low", b))
                    for i in range(NI):
                        last = pe.transpose(t[:, i * P:(i + 1) * P], ON[:, i * D:i * D + P], ident[:, :])
                    last.then_inc(*ev("p_hwt", b))
                    pe.wait_ge(*on("hwt_low", b))
                    pe.wait_ge(*on("split", "wexpb"))
                    wh, wl = item("wexpb")
                    for i in range(NI):
                        split_mm(place[("y", "ffn0", b, i)][:, :], sgh[:, 0, i * P:(i + 1) * P], sgh[:, 1, i * P:(i + 1) * P], wh[:, 0, :], wl[:, 0, :],
                                 False, True).then_inc(*ev("p_y", "ffn0", b, i))
                elif what == "qkv1":
                    b, = k
                    pe.wait_ge(*on("h_low", 3, b, NI - 1))
                    for n, name in enumerate(("wq1", "wk1", "wv1")):
                        pe.wait_ge(*on("split_v" if name in LOW_ON_VECTOR else "split", name))
                        wh, wl = item(name)
                        for mp in range(2):
                            t = bank(pe, ringA, ("q1", b, n, mp), ("qkv1", b, n, mp))
                            for j in range(2):
                                m = 2 * mp + j
                                for c in range(C):
                                    last = split_mm(t[:, j * T:(j + 1) * T], wh[:, c, m * P:(m + 1) * P], wl[:, c, m * P:(m + 1) * P],
                                                    HH[:, b, c, :], HL[:, b, c, :], c == 0, c == C - 1)
                            last.then_inc(*ev("p_q1", b, n, mp))
                elif what == "smax1":
                    u, = k
                    for g4 in range(NG // 4):
                        scores1(pe, u, g4)
                    turn1(pe, u)
                elif what == "att1":
                    u, other = k
                    for g4 in range(NG // 4 + 1):
                        if g4 < NG // 4:
                            pe.wait_ge(*on("diag", u, g4))
                            t = bank(pe, ringA, ("t1", u, g4), ("e1", u, g4))
                            pe.matmul(t[:, :], onesb[:, :], DIAG[:, g4 % 2, :], start=True, stop=False, skip_group_check=True)
                            for j in range(4):
                                g = 4 * g4 + j
                                last = pe.matmul(t[:, j * P:(j + 1) * P], group(u, 1, slice(0, ROWS1), g),
                                                 group(u, 0, slice(0, ROWS1), g), start=False, stop=True, skip_group_check=True)
                            last.then_inc(*ev("p_t1", u, g4))
                            if other is not None:
                                scores1(pe, other, g4)
                        if g4 >= 1:
                            n = g4 - 1
                            pe.wait_ge(*on("e1", u, n))
                            if n == 0:
                                pe.wait_ge(*on("vp", u))
                            t = bank(pe, ringB, ("o1", u, n), ("ots", u, n))
                            pt = PT[n // 3 % 2][:, n % 3 * 512:(n % 3 + 1) * 512]
                            for j in range(4):
                                last = pe.matmul(t[0:17, j * P:(j + 1) * P], VP[:, 4 * n + j, :], pt[:, j * P:(j + 1) * P],
                                                 start=True, stop=True)
                            last.then_inc(*ev("p_o1", u, n))
                    if other is not None:
                        turn1(pe, other)
                elif what == "out1":
                    u, = k
                    pe.wait_ge(*on("d_o1", u))
                    t = bank(pe, ringB, ("den1", u), ("rden1", u))
                    pe.transpose(t[:, 0:NH], ON[0:NH, 512:512 + P], ident[0:NH, 0:NH]).then_inc(*ev("p_den1", u))
                    t = bank(pe, ringB, ("y", "out1", u), ("x1o", u))
                    for m in range(C):
                        last = pe.transpose(t[:, m * P:(m + 1) * P], ON[:, m * P:(m + 1) * P], ident[:, :])
                    last.then_inc(*ev("p_y", "out1", u))
                elif what in ("kvctx", "kvlat"):
                    b, = k
                    if what == "kvctx":
                        pe.wait_ge(*on("split", f"ctxt{b}"))
                        xh, xl = item(f"ctxt{b}")
                        n, tiles = CTX, 4
                    else:
                        pe.wait_ge(*on("h_low", 4, b, NI - 1))
                        xh, xl = HH[:, b, :, :], HL[:, b, :, :]
                        n, tiles = T, 2
                    pe.wait_ge(*on("split", "wxk"))
                    wh, wl = item("wxk")
                    for kv in range(KV):
                        t = bank(pe, ringA, (what, b, kv), ("kx_low", what, b, kv))
                        for c in range(C):
                            last = split_mm(t[0:XD, 0:n], wh[:, c, kv * XD:(kv + 1) * XD], wl[:, c, kv * XD:(kv + 1) * XD],
                                            xh[:, c, :], xl[:, c, :], c == 0, c == C - 1)
                        last.then_inc(*ev("p_kx", what, b, kv))
                    pe.wait_ge(*on("split", "wxv"))
                    wh, wl = item("wxv")
                    for st in range(tiles):
                        t = bank(pe, ringA, (what, "v", b, st), ("vx", what, b, st))
                        for c in range(C):
                            last = split_mm(t[:, 0:KV * XD], xh[:, c, st * P:(st + 1) * P], xl[:, c, st * P:(st + 1) * P],
                                            wh[:, c, :], wl[:, c, :], c == 0, c == C - 1)
                        last.then_inc(*ev("p_vx", what, b, st))
                elif what == "q4":
                    kv, b, j = k
                    pe.wait_ge(*on("split", f"wxq{kv}"))
                    pe.wait_ge(*on("h_low", 4, b, NI - 1))
                    wh, wl = item(f"wxq{kv}")
                    t = bank(pe, ringA, ("q4", kv, b, j), ("q4_low", kv, b, j))
                    for h in range(2):
                        f = (2 * j + h) * XD
                        for c in range(C):
                            last = split_mm(t[0:XD, h * T:(h + 1) * T], wh[:, c, f:f + XD], wl[:, c, f:f + XD],
                                            HH[:, b, c, :], HL[:, b, c, :], c == 0, c == C - 1)
                    last.then_inc(*ev("p_q4", kv, b, j))
                elif what == "smax4":
                    kv, b = k
                    for n in range(16):
                        scores4(pe, kv, b, n)
                elif what == "mrow4":
                    kv, b = k
                    pe.wait_ge(*on("m4s", kv, b))
                    t = bank(pe, ringA, ("mr4", kv, b), ("mrow4", kv, b))
                    pe.transpose(t[0:8, 0:P], small[:, 16:24], ident[:, :]).then_inc(*ev("p_mr4", kv, b))
                elif what == "att4":
                    kv, b, other, h0, h1 = k
                    n = 2 * kv + b
                    if h0 == 0:
                        pe.wait_ge(*on("d_m4", kv, b))
                        pe.wait_ge(*on("vx", "kvlat", b, 1))
                        pe.wait_ge(*on("kx_ones"))
                        for i in range(NI):
                            bank(pe, ringB, ("o4", kv, b, i), ("on4", kv, b, i))

                    def values4(h):
                        pt = PT[h % 2][:, :].rearrange("p (s q) -> p s q", q=T)
                        pe.wait_ge(*on("e4", kv, b, h, 2))
                        for i in range(NI):
                            for st in range(6):
                                last = pe.matmul(place[("o4", kv, b, i)][:, h * (XD + 1):(h + 1) * (XD + 1)], pt[:, st, i * P:(i + 1) * P], vx(b)[:, st, kv, :],
                                                 start=st == 0, stop=st == 5)
                        last.then_inc(*ev("p_o4", kv, b, h))
                    for h in range(h0, h1):
                        for s2 in range(3):
                            t = bank(pe, ringA, ("t4", kv, b, h, s2), ("e4", kv, b, h, s2))
                            for j in range(2):
                                o = t[:, j * T:(j + 1) * T]
                                ks = slice((2 * s2 + j) * P, (2 * s2 + j + 1) * P)
                                pe.matmul(o, kx(b, 0)[0:XD + 1, kv, ks], qx(n, 0)[0:XD + 1, h, :], start=True, stop=False)
                                pe.matmul(o, kx(b, 0)[0:XD, kv, ks], qx(n, 1)[0:XD, h, :], start=False, stop=False)
                                last = pe.matmul(o, kx(b, 1)[0:XD, kv, ks], qx(n, 0)[0:XD, h, :], start=False, stop=True)
                            last.then_inc(*ev("p_t4", kv, b, h, s2))
                            if other:
                                scores4(pe, *other, 4 * h + s2)
                        if other:
                            scores4(pe, *other, 4 * h + 3)
                        if h >= 1:
                            values4(h - 1)
                    if h1 == GQ:
                        values4(GQ - 1)
                elif what == "turn4":
                    kv, b = k
                    for i in range(NI):
                        pe.wait_ge(*on("on4", kv, b, i))
                        t = bank(pe, ringA, ("ot4", kv, b, i), ("ot4_low", kv, b, i))
                        for c in range(3):
                            last = pe.transpose(t[:, c * P:(c + 1) * P], ON[:, i * 384 + c * P:i * 384 + (c + 1) * P], ident[:, :])
                        last.then_inc(*ev("p_ot4", kv, b, i))
                elif what == "out4":
                    kv, b = k
                    pe.wait_ge(*on("split", f"wxo{kv}"))
                    wh, wl = item(f"wxo{kv}")
                    for i in range(NI):
                        pe.wait_ge(*on("ot4_low", kv, b, i))
                        t = bank(pe, ringA, ("y", "out4", kv, b, i), ("x", "out4", kv, b, i))
                        for c in range(3):
                            last = split_mm(t[:, :], sg3[:, 0, c, i * P:(i + 1) * P], sg3[:, 1, c, i * P:(i + 1) * P],
                                            wh[:, c, :], wl[:, c, :], c == 0, c == 2)
                        last.then_inc(*ev("p_y", "out4", kv, b, i))
                elif what == "ffn1a":
                    b, = k
                    pe.wait_ge(*on("mean", b))
                    pe.wait_ge(*on("d_mix"))
                    t = bank(pe, ringA, ("cq", b), ("cq", b))
                    for c in range(C):
                        last = pe.matmul(t[:, 0:1], wqx[:, c, :], small[:, 32 + c:33 + c], start=c == 0, stop=c == C - 1)
                    last.then_inc(*ev("p_cq", b))
                    pe.wait_ge(*on("cq", b))
                    t = bank(pe, ringA, ("cs1", b), ("cexp", b))
                    pe.matmul(t[0:1, 0:E1], small[:, 36:37], keys_t[:, :], start=True, stop=True).then_inc(*ev("p_cs1", b))
                    pe.wait_ge(*on("split", "wdown"))
                    wh, wl = item("wdown")
                    pe.wait_ge(*on("h_low", 5, b, NI - 1))
                    for mp in range(2):
                        t = bank(pe, ringB, ("dn", b, mp), ("dn_low", b, mp))
                        for j in range(2):
                            m = 2 * mp + j
                            for c in range(C):
                                last = split_mm(t[:, j * T:(j + 1) * T], wh[:, c, m * P:(m + 1) * P], wl[:, c, m * P:(m + 1) * P],
                                                HH[:, b, c, :], HL[:, b, c, :], c == 0, c == C - 1)
                        last.then_inc(*ev("p_dn", b, mp))
                    pe.wait_ge(*on("coef", b))
                    t = bank(pe, ringA, ("cc", b), ("cc", b))
                    for m in range(C):
                        last = pe.matmul(t[:, m:m + 1], expand[0:1, m * P:(m + 1) * P], ident[0:1, 0:1], start=True, stop=True)
                    last.then_inc(*ev("p_cc", b))
                elif what == "ffn1b":
                    b, = k
                    pe.wait_ge(*on("split", "worg"))
                    oh, ol = item("worg")
                    pe.wait_ge(*on("split", "wup"))
                    uh, ul = item("wup")
                    for i in range(NI):
                        t = bank(pe, ringA, ("y", "ffn1", b, i), ("x", "ffn1", b, i))
                        for c in range(C):
                            split_mm(t[:, :], HH[:, b, c, i * P:(i + 1) * P], HL[:, b, c, i * P:(i + 1) * P],
                                     oh[:, c, :], ol[:, c, :], c == 0, False)
                        pe.wait_ge(*on("dn_low", b, 1))
                        for c in range(C):
                            last = split_mm(t[:, :], sg4[:, 0, c, i * P:(i + 1) * P], sg4[:, 1, c, i * P:(i + 1) * P],
                                            uh[:, c, :], ul[:, c, :], False, c == C - 1)
                        last.then_inc(*ev("p_y", "ffn1", b, i))

        @block.scalar
        def _(act):
            def turned1(act, u):
                act.wait_ge(*on("p_v1", u))
                if u:
                    act.wait_ge(*on("p_o1", u - 1, 7))
                act.wait_ge(*on("vp_ones"))
                act.activation(VP[:, :, 0:HD], place[("v1", u)][:, :].rearrange("p (g d) -> p g d", d=HD), ACT.Copy).then_inc(*ev("vp", u))

            def high0(act, b, c):
                act.wait_ge(*on("p_v0", b))
                act.wait_ge(*on("normed0", b, c))
                act.activation(HH[:, b, c, :], on0, ACT.Copy).then_inc(*ev("ot0_high", b, c))

            def outs1(act, u, g4):
                act.wait_ge(*on("p_o1", u, g4))
                if g4 == 0 and u:
                    act.wait_ge(*on("d_o1", u - 1))
                act.activation(OTS[0:17, :, :].rearrange("p h (j g) -> p g h j", j=4)[:, 4 * g4:4 * g4 + 4, :, :],
                               place[("o1", u, g4)][0:17, :].rearrange("p (g h j) -> p g h j", g=4, h=NH), ACT.Copy).then_inc(*ev("ots", u, g4))

            for step in schedule:
                what, *k = step
                if what == "w":
                    name, = k
                    n = ITEM[name]
                    _, r, c, slot = ITEMS[n]
                    before = [m for m in range(n) if ITEMS[m][3] == slot]
                    if before:
                        act.wait_ge(*on(*last_use[ITEMS[before[-1]][0]]))
                    act.wait_ge(*on(f"d_stage{n % 2}", name))
                    act.activation(WH[slot][:, 0:r * c], STAGE[n % 2][:, 0:r * c], ACT.Copy).then_inc(*ev("split_high", name))
                elif what == "turn":
                    s, b = k
                    for i in range(NI):
                        act.wait_ge(*on("p_hT", s, b, i))
                        t = place[("hT", s, b, i)]
                        if s == 1:
                            act.activation(q1t(b)[:, :, i * P:(i + 1) * P], t[:, 0:256].bitcast(BF16).rearrange("p (c t) -> p c t", c=C),
                                           ACT.Copy).then_inc(*ev("q1T", b, i))
                        else:
                            act.activation(HH[:, b, :, i * P:(i + 1) * P], t[:, :].rearrange("p (c t) -> p c t", c=C),
                                           ACT.Copy).then_inc(*ev("h_high", s, b, i))
                elif what == "qkv0":
                    b, = k
                    if b:
                        act.wait_ge(*on("d_w0_0"))
                    for mp in range(2):
                        act.wait_ge(*on("p_q0", b, mp))
                        act.activation(sg4[:, 0, 2 * mp:2 * mp + 2, :], place[("q0", b, mp)][:, :].rearrange("p (m t) -> p m t", m=2),
                                       ACT.Copy).then_inc(*ev("q0_high", b, mp))
                    act.wait_ge(*on("p_k0", b))
                    act.wait_ge(*on("consts_v"))
                    act.activation(KS0[0:HD, b, :], place[("k0", b)][0:HD, 0:T], ACT.Copy).then_inc(*ev("k0_high", b))
                elif what == "mrow0":
                    b, = k
                    act.wait_ge(*on("p_mr0", b))
                    if b:
                        act.wait_ge(*on("d_m0_0"))
                    act.activation(MT[:, :], place[("mr0", b)][0:NH, 0:T], ACT.Copy, scale=-1.0).then_inc(*ev("mrow0", b))
                elif what == "att0":
                    b, other, g0, g1 = k
                    for g in range(g0, g1):
                        if g in (5, 7):
                            high0(act, b, (g - 5) // 2)
                        if g == NH // 4:
                            high0(act, b, 2)
                            continue
                        if g >= 2:
                            act.wait_ge(*on("p_o0", b, g - 2, 1))
                        elif b:
                            act.wait_ge(*on("p_o0", b - 1, 6 + g, 1))
                        for j in range(3):
                            act.wait_ge(*on("p_t0", b, g, j))
                            act.activation(PT[g % 2][:, j * 512:(j + 1) * 512], place[("t0", b, g, j)][:, :], ACT.Exp,
                                           scale=0.25).then_inc(*ev("e0", b, g, j))
                elif what == "last0":
                    high0(act, k[0], C - 1)
                elif what == "ffn0a":
                    b, = k
                    act.wait_ge(*on("lmm", b))
                    act.activation(rt[:, :, 1, :], rt[:, :, 0, :], ACT.Exp).then_inc(*ev("lexp", b))
                elif what == "ffn0b":
                    b, = k
                    act.wait_ge(*on("p_hwt", b))
                    act.activation(sgh[:, 0, :], place[("hwt", b)][:, 0:T], ACT.Copy).then_inc(*ev("hwt_high", b))
                elif what == "qkv1":
                    b, = k
                    for n in range(2):
                        act.wait_ge(*on("qkv1", b, n, 1))
                        if b:
                            act.wait_ge(*on("d_w1_0", 2))
                        act.activation(parts1[:, n, 0, :], flat1[n], ACT.Copy).then_inc(*ev("part_high", b, n))
                        act.wait_ge(*on("rest", b, n))
                        act.activation(parts1[:, n, 1, :], flat1[n], ACT.Copy).then_inc(*ev("part_mid", b, n))
                elif what == "smax1":
                    turned1(act, k[0])
                elif what == "att1":
                    u, other = k
                    for g4 in range(NG // 4):
                        act.wait_ge(*on("p_t1", u, g4))
                        if g4 == 0 and u == 0:
                            act.wait_ge(*on("part_low", 1, 0))
                        if g4 == 2 and u == 0:
                            act.wait_ge(*on("d_w1_1", 2))
                        if g4 >= 6:
                            act.wait_ge(*on("p_o1", u, g4 - 6))
                        act.activation(PT[g4 // 3 % 2][:, g4 % 3 * 512:(g4 % 3 + 1) * 512], place[("t1", u, g4)][:, :], ACT.Exp,
                                       scale=0.25).then_inc(*ev("e1", u, g4))
                        if g4 >= 2:
                            outs1(act, u, g4 - 2)
                    outs1(act, u, 6)
                    outs1(act, u, 7)
                    if other is not None:
                        turned1(act, other)
                elif what in ("kvctx", "kvlat"):
                    b, = k
                    s0, n = (0, CTX) if what == "kvctx" else (CTX, T)
                    for kv in range(KV):
                        act.wait_ge(*on("p_kx", what, b, kv))
                        act.activation(kx(b, 0)[0:XD, kv, s0:s0 + n], place[(what, b, kv)][0:XD, 0:n], ACT.Copy).then_inc(*ev("kx_high", what, b, kv))
                    for st in range(n // P):
                        act.wait_ge(*on("p_vx", what, b, st))
                        act.wait_ge(*on("vx_ones"))
                        act.activation(vx(b)[:, s0 // P + st, :, 0:XD], place[(what, "v", b, st)][:, 0:KV * XD].rearrange("p (k d) -> p k d", k=KV),
                                       ACT.Copy).then_inc(*ev("vx", what, b, st))
                elif what == "q4":
                    kv, b, j = k
                    n = 2 * kv + b
                    act.wait_ge(*on("p_q4", kv, b, j))
                    if n >= 2:
                        act.wait_ge(*on("p_t4", (n - 2) // 2, n % 2, GQ - 1, 2))
                    act.activation(qx(n, 0)[0:XD, 2 * j:2 * j + 2, :], place[("q4", kv, b, j)][0:XD, :].rearrange("p (h t) -> p h t", h=2),
                                   ACT.Copy).then_inc(*ev("q4_high", kv, b, j))
                elif what == "mrow4":
                    kv, b = k
                    act.wait_ge(*on("p_mr4", kv, b))
                    if kv or b:
                        act.wait_ge(*on("d_m4", *UNITS4[2 * kv + b - 1]))
                    act.activation(MT[0:8, 0:P], place[("mr4", kv, b)][0:8, 0:P], ACT.Copy, scale=-1.0).then_inc(*ev("mrow4", kv, b))
                elif what == "att4":
                    kv, b, other, h0, h1 = k
                    for h in range(h0, h1):
                        if h >= 2:
                            act.wait_ge(*on("p_o4", kv, b, h - 2))
                        elif kv or b:
                            act.wait_ge(*on("p_o4", *UNITS4[2 * kv + b - 1], h + 2))
                        for s2 in range(3):
                            act.wait_ge(*on("p_t4", kv, b, h, s2))
                            act.activation(PT[h % 2][:, s2 * 512:(s2 + 1) * 512], place[("t4", kv, b, h, s2)][:, :], ACT.Exp,
                                           scale=SX_SCALE).then_inc(*ev("e4", kv, b, h, s2))
                elif what == "turn4":
                    kv, b = k
                    for i in range(NI):
                        act.wait_ge(*on("p_ot4", kv, b, i))
                        if kv or b:
                            act.wait_ge(*on("p_y", "out4", *UNITS4[2 * kv + b - 1], i))
                        act.activation(sg3[:, 0, :, i * P:(i + 1) * P], place[("ot4", kv, b, i)][:, 0:384].rearrange("p (c t) -> p c t", c=3),
                                       ACT.Copy).then_inc(*ev("ot4_high", kv, b, i))
                elif what == "ffn1a":
                    b, = k
                    act.wait_ge(*on("cmax", b))
                    act.activation(small[0:1, 48:56], place[("cs1", b)][0:1, 0:E1], ACT.Exp, scale=1.0 / math.sqrt(128.0),
                                   bias=small[0:1, 41:42]).then_inc(*ev("cexp", b))
                    if b:
                        act.wait_ge(*on("p_y", "ffn1", 0, NI - 1))
                    for mp in range(2):
                        act.wait_ge(*on("p_dn", b, mp))
                        act.wait_ge(*on("cc", b))
                        for j in range(2):
                            m = 2 * mp + j
                            act.activation(sg4[:, 0, m, :], place[("dn", b, mp)][:, j * T:(j + 1) * T], ACT.Copy,
                                           scale=small[:, 44 + m:45 + m]).then_inc(*ev("dn_high", b, m))

        @block.vector
        def _(dve):
            def link(ins):
                ins.then_inc(*ev("v_step"))
                dve.wait_ge(semaphore("v_step"), total["v_step"])

            def maxima0(dve, b, n):
                i, g = (0, n) if n < 8 else (1, n - 8)
                per = 4 // (i + 1)
                dve.wait_ge(*on("p_s0", b, n))
                dve.tensor_reduce(MX[:, b, i, g * per:(g + 1) * per], place[("s0", b, n)][:, :].rearrange("p (h k) -> p h k", h=per),
                                  AX, ALU.max).then_inc(*ev("m0", b, n))

            def normed0(dve, b, c):
                dve.wait_ge(*on(f"d_ot0_{c}", b))
                if b or c:
                    dve.wait_ge(*so_far("normed0"))
                    dve.wait_ge(*so_far("ot0_low"))
                link(dve.reciprocal(rsum0, sum0[:, c, :]))
                dve.tensor_tensor(out=on0, in0=ot0[:, c, :], in1=rsum0, op=ALU.mult).then_inc(*ev("normed0", b, c))

            def low0(dve, b, c):
                dve.wait_ge(*on("ot0_high", b, c))
                low(HL[:, b, c, :], on0, HH[:, b, c, :], ("ot0_low", b, c))

            def maxima1(dve, u, g4):
                dve.wait_ge(*on("p_s1", u, g4))
                dve.tensor_reduce(mx1[:, (u % 2) * 32 + 4 * g4:(u % 2) * 32 + 4 * g4 + 4], place[("s1", u, g4)][:, :].rearrange("p (g k) -> p g k", g=4),
                                  AX, ALU.max).then_inc(*ev("m1", u, g4))

            def maxima4(dve, kv, b, n0, n1):
                if n0 == 0 and (kv or b):
                    dve.wait_ge(*on("p_mr4", *UNITS4[2 * kv + b - 1]))
                for n in range(n0, n1):
                    dve.wait_ge(*on("p_s4", kv, b, n))
                    dve.tensor_reduce(small[:, n:n + 1], place[("s4", kv, b, n)][:, 0:384], AX, ALU.max).then_inc(*ev("m4", kv, b, n))
                if n1 == 16:
                    dve.wait_ge(*on("m4", kv, b, 15))
                    dve.tensor_reduce(small[:, 16:24], small[:, 0:16].rearrange("p (g j) -> p g j", j=2), AX, ALU.max).then_inc(*ev("m4s", kv, b))

            mx1 = MX[:, :, :, :].rearrange("p b i h -> p (b i h)")

            def low(o, t, high, key):
                dve.tensor_tensor(out=o, in0=t, in1=plain(high), op=ALU.subtract).then_inc(*ev(*key))

            dve.memset(V0[:, :, :, HD:2 * HD], 1.0)
            dve.memset(onesb[:, :], 1.0)
            dve.memset(plain(KS0[:, :, :]), 1.0).then_inc(*ev("consts_v"))
            dve.wait_ge(*on("d_sc"))
            link(dve.reciprocal(sc[:, 4:5], sc[:, 0:1]))
            link(dve.reciprocal(sc[:, 5:6], sc[:, 2:3]))
            link(dve.tensor_scalar(sc[:, 6:7], sc[:, 1:2], -128.0, None, ALU.add))
            link(dve.tensor_scalar(sc[:, 7:8], sc[:, 3:4], -128.0, None, ALU.add))
            link(dve.tensor_tensor(out=sc[:, 8:9], in0=sc[:, 0:1], in1=sc[:, 2:3], op=ALU.mult))
            link(dve.tensor_scalar(sc[:, 9:10], sc[:, 6:7], sc[:, 8:9], -1.0, ALU.mult, ALU.mult))
            link(dve.tensor_scalar(sc[:, 10:11], sc[:, 9:10], sc[:, 7:8], -float(CTX), ALU.mult, ALU.mult))
            link(dve.tensor_scalar(sc[:, 11:12], sc[:, 7:8], -1.0, None, ALU.mult))
            for step in schedule:
                what, *k = step
                if what == "w" and k[0] in LOW_ON_VECTOR:
                    name, = k
                    n = ITEM[name]
                    _, r, c, slot = ITEMS[n]
                    dve.wait_ge(*on("split_high", name))
                    dve.tensor_tensor(out=WL[slot][:, 0:r * c], in0=STAGE[n % 2][:, 0:r * c], in1=plain(WH[slot][:, 0:r * c]),
                                      op=ALU.subtract).then_inc(*ev("split_v", name))
                elif what == "norm":
                    s, b = k
                    if s == 0:
                        dve.wait_ge(*on(f"d_x{b}"))
                    for i in range(NI):
                        last = dve.bn_stats(stats[:, i, :], X[:, 2 * b + i, :])
                    link(last)
                    if s or b:
                        dve.wait_ge(*so_far("h"))
                    for i in range(NI):
                        last = dve.bn_aggr(mv[:, i, :], stats[:, i, :])
                    link(last)
                    dve.tensor_scalar(var[:, :], mv[:, :, 1], EPS, None, ALU.add).then_inc(*ev("var", s, b))
                    dve.wait_ge(*on("rstd", s, b))
                    for i in range(NI):
                        ins = dve.tensor_scalar(H[:, i, :], X[:, 2 * b + i, :], mv[:, i, 0:1], rstd[:, i:i + 1], ALU.subtract, ALU.mult)
                        if s == 1:
                            link(ins)
                            link(dve.tensor_scalar(H[:, i, :], H[:, i, :], sc[:, 4:5], sc[:, 1:2], ALU.mult, ALU.add))
                            link(dve.tensor_scalar(H[:, i, :], H[:, i, :], 0.0, 255.0, ALU.max, ALU.min))
                            if b:
                                dve.wait_ge(*on("p_hT", 1, 0, i))
                            dve.tensor_scalar(q1n[:, i, :], H[:, i, :], ROUND, ROUND + 128.0, ALU.add, ALU.subtract).then_inc(*ev("h", s, b, i))
                        else:
                            ins.then_inc(*ev("h", s, b, i))
                    if s == 1:
                        for i in range(NI):
                            dve.wait_ge(*on("h", s, b, i))
                            link(dve.tensor_reduce(small[:, 2 * b + i:2 * b + i + 1], q1n[:, i, :], AX, ALU.add))
                            link(dve.tensor_scalar(small[:, 2 * b + i:2 * b + i + 1], small[:, 2 * b + i:2 * b + i + 1], sc[:, 11:12], None, ALU.mult))
                elif what == "turn":
                    s, b = k
                    if s != 1:
                        for i in range(NI):
                            dve.wait_ge(*on("p_hT", s, b, i))
                            t = place[("hT", s, b, i)]
                            if s == 5:
                                dve.wait_ge(*on("h_high", s, b, i))
                                link(dve.tensor_reduce(small[:, 24 + 4 * i:28 + 4 * i], t[:, :].rearrange("p (c t) -> p c t", c=C), AX, ALU.add))
                            dve.wait_ge(*on("h_high", s, b, i))
                            low(HL[:, b, :, i * P:(i + 1) * P], t[:, :].rearrange("p (c t) -> p c t", c=C), HH[:, b, :, i * P:(i + 1) * P], ("h_low", s, b, i))
                        if s == 5:
                            link(dve.tensor_tensor(out=small[:, 32:36], in0=small[:, 24:28], in1=small[:, 28:32], op=ALU.add))
                            dve.tensor_scalar(small[:, 32:36], small[:, 32:36], 1.0 / T, None, ALU.mult).then_inc(*ev("mean", b))
                elif what == "qkv0":
                    b, = k
                    for mp in range(2):
                        dve.wait_ge(*on("p_q0", b, mp))
                        dve.wait_ge(*on("q0_high", b, mp))
                        low(sg4[:, 1, 2 * mp:2 * mp + 2, :], place[("q0", b, mp)][:, :].rearrange("p (m t) -> p m t", m=2),
                            sg4[:, 0, 2 * mp:2 * mp + 2, :], ("q0_low", b, mp))
                    dve.wait_ge(*on("k0_high", b))
                    low(KL0[:, b, :], place[("k0", b)][0:HD, 0:T], KS0[0:HD, b, :], ("k0_low", b))
                    dve.wait_ge(*on("p_v0", b))
                    dve.tensor_copy(V0[:, b, :, 0:HD], place[("v0", b)][:, 0:2 * HD].rearrange("p (i d) -> p i d", i=NI)).then_inc(*ev("v0_out", b))
                elif what == "smax0":
                    b, = k
                    for n in range(24):
                        maxima0(dve, b, n)
                elif what == "att0":
                    b, other, g0, g1 = k

                    def copied(g):
                        for j in range(2):
                            dve.wait_ge(*on("p_o0", b, g, j))
                            if b or g >= 2:
                                dve.wait_ge(*on(f"d_on{g % 2}", *((b, g - 2) if g >= 2 else (b - 1, NH // 4 - 2 + g))))
                            dve.tensor_copy(sent0(g)[:, 2 * j:2 * j + 2, :], place[("o0", b, g, j)][0:2 * HD, :].rearrange("p (h t) -> p h t", h=2)
                                            ).then_inc(*ev("on0", b, g, j))
                    for g in range(g0, g1):
                        if other is not None and g < NH // 4:
                            for n in range(3 * g, 3 * g + 3):
                                maxima0(dve, other, n)
                        if g in (5, 7):
                            low0(dve, b, (g - 5) // 2)
                        if g >= 1:
                            copied(g - 1)
                        if g in (4, 6):
                            normed0(dve, b, (g - 4) // 2)
                        if g == NH // 4:
                            normed0(dve, b, 2)
                            low0(dve, b, 2)
                elif what == "last0":
                    normed0(dve, k[0], C - 1)
                    low0(dve, k[0], C - 1)
                elif what == "out0":
                    b, = k
                    for i in range(NI):
                        dve.wait_ge(*on("p_y", "out0", b, i))
                        x = X[:, 2 * b + i, :]
                        dve.tensor_tensor(out=x, in0=place[("y", "out0", b, i)][:, :], in1=x, op=ALU.add).then_inc(*ev("x", "out0", b, i))
                    dve.wait_ge(*on("x", "out0", b, NI - 1))
                elif what == "ctxq":
                    b, = k
                    name = f"ctxn{b}"
                    n = ITEM[name]
                    st = STAGE[n % 2]
                    dve.wait_ge(*on(f"d_stage{n % 2}", name))
                    link(dve.tensor_scalar(st[:, :], st[:, :], sc[:, 5:6], sc[:, 3:4], ALU.mult, ALU.add))
                    link(dve.tensor_scalar(st[:, :], st[:, :], 0.0, 255.0, ALU.max, ALU.min))
                    dve.tensor_scalar(q2n(b).rearrange("p c n -> p (c n)"), st[:, :], ROUND, ROUND + 128.0, ALU.add, ALU.subtract).then_inc(*ev("q2", b))
                elif what == "quant":
                    b, = k
                    dve.wait_ge(*on("p_cs", b))
                    dve.tensor_scalar(corr(b), place[("cs", b)][:, :], sc[:, 9:10], sc[:, 10:11], ALU.mult, ALU.add).then_inc(*ev("corr", b))
                    dve.wait_ge(*on("corr", b))
                    for i in range(NI):
                        dve.wait_ge(*on("p_y", "quant", b, i))
                        x = X[:, 2 * b + i, :]
                        dve.tensor_scalar(H[:, i, :], place[("y", "quant", b, i)][:, :], small[:, 2 * b + i:2 * b + i + 1], sc[:, 8:9],
                                          ALU.add, ALU.mult).then_inc(*ev("x1t", b, i))
                        dve.wait_ge(*on("x1t", b, i))
                        link(dve.tensor_tensor(out=H[:, i, :], in0=H[:, i, :], in1=corr(b), op=ALU.add))
                        dve.tensor_tensor(out=x, in0=H[:, i, :], in1=x, op=ALU.add).then_inc(*ev("x", "quant", b, i))
                    dve.wait_ge(*on("x", "quant", b, NI - 1))
                elif what == "ffn0a":
                    b, = k
                    n = E0 * R0 + E0
                    if b == 0:
                        dve.wait_ge(*on("d_on0", 1, NH // 4 - 2))
                        dve.wait_ge(*on("d_on1", 1, NH // 4 - 1))
                    dve.wait_ge(*on("p_g0", b))
                    tv = place[("g0", b)][:, 0:2 * n].rearrange("p (i n) -> p i n", i=NI)
                    logits = tv[:, :, E0 * R0:n]
                    link(dve.tensor_reduce(small[:, 8:10], logits, AX, ALU.max))
                    dve.tensor_tensor(out=rt[:, :, 0, :], in0=logits, in1=small[:, 8:10].unsqueeze(2).broadcast_to([P, NI, E0]),
                                      op=ALU.subtract).then_inc(*ev("lmm", b))
                    dve.wait_ge(*on("lexp", b))
                    for i in range(NI):
                        ex = rt[:, i, 1, :]
                        other = ex.unsqueeze(1).broadcast_to([P, E0, E0])
                        own = ex.unsqueeze(2).broadcast_to([P, E0, E0])
                        gt = rc[:, i, 0, :].rearrange("p (e j) -> p e j", e=E0)
                        eq = rc[:, i, 1, :].rearrange("p (e j) -> p e j", e=E0)
                        dve.tensor_tensor(out=gt, in0=other, in1=own, op=ALU.is_gt)
                        link(dve.tensor_tensor(out=eq, in0=other, in1=own, op=ALU.is_equal))
                        dve.wait_ge(*on("consts"))
                        link(dve.tensor_tensor(out=eq, in0=eq, in1=tri[:, :, :], op=ALU.mult))
                        link(dve.tensor_tensor(out=gt, in0=gt, in1=eq, op=ALU.add))
                        link(dve.tensor_reduce(rt[:, i, 2, :], gt, AX, ALU.add))
                        link(dve.tensor_scalar(rt[:, i, 2, :], rt[:, i, 2, :], 2.0, None, ALU.is_lt))
                        link(dve.tensor_tensor(out=rt[:, i, 3, :], in0=rt[:, i, 2, :], in1=ex, op=ALU.mult))
                        link(dve.tensor_reduce(small[:, 10 + i:11 + i], rt[:, i, 3, :], AX, ALU.add))
                        link(dve.reciprocal(small[:, 12 + i:13 + i], small[:, 10 + i:11 + i]))
                        link(dve.tensor_scalar(rt[:, i, 3, :], rt[:, i, 3, :], small[:, 12 + i:13 + i], 2.0, ALU.mult, ALU.mult))
                        dve.tensor_tensor(out=ON[:, i * D:i * D + P].rearrange("p (e r) -> p e r", e=E0),
                                          in0=tv[:, i, 0:E0 * R0].rearrange("p (e r) -> p e r", e=E0),
                                          in1=rt[:, i, 3, :].unsqueeze(2).broadcast_to([P, E0, R0]), op=ALU.mult).then_inc(*ev("hw", b, i))
                elif what == "ffn0b":
                    b, = k
                    dve.wait_ge(*on("hwt_high", b))
                    low(sgh[:, 1, :], place[("hwt", b)][:, 0:T], sgh[:, 0, :], ("hwt_low", b))
                    for i in range(NI):
                        x = X[:, 2 * b + i, :]
                        dve.wait_ge(*on("p_y", "ffn0", b, i))
                        dve.tensor_tensor(out=x, in0=place[("y", "ffn0", b, i)][:, :], in1=x, op=ALU.add).then_inc(*ev("x", "ffn0", b, i))
                        dve.wait_ge(*on("x", "ffn0", b, i))
                        if b == 0 and i == 0:
                            dve.wait_ge(*on("d_bias0"))
                        link(dve.tensor_tensor(out=x, in0=x, in1=bias0, op=ALU.add))
                elif what == "qkv1":
                    b, = k
                    if b == 0:
                        dve.wait_ge(*on("x", "ffn0", 1, 1))
                        dve.memset(VP[:, :, HD:HD + 1], 1.0).then_inc(*ev("vp_ones"))
                        dve.wait_ge(*on("d_biases"))
                        dve.wait_ge(*on("p_hT", 3, 0, 1))
                    else:
                        dve.wait_ge(*on("d_w1_0", 2))

                    def projected(n):
                        for mp in range(2):
                            dve.wait_ge(*on("p_q1", b, n, mp))
                            dve.tensor_tensor(out=proj1[n][:, 2 * mp:2 * mp + 2, :, :], in0=place[("q1", b, n, mp)][:, :].rearrange("p (m i t) -> p m i t", m=2, i=NI),
                                              in1=biases[:, n, 2 * mp:2 * mp + 2].unsqueeze(2).unsqueeze(3).broadcast_to([P, 2, NI, P]), op=ALU.add
                                              ).then_inc(*ev("qkv1", b, n, mp))

                    def split3(n):
                        dve.wait_ge(*on("part_high", b, n))
                        dve.tensor_tensor(out=flat1[n], in0=flat1[n], in1=parts1[:, n, 0, :], op=ALU.subtract).then_inc(*ev("rest", b, n))
                        dve.wait_ge(*on("part_mid", b, n))
                        dve.tensor_tensor(out=parts1[:, n, 2, :], in0=flat1[n], in1=parts1[:, n, 1, :], op=ALU.subtract).then_inc(*ev("part_low", b, n))
                    projected(0)
                    projected(1)
                    split3(0)
                    projected(2)
                    split3(1)
                elif what == "smax1":
                    for g4 in range(NG // 4):
                        maxima1(dve, k[0], g4)
                elif what == "att1":
                    u, other = k

                    def diag(u, g4):
                        if g4 >= 2:
                            dve.wait_ge(*on("p_t1", u, g4 - 2))
                        elif u:
                            dve.wait_ge(*on("p_t1", u - 1, 6 + g4))
                        m = mx1[:, (u % 2) * 32 + 4 * g4:(u % 2) * 32 + 4 * g4 + 4]
                        dve.tensor_tensor(out=DIAG[:, g4 % 2, :].rearrange("p (g k) -> p g k", g=4), in0=negid[:, :].unsqueeze(1).broadcast_to([P, 4, P]),
                                          in1=m.unsqueeze(2).broadcast_to([P, 4, P]), op=ALU.mult).then_inc(*ev("diag", u, g4))
                    if u == 0:
                        dve.wait_ge(*on("m1", u, 7))
                        diag(u, 0)
                        diag(u, 1)
                    for g4 in range(NG // 4):
                        if g4 + 2 < NG // 4:
                            diag(u, g4 + 2)
                        if other is not None:
                            maxima1(dve, other, g4)
                    if other is not None:
                        dve.wait_ge(*on("m1", other, 7))
                        diag(other, 0)
                        diag(other, 1)
                elif what == "out1":
                    u, = k
                    x = X[:, u, :]
                    dve.wait_ge(*on("p_den1", u))
                    dve.reciprocal(rden[:, :], place[("den1", u)][:, 0:NH]).then_inc(*ev("rden1", u))
                    dve.wait_ge(*on("rden1", u))
                    dve.wait_ge(*on("p_y", "out1", u))
                    t = H[:, 0, :]
                    dve.tensor_tensor(out=t.rearrange("p (m h d) -> p m h d", m=C, d=HD), in0=place[("y", "out1", u)][:, :].rearrange("p (m h d) -> p m h d", m=C, d=HD),
                                      in1=rden[:, :].rearrange("p (h m) -> p m h", m=C).unsqueeze(3).broadcast_to([P, C, NH // C, HD]), op=ALU.mult
                                      ).then_inc(*ev("x1o", u))
                    dve.wait_ge(*on("x1o", u))
                    link(dve.tensor_tensor(out=x, in0=t, in1=x, op=ALU.add))
                elif what in ("kvctx", "kvlat"):
                    b, = k
                    s0, n = (0, CTX) if what == "kvctx" else (CTX, T)
                    for kv in range(KV):
                        dve.wait_ge(*on("kx_high", what, b, kv))
                        low(kx(b, 1)[0:XD, kv, s0:s0 + n], place[(what, b, kv)][0:XD, 0:n], kx(b, 0)[0:XD, kv, s0:s0 + n], ("kx_low", what, b, kv))
                    if what == "kvctx" and b == 0:
                        dve.wait_ge(*on("d_w2", 3))
                        dve.wait_ge(*on("d_o1", 3))
                        dve.memset(vx(0)[:, :, :, XD:XD + 1], 1.0)
                        dve.memset(vx(1)[:, :, :, XD:XD + 1], 1.0).then_inc(*ev("vx_ones"))
                elif what == "q4":
                    kv, b, j = k
                    n = 2 * kv + b
                    dve.wait_ge(*on("q4_high", kv, b, j))
                    low(qx(n, 1)[0:XD, 2 * j:2 * j + 2, :], place[("q4", kv, b, j)][0:XD, :].rearrange("p (h t) -> p h t", h=2),
                        qx(n, 0)[0:XD, 2 * j:2 * j + 2, :], ("q4_low", kv, b, j))
                elif what == "smax4":
                    maxima4(dve, *k, 0, 16)
                elif what == "att4":
                    kv, b, other, h0, h1 = k
                    if other:
                        maxima4(dve, *other, 4 * h0, 4 * h1)
                    for i in range(NI if h1 == GQ else 0):
                        dve.wait_ge(*on("p_o4", kv, b, GQ - 1))
                        tv = place[("o4", kv, b, i)][:, 0:GQ * (XD + 1)].rearrange("p (h d) -> p h d", h=GQ)
                        if kv or b or i:
                            dve.wait_ge(*so_far("on4"))
                        link(dve.reciprocal(rden[:, 4 * i:4 * i + 4], tv[:, :, XD]))
                        if kv or b:
                            dve.wait_ge(*on("p_ot4", *UNITS4[2 * kv + b - 1], i))
                        dve.tensor_tensor(out=ON[:, i * 384:(i + 1) * 384].rearrange("p (h d) -> p h d", h=GQ), in0=tv[:, :, 0:XD],
                                          in1=rden[:, 4 * i:4 * i + 4].unsqueeze(2).broadcast_to([P, GQ, XD]), op=ALU.mult).then_inc(*ev("on4", kv, b, i))
                elif what == "turn4":
                    kv, b = k
                    for i in range(NI):
                        dve.wait_ge(*on("ot4_high", kv, b, i))
                        low(sg3[:, 1, :, i * P:(i + 1) * P], place[("ot4", kv, b, i)][:, 0:384].rearrange("p (c t) -> p c t", c=3),
                            sg3[:, 0, :, i * P:(i + 1) * P], ("ot4_low", kv, b, i))
                elif what == "out4":
                    kv, b = k
                    for i in range(NI):
                        dve.wait_ge(*on("p_y", "out4", kv, b, i))
                        x = X[:, 2 * b + i, :]
                        dve.tensor_tensor(out=x, in0=place[("y", "out4", kv, b, i)][:, :], in1=x, op=ALU.add).then_inc(*ev("x", "out4", kv, b, i))
                    dve.wait_ge(*on("x", "out4", kv, b, NI - 1))
                elif what == "ffn1a":
                    b, = k
                    dve.wait_ge(*on("p_cq", b))
                    dve.tensor_copy(small[:, 36:37], place[("cq", b)][:, 0:1]).then_inc(*ev("cq", b))
                    dve.wait_ge(*on("p_cs1", b))
                    link(dve.tensor_reduce(small[0:1, 40:41], place[("cs1", b)][0:1, 0:E1], AX, ALU.max))
                    dve.tensor_scalar(small[0:1, 41:42], small[0:1, 40:41], -1.0 / math.sqrt(128.0), None, ALU.mult).then_inc(*ev("cmax", b))
                    dve.wait_ge(*on("cexp", b))
                    link(dve.tensor_reduce(small[0:1, 42:43], small[0:1, 48:56], AX, ALU.add))
                    link(dve.reciprocal(small[0:1, 43:44], small[0:1, 42:43]))
                    link(dve.tensor_scalar(small[0:1, 56:64], small[0:1, 48:56], small[0:1, 43:44], None, ALU.mult))
                    dve.tensor_copy(expand[0:1, :].rearrange("p (e r) -> p e r", e=E1), small[0:1, 56:64].unsqueeze(2).broadcast_to([1, E1, R1])).then_inc(*ev("coef", b))
                    dve.wait_ge(*on("p_cc", b))
                    dve.tensor_copy(small[:, 44:48], place[("cc", b)][:, 0:4]).then_inc(*ev("cc", b))
                    dve.wait_ge(*on("cc", b))
                    for m in range(C):
                        dve.wait_ge(*on("dn_high", b, m | 1))
                        ins = dve.scalar_tensor_tensor(out=sg4[:, 1, m, :], in0=place[("dn", b, m // 2)][:, m % 2 * T:(m % 2 + 1) * T],
                                                       scalar=small[:, 44 + m:45 + m], in1=plain(sg4[:, 0, m, :]), op0=ALU.mult, op1=ALU.subtract)
                        if m % 2:
                            ins.then_inc(*ev("dn_low", b, m // 2))
                elif what == "ffn1b":
                    b, = k
                    for i in range(NI):
                        dve.wait_ge(*on("p_y", "ffn1", b, i))
                        x = X[:, 2 * b + i, :]
                        dve.tensor_tensor(out=x, in0=place[("y", "ffn1", b, i)][:, :], in1=x, op=ALU.add).then_inc(*ev("x", "ffn1", b, i))
            dve.nop().then_inc(*ev("finished"))

        @block.gpsimd
        def _(pool):
            def load(n):
                if n >= len(ITEMS):
                    return
                name, r, c, _ = ITEMS[n]
                if n >= 2:
                    before, _, _, slot = ITEMS[n - 2]
                    pool.wait_ge(*(on("q2", int(before[-1])) if slot is None else on("split_v" if before in LOW_ON_VECTOR else "split", before)))
                pool.dma_start(STAGE[n % 2][:, 0:r * c].rearrange("p (r c) -> p r c", r=r),
                               dram[name].rearrange("(r p) c -> p r c", p=P)).then_inc(*ev(f"d_stage{n % 2}", name, by=16))

            load(0)
            load(1)
            pool.memset(ident[:, :], 0.0).then_inc(*ev("zeros"))
            pool.wait_ge(*on("zeros"))
            pool.affine_select(out=ident[:, :], in_=ident[:, :], compare_op=ALU.not_equal, fill=1.0, base=0, pattern=[[-1, P]],
                               channel_multiplier=1).then_inc(*ev("ident"))
            pool.memset(minushalf[:, :], -0.5).then_inc(*ev("minushalf"))
            pool.wait_ge(*on("minushalf"))
            loaded = 2
            for step in schedule:
                what, *k = step
                if what == "consts":
                    pool.memset(negid[:, :], 0.0)
                    pool.memset(identb[:, :], 0.0)
                    pool.memset(mask_s[:, :], 0.0)
                    pool.memset(mask_t[:, :], 0.0)
                    pool.memset(rows_a[:, :], 0.0)
                    pool.memset(rows_b[:, :], -BIG)
                    pool.memset(tri[:, :, :], 1.0).then_inc(*ev("flat"))
                    pool.wait_ge(*on("flat"))
                    for m, fill in ((negid, -1.0), (identb, 1.0)):
                        pool.affine_select(out=m[:, :], in_=m[:, :], compare_op=ALU.not_equal, fill=fill, base=0, pattern=[[-1, P]], channel_multiplier=1)
                    pool.affine_select(out=mask_s[:, :], in_=mask_s[:, :], compare_op=ALU.is_ge, fill=-BIG, base=0, pattern=[[-1, P]], channel_multiplier=1)
                    pool.affine_select(out=mask_t[:, :], in_=mask_t[:, :], compare_op=ALU.is_ge, fill=-BIG, base=0, pattern=[[1, P]], channel_multiplier=-1)
                    for m, fill in ((rows_a, 1.0), (rows_b, 0.0)):
                        v = m[:, :].rearrange("p (j g) -> p j g", j=4)
                        pool.affine_select(out=v, in_=v, compare_op=ALU.not_equal, fill=fill, base=0, pattern=[[1, 4], [0, 32]], channel_multiplier=-1)
                    pool.affine_select(out=tri[:, :, :], in_=tri[:, :, :], compare_op=ALU.is_gt, fill=0.0, base=0,
                                       pattern=[[1, E0], [-1, E0]], channel_multiplier=0).then_inc(*ev("consts"))
                elif what == "w":
                    name, = k
                    n = ITEM[name]
                    _, r, c, slot = ITEMS[n]
                    while loaded <= n:
                        load(loaded)
                        loaded += 1
                    before = [m for m in range(n) if ITEMS[m][3] == slot]
                    if before:
                        pool.wait_ge(*on(*last_use[ITEMS[before[-1]][0]]))
                    if name not in LOW_ON_VECTOR:
                        pool.wait_ge(*on("split_high", name))
                        pool.tensor_tensor(out=WL[slot][:, 0:r * c], in0=STAGE[n % 2][:, 0:r * c], in1=plain(WH[slot][:, 0:r * c]),
                                           op=ALU.subtract).then_inc(*ev("split", name))
                    while loaded <= min(n + 2, len(ITEMS) - 1):
                        load(loaded)
                        loaded += 1
                elif what == "kvlat" and k[0] == 1:
                    pool.wait_ge(*on("p_t1", 3, NG // 4 - 1))
                    pool.wait_ge(*so_far("rstd"))
                    pool.wait_ge(*on("consts"))
                    for b in range(B):
                        pool.memset(plain(kx(b, 0)[XD:XD + 1, :, :]), 1.0).then_inc(*ev("kx_ones"))
                        pool.wait_ge(*so_far("kx_ones"))
                elif what == "norm":
                    s, b = k
                    pool.wait_ge(*on("var", s, b))
                    pool.tensor_tensor(out=rstd[:, :], in0=var[:, :], in1=minushalf[:, :], op=ALU.pow).then_inc(*ev("rstd", s, b))

        @block.sync
        def _(sp):
            sp.dma_start(X[:, 0:2, :], dram["x"][0:T, :].rearrange("(i p) d -> p i d", p=P)).then_inc(*ev("d_x0", by=16))
            sp.dma_start(sc[:, 0:4], dram["scales"].partition_broadcast(P)).then_inc(*ev("d_sc", by=16))
            sp.dma_start(X[:, 2:4, :], dram["x"][T:2 * T, :].rearrange("(i p) d -> p i d", p=P)).then_inc(*ev("d_x1", by=16))
            sp.dma_start(biases[:, :, :], dram["biases1"]).then_inc(*ev("d_biases", by=16))
            sp.dma_start(bias0, dram["bias0"].partition_broadcast(P)).then_inc(*ev("d_bias0", by=16))
            sp.dma_start(keys_t[:, :], dram["keys"]).then_inc(*ev("d_mix", by=16))
            sp.dma_start(wqx[:, :, :], dram["wqx"].rearrange("(c p) k -> p c k", p=P)).then_inc(*ev("d_mix", by=16))
            for step in schedule:
                what, *k = step
                if what == "qkv0":
                    b, = k
                    sp.wait_ge(*on("q0_high", b, 1))
                    sp.wait_ge(*on("q0_low", b, 1))
                    sp.dma_start(scratch0[b].rearrange("s (m p) t -> p s m t", p=P), plain(SG[:, :]).rearrange("p (s m t) -> p s m t", s=2, m=C)
                                 ).then_inc(*ev(f"d_w0_{b}", by=16))
                    sp.wait_ge(*on("k0_low", b))
                    sp.dma_start(plain(KS0[HD:2 * HD, b, :]), plain(KS0[0:HD, b, :])).then_inc(*ev(f"d_k0_{b}", by=16))
                    sp.dma_start(plain(KS0[2 * HD:3 * HD, b, :]), plain(KL0[:, b, :])).then_inc(*ev(f"d_k0_{b}", by=16))
                    sp.wait_ge(*on(f"d_w0_{b}"))
                    for row, half in enumerate((0, 1, 0)):
                        sp.dma_start(plain(qs0(b)[row * HD:(row + 1) * HD, :, :]), scratch0[b, half].rearrange("(h d) t -> d h t", d=HD)
                                     ).then_inc(*ev(f"d_q0_{b}", by=16))
                elif what == "mrow0":
                    b, = k
                    sp.wait_ge(*on("mrow0", b))
                    sp.dma_start(plain(qs0(b)[48:49, :, :]), plain(MT[:, :])).then_inc(*ev(f"d_m0_{b}", by=16))
                elif what == "att0":
                    b, _, g0, g1 = k
                    for g in range(max(g0 - 1, 0), g1 - 1):
                        sp.wait_ge(*on("on0", b, g, 1))
                        for n in range(2):
                            sp.dma_start(scratch3[b, n, g * 4 * HD:(g + 1) * 4 * HD, :].rearrange("(h d) t -> d h t", d=HD),
                                         sent0(g)[n * HD:(n + 1) * HD, :, :]).then_inc(*ev(f"d_on{g % 2}", b, g, by=16))
                        if g % 2:
                            c = g // 2
                            sp.wait_ge(*on("d_on0", b, g - 1))
                            sp.wait_ge(*on("d_on1", b, g))
                            sp.wait_ge(*on("d_w0_1"))
                            if b:
                                sp.wait_ge(*on("ot0_low", 0, c))
                            sp.dma_start(plain(SG[:, :]).rearrange("p (n c t) -> p n c t", n=2, c=C)[:, :, c, :],
                                         scratch3[b, :, c * P:(c + 1) * P, :].rearrange("n p t -> p n t")).then_inc(*ev(f"d_ot0_{c}", b, by=16))
                elif what == "qkv1":
                    b, = k
                    for n in (0, 1):
                        if n == 1:
                            sp.wait_ge(*on("qkv1", b, 2, 1))
                            for i in range(NI):
                                sp.dma_start(scratch1v[b, i, :, :, :].rearrange("d h f -> h d f"),
                                             flat1[2][:, i * 512:(i + 1) * 512]).then_inc(*ev(f"d_w1_{b}", 1, by=16))
                        for part, done in enumerate(("part_high", "part_mid", "part_low")):
                            sp.wait_ge(*on(done, b, n))
                            for i in range(NI):
                                sp.dma_start(scratch1[b, n, part, i, :, :, :].rearrange("d h f -> h d f"),
                                             parts1[:, n, part, i * 512:(i + 1) * 512]).then_inc(*ev(f"d_w1_{b}", 2 * n, by=16))
                elif what == "load1":
                    u, = k
                    b, i = divmod(u, NI)
                    name = f"d_l1_{u % 3}"
                    sp.wait_ge(*on(f"d_w1_{b}", 2))
                    if u < 3:
                        sp.wait_ge(*on("p_t0", 1, 7, 2))
                        sp.wait_ge(*on("consts"))
                        sp.dma_start(st1(u, 0)[0:4, :, :], rows_b[:, :].unsqueeze(1).broadcast_to([4, NH, P])).then_inc(*ev(name, u, by=16))
                        sp.dma_start(st1(u, 1)[0:4, :, :], rows_a[:, :].unsqueeze(1).broadcast_to([4, NH, P])).then_inc(*ev(name, u, by=16))
                    else:
                        sp.wait_ge(*on("p_t1", u - 3, 7))
                    for n in range(2):
                        at = 0
                        while at < len(PAIRS1):
                            first, to = PAIRS1[at][n], at + 1
                            step = PAIRS1[to][n] - first if to < len(PAIRS1) else 0
                            while to < len(PAIRS1) and step >= 0 and PAIRS1[to][n] == first + step * (to - at):
                                to += 1
                            if step > 0 and to > at + 1:
                                of = scratch1[b, n, first:first + to - at, i, :, :, :].rearrange("s d h f -> s d (h f)")
                            else:
                                of = scratch1[b, n, first, i, :, :, :].rearrange("d h f -> d (h f)").unsqueeze(0).broadcast_to([to - at, HD, NH * P])
                            sp.dma_start(st1(u, n)[4 + at * HD:4 + to * HD, :, :].rearrange("p h t -> p (h t)"), of).then_inc(*ev(name, u, by=16))
                            at = to
                elif what == "loadv":
                    u, = k
                    b, i = divmod(u, NI)
                    sp.wait_ge(*on(f"d_w1_{b}", 2))
                    if u:
                        sp.wait_ge(*on("p_v1", u - 1))
                    sp.dma_start(v1, scratch1v[b, i, :, :, :].rearrange("d h f -> d (h f)")).then_inc(*ev("d_v1", u, by=16))
                elif what == "att1":
                    u, other = k
                    sp.wait_ge(*on("ots", u, 7))
                    if u == 0:
                        sp.wait_ge(*on("d_w1_1", 2))
                    else:
                        sp.wait_ge(*on("p_y", "out1", u - 1))
                    for m in range(C):
                        sp.dma_start(scratch2[u, m * P:(m + 1) * P, :].rearrange("(h d) t -> d h t", d=HD),
                                     OTS[0:HD, :, :].rearrange("p (h m) t -> p m h t", m=C)[:, m, :, :]).then_inc(*ev("d_w2", u, by=16))
                    sp.dma_start(ON[0:NH, 512:512 + P], OTS[HD:HD + 1, :, :]).then_inc(*ev("d_o1", u, by=16))
                    sp.wait_ge(*on("d_w2", u))
                    sp.dma_start(ON[:, 0:512].rearrange("p (m t) -> p m t", m=C), scratch2[u, 0:D, :].rearrange("(m p) t -> p m t", p=P)
                                 ).then_inc(*ev("d_o1", u, by=16))
                    sp.wait_ge(*on("d_o1", u))
                elif what == "mrow4":
                    kv, b = k
                    sp.wait_ge(*on("mrow4", kv, b))
                    for i in range(NI):
                        sp.dma_start(plain(qx(2 * kv + b, 0)[XD:XD + 1, :, i * P:(i + 1) * P]), plain(MT[i * 4:(i + 1) * 4, 0:P])
                                     ).then_inc(*ev("d_m4", kv, b, by=16))
                    sp.wait_ge(*on("d_m4", kv, b))
                elif what == "ffn1b":
                    b, = k
                    for i in range(NI):
                        sp.wait_ge(*on("x", "ffn1", b, i))
                        sp.dma_start(out[b * T + i * P:b * T + (i + 1) * P, :], X[:, 2 * b + i, :]).then_inc(*ev("d_out", by=16))
            if schedule[-1][0] != "ffn1b":
                sp.wait_ge(*on("finished"))
                sp.dma_start(out.rearrange("(i p) d -> p i d", p=P), X[:, :, :]).then_inc(*ev("d_out", by=16))
            sp.wait_ge(*on("d_out"))
    return found


def kernel(**inputs):
    import numpy as np
    import concourse.bacc as bacc
    from concourse.bass_utils import run_bass_kernel_spmd as run

    a = {k: np.asarray(v) for k, v in inputs.items()}
    t = {
        "x": a["x"].reshape(B * T, D), "wq0": a["L0_attn_wq"], "wo0": a["L0_attn_wo"],
        "wkv0": np.concatenate([a["L0_attn_wk"], a["L0_attn_wv"]], axis=1),
        "ctxn0": a["ctx_4096"][0], "ctxn1": a["ctx_4096"][1], "ctxt0": a["ctx_4096"][0].T, "ctxt1": a["ctx_4096"][1].T,
        "scales": np.concatenate([a[f"L0_xattn_{n}"] for n in ("x1_scale", "x1_zp", "x2_scale", "x2_zp")]),
        "wbase": a["L0_ffn_W_base"].T, "bias0": a["L0_ffn_b_base"],
        "wexp": np.concatenate([a["L0_ffn_A"].reshape(E0 * R0, D).T, a["L0_ffn_W_router"].T], axis=1),
        "wexpb": a["L0_ffn_B"].transpose(0, 2, 1).reshape(E0 * R0, D),
        "wq1": a["L1_attn_wq"].T, "wk1": a["L1_attn_wk"].T, "wv1": a["L1_attn_wv"].T,
        "biases1": np.stack([a[f"L1_attn_b{n}"].reshape(C, P).T for n in "qkv"], axis=1),
        "wxk": a["L1_xattn_Wk"].T, "wxv": a["L1_xattn_Wv"].T,
        "worg": a["L1_ffn_W_org"].T, "wdown": a["L1_ffn_lora_down"].transpose(1, 0, 2).reshape(D, E1 * R1),
        "wup": a["L1_ffn_lora_up"].reshape(E1 * R1, D), "keys": a["L1_ffn_lora_keys"].T, "wqx": a["L1_ffn_Wq"].T,
    }
    for kv in range(KV):
        t[f"wxq{kv}"] = a["L1_xattn_Wq"].T[:, kv * GQ * XD:(kv + 1) * GQ * XD]
        t[f"wxo{kv}"] = a["L1_xattn_Wo"].T[kv * GQ * XD:(kv + 1) * GQ * XD, :]
    arrays = {f"in_{k}": np.ascontiguousarray(v) for k, v in t.items()}

    def build(counts):
        nc = bacc.Bacc("TRN2", target_bir_lowering=False, num_devices=1, dynamic_dma_scratch_size=8192)
        dram = {k: nc.dram_tensor(f"in_{k}", arrays[f"in_{k}"].shape, mybir.dt.from_np(arrays[f"in_{k}"].dtype), kind="ExternalInput").ap() for k in t}
        out = nc.dram_tensor("out_0", (B * T, D), F32, kind="ExternalOutput").ap()
        return nc, program(nc, dram, out, counts, SCHEDULE)

    _, counts = build({})
    nc, _ = build(counts)
    got = run(nc, [arrays], core_ids=[0]).results[0]["out_0"]
    return got.reshape(B, T, D)
```
